# Optimizing a Trainium2 kernel written in Bass

```python
import numpy as np
import jax
import jax.numpy as jnp

def _softmax(x, axis=-1):
    return jax.nn.softmax(x, axis=axis)

def _gelu(x):
    return jax.nn.gelu(x, approximate=True)

def _silu(x):
    return jax.nn.silu(x)

def _sigmoid(x):
    return jax.nn.sigmoid(x)

def _layernorm(x, axis=-1, eps=1e-05):
    m = jnp.mean(x, axis=axis, keepdims=True)
    v = jnp.var(x, axis=axis, keepdims=True)
    return (x - m) / jnp.sqrt(v + eps)

def _scatter_add(tgt, idx, src, axis=0):
    return tgt.at[idx].add(src)

def _segment_sum(src, seg, n):
    return jax.ops.segment_sum(src, seg, n)
kernel_name = 'mk_gnn_preln_d2_gnn_r8_dfebb2'

def setup_inputs(seed: int=0):
    np.random.seed(seed)
    _w = jnp.asarray

    def _rec_inputs():
        import jax
        import jax.numpy as jnp
        _gk = jax.random.key(seed)
        x = -0.0003713 + 1 * jax.random.normal(jax.random.fold_in(_gk, 1), (6250, 128), jnp.float32)
        src = jax.random.randint(jax.random.fold_in(_gk, 2), (200000,), 0, 6250, jnp.int32)
        dst = jax.random.randint(jax.random.fold_in(_gk, 3), (200000,), 0, 6250, jnp.int32)
        _o = jnp.argsort(dst, stable=True)
        src = src[_o]
        dst = dst[_o]
        return (x, src, dst)
    x, src, dst = _rec_inputs()

    def _L0_gnn_setup():
        import jax, jax.numpy as jnp
        import numpy as np
        N_NODES = 12500
        N_EDGES = 400000
        NFEAT = 128
        NHID = 128

        def gcn_conv(x, edge_index, W, b):
            n = x.shape[0]
            loop = jnp.arange(n, dtype=edge_index.dtype)
            src = jnp.concatenate([edge_index[0], loop])
            dst = jnp.concatenate([edge_index[1], loop])
            deg = jax.ops.segment_sum(jnp.ones_like(dst, dtype=x.dtype), dst, num_segments=n)
            dinv = jnp.where(deg > 0, jax.lax.rsqrt(jnp.maximum(deg, 1.0)), 0.0)
            norm = dinv[src] * dinv[dst]
            h = x @ W
            msg = h[src] * norm[:, None]
            out = jax.ops.segment_sum(msg, dst, num_segments=n)
            return out + b
        key = jax.random.key(seed)
        k1, k2, k3, k4 = jax.random.split(key, 4)
        x = jax.random.normal(k1, (N_NODES, NFEAT), dtype=jnp.float32)
        edge_index = jax.random.randint(k2, (2, N_EDGES), 0, N_NODES, dtype=jnp.int64)
        W1 = jax.random.normal(k3, (NFEAT, NHID), dtype=jnp.float32) * 0.05
        b1 = jnp.zeros((NHID,), dtype=jnp.float32)
        W2 = jax.random.normal(k4, (NHID, NHID), dtype=jnp.float32) * 0.05
        b2 = jnp.zeros((NHID,), dtype=jnp.float32)
        return {'x': x, 'edge_index': edge_index, 'W1': W1, 'b1': b1, 'W2': W2, 'b2': b2}
    _L0_gnn_all = _L0_gnn_setup()
    _L0_gnn_in = {k: v for k, v in _L0_gnn_all.items() if k in ('W1', 'b1', 'W2', 'b2')}
    del _L0_gnn_all

    def _L1_gnn_setup():
        import jax, jax.numpy as jnp
        import numpy as np
        N_NODES = 6250
        N_EDGES = 75000
        D = 128
        D_OUT = 128
        key = jax.random.key(seed)
        ks = jax.random.split(key, 6)
        features = jax.random.normal(ks[0], (N_NODES, D), dtype=jnp.float32)
        edge_index = jax.random.randint(ks[1], (2, N_EDGES), 0, N_NODES, dtype=jnp.int64)

        def xavier(k, shape):
            gain = float(np.sqrt(2.0))
            fan_out, fan_in = shape
            bound = gain * float(np.sqrt(6.0 / (fan_in + fan_out)))
            return jax.random.uniform(k, shape, jnp.float32, -bound, bound)
        W_neigh = xavier(ks[2], (D, D))
        b_neigh = jnp.zeros((D,), jnp.float32)
        W_edge = xavier(ks[3], (D, 2 * D))
        b_edge = jnp.zeros((D,), jnp.float32)
        W_lin = xavier(ks[4], (D_OUT, 2 * D))
        b_lin = jnp.zeros((D_OUT,), jnp.float32)
        return {'features': features, 'edge_index': edge_index, 'W_neigh': W_neigh, 'b_neigh': b_neigh, 'W_edge': W_edge, 'b_edge': b_edge, 'W_lin': W_lin, 'b_lin': b_lin}
    _L1_gnn_all = _L1_gnn_setup()
    _L1_gnn_in = {k: v for k, v in _L1_gnn_all.items() if k in ('W_neigh', 'b_neigh', 'W_edge', 'b_edge', 'W_lin', 'b_lin')}
    del _L1_gnn_all
    return {'x': x, 'src': src, 'dst': dst, 'L0_gnn_W1': _L0_gnn_in['W1'], 'L0_gnn_b1': _L0_gnn_in['b1'], 'L0_gnn_W2': _L0_gnn_in['W2'], 'L0_gnn_b2': _L0_gnn_in['b2'], 'L1_gnn_W_neigh': _L1_gnn_in['W_neigh'], 'L1_gnn_b_neigh': _L1_gnn_in['b_neigh'], 'L1_gnn_W_edge': _L1_gnn_in['W_edge'], 'L1_gnn_b_edge': _L1_gnn_in['b_edge'], 'L1_gnn_W_lin': _L1_gnn_in['W_lin'], 'L1_gnn_b_lin': _L1_gnn_in['b_lin']}

def reference(x, src, dst, L0_gnn_W1, L0_gnn_b1, L0_gnn_W2, L0_gnn_b2, L1_gnn_W_neigh, L1_gnn_b_neigh, L1_gnn_W_edge, L1_gnn_b_edge, L1_gnn_W_lin, L1_gnn_b_lin):
    import jax
    import jax.numpy as jnp

    def _L0_gnn_ref(x, edge_index, W1, b1, W2, b2):
        import jax, jax.numpy as jnp
        import numpy as np
        N_NODES = 12500
        N_EDGES = 400000
        NFEAT = 128
        NHID = 128

        def gcn_conv(x, edge_index, W, b):
            n = x.shape[0]
            loop = jnp.arange(n, dtype=edge_index.dtype)
            src = jnp.concatenate([edge_index[0], loop])
            dst = jnp.concatenate([edge_index[1], loop])
            deg = jax.ops.segment_sum(jnp.ones_like(dst, dtype=x.dtype), dst, num_segments=n)
            dinv = jnp.where(deg > 0, jax.lax.rsqrt(jnp.maximum(deg, 1.0)), 0.0)
            norm = dinv[src] * dinv[dst]
            h = x @ W
            msg = h[src] * norm[:, None]
            out = jax.ops.segment_sum(msg, dst, num_segments=n)
            return out + b
        h = jax.nn.relu(gcn_conv(x, edge_index, W1, b1))
        h = jax.nn.relu(gcn_conv(h, edge_index, W2, b2))
        return h

    def _L1_gnn_ref(features, edge_index, W_neigh, b_neigh, W_edge, b_edge, W_lin, b_lin):
        import jax, jax.numpy as jnp
        import numpy as np
        N_NODES = 6250
        N_EDGES = 75000
        D = 128
        D_OUT = 128
        n = features.shape[0]
        dst = edge_index[0]
        src = edge_index[1]
        h = features @ W_neigh.T + b_neigh
        h_src = h[src]
        edge_feats = jnp.abs(h[dst] - h_src)
        new_h = jnp.concatenate([h_src, edge_feats], axis=-1) @ W_edge.T + b_edge
        seg_sum = jax.ops.segment_sum(new_h, dst, num_segments=n)
        cnt = jax.ops.segment_sum(jnp.ones((dst.shape[0],), jnp.float32), dst, num_segments=n)[:, None]
        s = (h + seg_sum) / jnp.maximum(cnt, 1.0)
        z = jnp.concatenate([features, s], axis=-1) @ W_lin.T + b_lin
        return z
    edge_index = jnp.stack([src, dst])
    h = jnp.maximum(_layernorm(x, axis=-1), 0.0)
    x = x + _L0_gnn_ref(h, edge_index, L0_gnn_W1, L0_gnn_b1, L0_gnn_W2, L0_gnn_b2)
    h = jnp.maximum(_layernorm(x, axis=-1), 0.0)
    x = x + _L1_gnn_ref(h, edge_index, L1_gnn_W_neigh, L1_gnn_b_neigh, L1_gnn_W_edge, L1_gnn_b_edge, L1_gnn_W_lin, L1_gnn_b_lin)
    return x

_drawn_inputs = setup_inputs


def setup_inputs(seed=0):
    import zlib

    import numpy as np

    out = dict(_drawn_inputs(seed))
    spreads = {'L0_gnn_b1': (0.0, 0.426),
     'L0_gnn_b2': (0.0, 0.1),
     'L1_gnn_b_neigh': (0.0, 0.1),
     'L1_gnn_b_edge': (0.0, 0.1),
     'L1_gnn_b_lin': (0.0, 0.1)}
    factors = {}
    for name, (base, spread) in spreads.items():
        noise = np.random.default_rng([zlib.crc32(name.encode()), seed]).standard_normal(out[name].shape)
        drawn = base * np.exp(spread * noise) if base else spread * noise
        out[name] = jnp.asarray(drawn.astype(out[name].dtype))
    for name, factor in factors.items():
        out[name] = (out[name] * factor).astype(out[name].dtype)
    return out
```

```python
from contextlib import ExitStack

import concourse.bass as bass
from concourse import mybir

P = 128
N_NODES, N_EDGES, D = 6250, 200000, 128
NB = -(-N_NODES // P)
LAST = N_NODES - (NB - 1) * P
G = 4
NG = -(-NB // G)
NBP = NG * G
GC = G * P
CH = 7
NCH = NB // CH
WIN, WC = 36, 9
NWC = WIN // WC
FULL_G = N_EDGES // (P * P)
TAIL = N_EDGES - FULL_G * P * P
TAIL_ROWS, TAIL_EDGES = TAIL // P, TAIL % P
EG = FULL_G + 1
NT = EG * P
PAD_DST = 200 * P
EPS = 1e-5


def gnn(nc, x, src, dst, W1, b1, W2, b2, Wn, bn, We, be, Wl, bl, out):
    f32, bf16, i32 = mybir.dt.float32, mybir.dt.bfloat16, mybir.dt.int32
    ALU = mybir.AluOpType
    ACT = mybir.ActivationFunctionType
    AX = mybir.AxisListType
    ds = bass.ds

    adj = nc.dram_tensor("adj", (NG, NCH, P, CH, GC), bf16, kind="Internal").ap()
    rows = nc.dram_tensor("slot_rows", (2, NB, NB, P), bf16, kind="Internal").ap()

    src1 = src.rearrange("(o e) -> o e", o=1)
    dst1 = dst.rearrange("(o e) -> o e", o=1)

    ctx = ExitStack()
    with ctx:
        def sb(name, shape, dt, c=ctx):
            return c.enter_context(nc.sbuf_tensor(name, shape, dt))

        def ps(name, shape, c):
            return c.enter_context(nc.psum_tensor(name, shape, f32))

        def sem(name):
            return ctx.enter_context(nc.semaphore(name))

        def wait(eng, s, value):
            if not isinstance(value, int) or value > 0:
                eng.wait_ge(s, value)

        xN = sb("xN", [P, NBP, D], f32)
        hT = sb("hT", [P, NBP * P], f32)
        dinvT = sb("dinvT", [P, NBP * P], f32)
        gp = sb("gp", [P, NBP, 3, D], bf16)
        tab = sb("tab", [P, NB, 2, NB], bf16)
        cntN = sb("cntN", [P, NB], f32)
        ident = sb("ident", [P, P], f32)
        identb = sb("identb", [P, P], bf16)
        onesb = sb("onesb", [P, P], bf16)
        onesf = sb("onesf", [P, P], f32)
        iotaN = sb("iotaN", [P, P, CH], bf16)
        tri = sb("tri", [P, P], bf16)
        idCol = sb("idCol", [P, 1], f32)
        idColF = sb("idColF", [P, 1], i32)
        W1s, W2s = sb("W1s", [P, D], f32), sb("W2s", [P, D], f32)
        WnT, Wl1T, Wl2T = (sb(n, [P, D], f32) for n in ("WnT", "Wl1T", "Wl2T"))
        W12, W22 = sb("W12", [P, D], f32), sb("W22", [P, D], f32)
        b1c, b2c, bec, bnc = (sb(n, [P, 1], f32) for n in ("b1c", "b2c", "bec", "bnc"))
        bnr, blr, ber = (sb(n, [P, D], f32) for n in ("bnr", "blr", "ber"))
        epsC = sb("epsC", [P, 1], f32)
        ctl = sb("ctl", [1, 64], i32)
        FLAG = 60

        c0 = ExitStack()
        with c0:
            keyC = sb("keyC", [P, NT], f32, c0)
            idS = sb("idS", [P, NT], bf16, c0)
            idD = sb("idD", [P, NT], bf16, c0)
            iotaS = sb("iotaS", [P, NB, WIN], bf16, c0)
            iotaR = sb("iotaR", [P, P, WIN], bf16, c0)
            dbase = sb("dbase", [P, NB], f32, c0)
            c1 = ExitStack()
            with c1:
                eD = sb("eD", [P, EG, P], i32, c1)
                eS = sb("eS", [P, EG, P], i32, c1)
                blkD = sb("blkD", [P, EG, P], i32, c1)
                blkS = sb("blkS", [P, EG, P], i32, c1)
                keyR = sb("keyR", [P, EG, P], f32, c1)
                tmax = sb("tmax", [P, EG], f32, c1)
                less = sb("less", [P, NB, EG], f32, c1)
                lessN = sb("lessN", [P, NB], f32, c1)
                dbN = sb("dbN", [P, NB], f32, c1)
                wld = sb("wld", [P, 5, D], f32, c1)
                pT = [ps(f"pT{i}", [P, GC], c1) for i in range(4)]
                pW = [ps(f"pW{i}", [P, GC], c1) for i in range(3)]
                s_pre, s_edge, s_w, s_x, s_b = (sem(n) for n in ("s_pre", "s_edge", "s_w", "s_x", "s_b"))
                s_const, s_dvec, s_col, s_colps, s_colout = (
                    sem(n) for n in ("s_const", "s_dvec", "s_col", "s_colps", "s_colout"))
                s_wt, s_wtout, s_win, s_w2, s_w2out = (
                    sem(n) for n in ("s_wt", "s_wtout", "s_win", "s_w2", "s_w2out"))
                s_pool = sem("s_pool")
                with nc.Block() as block:
                    @block.sync
                    def _(sp):
                        sp.wait_ge(s_pre, 2)
                        for e, a in ((eD, dst), (eS, src)):
                            sp.dma_start(e[:, 0:FULL_G, :], a[0:FULL_G * P * P].rearrange(
                                "(g p e) -> p g e", p=P, e=P)).then_inc(s_edge, 16)
                            sp.dma_start(e[0:TAIL_ROWS, FULL_G, :], a[FULL_G * P * P:N_EDGES - TAIL_EDGES]
                                         .rearrange("(p e) -> p e", e=P)).then_inc(s_edge, 16)
                            sp.dma_start(e[TAIL_ROWS:TAIL_ROWS + 1, FULL_G, 0:TAIL_EDGES],
                                         a[N_EDGES - TAIL_EDGES:N_EDGES].rearrange("(p e) -> p e", p=1)
                                         ).then_inc(s_edge, 16)
                        sp.wait_ge(s_pre, 3)
                        sp.dma_start(xN[:, 0:NB - 1, :], x[0:(NB - 1) * P, :].rearrange(
                            "(n p) d -> p n d", p=P)).then_inc(s_x, 16)
                        sp.dma_start(xN[0:LAST, NB - 1, :], x[(NB - 1) * P:N_NODES, :]).then_inc(s_x, 16)
                        sp.wait_ge(s_x, 32)

                    @block.scalar
                    def _(act):
                        for t, w in ((0, Wn), (1, We[:, 0:D]), (2, We[:, D:2 * D]),
                                     (3, Wl[:, 0:D]), (4, Wl[:, D:2 * D])):
                            act.dma_start(wld[:, t, :], w).then_inc(s_w, 16)
                        act.dma_start(W1s[:, :], W1).then_inc(s_b, 16)
                        act.dma_start(W2s[:, :], W2).then_inc(s_b, 16)
                        for c, b in ((b1c, b1), (b2c, b2), (bec, be), (bnc, bn)):
                            act.dma_start(c[:, :], b.rearrange("(p a) -> p a", a=1)).then_inc(s_b, 16)
                        act.dma_start(bnr[:, :], bn.partition_broadcast(P)).then_inc(s_b, 16)
                        act.dma_start(blr[:, :], bl.partition_broadcast(P)).then_inc(s_b, 16)
                        for t, w in enumerate((WnT, Wl1T, Wl2T)):
                            act.wait_ge(s_wt, t + 1)
                            nc.scalar.activation(w[:, :], pW[t][:, 0:D], ACT.Copy).then_inc(s_wtout, 1)
                        act.wait_ge(s_w2, 1)
                        for t, w in enumerate((W12, W22, ber)):
                            nc.scalar.activation(w[:, :], pW[0][:, t * D:(t + 1) * D],
                                                 ACT.Copy).then_inc(s_w2out, 1)
                        act.wait_ge(s_w2out, 3)
                        act.wait_ge(s_b, 8 * 16)

                    @block.gpsimd
                    def _(pool):
                        nc.gpsimd.memset(ident[:, :], 0.0).then_inc(s_pool, 1)
                        nc.gpsimd.memset(onesf[:, :], 1.0).then_inc(s_const, 1)
                        nc.gpsimd.memset(onesb[:, :], 1.0).then_inc(s_const, 1)
                        nc.gpsimd.memset(epsC[:, :], EPS).then_inc(s_const, 1)
                        pool.wait_ge(s_pool, 1)
                        nc.gpsimd.affine_select(out=ident[:, :], in_=ident[:, :], compare_op=ALU.not_equal,
                                                fill=1.0, base=0, pattern=[[-1, P]],
                                                channel_multiplier=1).then_inc(s_const, 1)
                        pool.wait_ge(s_const, 3)
                        nc.gpsimd.affine_select(out=tri[:, :], in_=onesb[:, :], compare_op=ALU.is_gt,
                                                fill=0.0, base=0, pattern=[[1, P]],
                                                channel_multiplier=-1).then_inc(s_const, 1)
                        nc.gpsimd.iota(idColF[:, :], pattern=[[0, 1]], base=1,
                                       channel_multiplier=1).then_inc(s_const, 1)
                        for t, step, off in ((dbN, 1, 0), (dbase, NB, 0)):
                            nc.gpsimd.iota(t[:, :], pattern=[[step, NB]], base=off, channel_multiplier=0,
                                           allow_small_or_imprecise_dtypes=True).then_inc(s_const, 1)
                        for t, n, rep, off in ((iotaS, NB, WIN, 0), (iotaN, P, CH, 1), (iotaR, P, WIN, 0)):
                            nc.gpsimd.iota(t[:, :, :], pattern=[[1, n], [0, rep]], base=off,
                                           channel_multiplier=0,
                                           allow_small_or_imprecise_dtypes=True).then_inc(s_const, 1)
                        pool.wait_ge(s_const, 11)

                    @block.vector
                    def _(dve):
                        nc.vector.memset(eD[:, FULL_G, :], PAD_DST).then_inc(s_pre, 1)
                        nc.vector.memset(eS[:, FULL_G, :], 0).then_inc(s_pre, 1)
                        nc.vector.memset(xN[:, NB - 1:NBP, :], 0.0).then_inc(s_pre, 1)
                        dve.wait_ge(s_const, 7)
                        nc.vector.tensor_copy(idCol[:, :], idColF[:, :]).then_inc(s_dvec, 1)
                        nc.vector.tensor_copy(identb[:, :], ident[:, :]).then_inc(s_dvec, 1)
                        dve.wait_ge(s_edge, 6 * 16)
                        nc.vector.tensor_scalar(blkD[:, :, :], eD[:, :, :], 7, None,
                                                ALU.arith_shift_right).then_inc(s_dvec, 1)
                        nc.vector.tensor_scalar(blkS[:, :, :], eS[:, :, :], 7, None,
                                                ALU.arith_shift_right).then_inc(s_dvec, 1)
                        nc.vector.tensor_scalar(eD[:, :, :], eD[:, :, :], P - 1, None,
                                                ALU.bitwise_and).then_inc(s_dvec, 1)
                        nc.vector.tensor_scalar(eS[:, :, :], eS[:, :, :], P - 1, None,
                                                ALU.bitwise_and).then_inc(s_dvec, 1)
                        dve.wait_ge(s_dvec, 6)
                        nc.vector.scalar_tensor_tensor(out=keyR[:, :, :], in0=blkD[:, :, :], scalar=float(NB),
                                                       in1=blkS[:, :, :], op0=ALU.mult,
                                                       op1=ALU.add).then_inc(s_dvec, 1)
                        nc.vector.tensor_reduce(tmax[:, :], blkD[:, :, :], axis=AX.X,
                                                op=ALU.max).then_inc(s_dvec, 1)
                        dve.wait_ge(s_dvec, 8)
                        nc.vector.tensor_scalar(blkS[:, :, :].bitcast(f32), eS[:, :, :], 1.0, None,
                                                ALU.add).then_inc(s_dvec, 1)
                        nc.vector.tensor_scalar(blkD[:, :, :].bitcast(f32), eD[:, :, :], 1.0, None,
                                                ALU.add).then_inc(s_dvec, 1)
                        dve.wait_ge(s_const, 8)
                        nc.vector.tensor_tensor(less[:, :, :], tmax[:, :].unsqueeze(1).to_broadcast([P, NB, EG]),
                                                dbN[:, :].unsqueeze(2).to_broadcast([P, NB, EG]),
                                                ALU.is_lt).then_inc(s_dvec, 1)
                        dve.wait_ge(s_dvec, 11)
                        nc.vector.tensor_reduce(lessN[:, :], less[:, :, :], axis=AX.X,
                                                op=ALU.add).then_inc(s_dvec, 1)
                        n = 0
                        for t in (keyC, idS, idD):
                            for g in range(0, EG, 4):
                                k = min(4, EG - g) * P
                                dve.wait_ge(s_colps, n + 1)
                                nc.vector.tensor_copy(t[:, g * P:g * P + k],
                                                      pT[n % 4][:, 0:k]).then_inc(s_colout, 1)
                                n += 1
                        dve.wait_ge(s_win, 1)
                        nc.vector.tensor_copy(ctl[0:1, 0:NB], pW[1][0:1, 0:NB]).then_inc(s_dvec, 1)
                        dve.wait_ge(s_dvec, 13)
                        dve.wait_ge(s_colout, n)

                    @block.tensor
                    def _(pe):
                        pe.wait_ge(s_const, 4)
                        pe.wait_ge(s_w, 5 * 16)
                        for t, k in enumerate((0, 3, 4)):
                            nc.tensor.transpose(pW[t][:, 0:D], wld[:, k, :], ident[:, :]).then_inc(s_wt, 1)
                        pe.wait_ge(s_wtout, 3)
                        pe.wait_ge(s_b, 8 * 16)
                        nc.tensor.matmul(pW[0][:, 0:D], wld[:, 1, :], Wl2T[:, :], start=True, stop=True)
                        nc.tensor.matmul(pW[0][:, D:2 * D], wld[:, 2, :], Wl2T[:, :], start=True, stop=True)
                        nc.tensor.matmul(pW[0][:, 2 * D:3 * D], bec[:, 0:1].to_broadcast([P, P]), Wl2T[:, :],
                                         start=True, stop=True).then_inc(s_w2, 1)
                        n = 0
                        for t, r in enumerate((keyR[:, :, :], blkS[:, :, :].bitcast(f32),
                                               blkD[:, :, :].bitcast(f32))):
                            pe.wait_ge(s_dvec, 10)
                            for g in range(0, EG, 4):
                                if n >= 4:
                                    pe.wait_ge(s_colout, n - 3)
                                for k in range(min(4, EG - g)):
                                    last = nc.tensor.transpose(pT[n % 4][:, k * P:(k + 1) * P], r[:, g + k, :],
                                                               ident[:, :])
                                last.then_inc(s_colps, 1)
                                n += 1
                        pe.wait_ge(s_dvec, 12)
                        nc.tensor.matmul(pW[1][0:1, 0:NB], onesf[:, 0:1], lessN[:, :], start=True,
                                         stop=True).then_inc(s_win, 1)

            c1 = ExitStack()
            with c1:
                kk = [sb(f"kk{i}", [P, WIN], bf16, c1) for i in range(2)]
                oh = [sb(f"oh{i}", [P, NB, WIN], bf16, c1) for i in range(2)]
                ohc = [sb(f"ohc{i}", [P, NB, NWC], bf16, c1) for i in range(2)]
                room = gp[:, :, :, :].rearrange("p b k d -> p (b k d)")
                nv, nr = 2 * NB * WIN, P * WIN
                val = [room[:, i * nv:(i + 1) * nv].rearrange("p (v s j) -> p v s j", v=2, s=NB)
                       for i in range(2)]
                ohr = [room[:, 2 * nv + i * nr:2 * nv + (i + 1) * nr].rearrange("p (r j) -> p r j", r=P)
                       for i in range(2)]
                picked = sb("picked", [P, NWC, WC, NB], bf16, c1)
                rank = [sb(f"rank{i}", [P, WIN], bf16, c1) for i in range(2)]
                cntB = sb("cntB", [P, NB, NB], f32, c1)
                rowS = [sb(f"rowS{i}", [2 * NB, P], bf16, c1) for i in range(2)]
                stat = sb("stat", [P, 4], f32, c1)
                pC = ps("pC", [P, NWC, GC], c1)
                pS = [ps(f"pS{i}", [P, GC], c1) for i in range(2)]
                pB = ps("pB", [P, GC], c1)
                pR = ps("pR", [P, GC], c1)
                (q_kk, q_oh, q_ohc, q_vs, q_vd, q_cnt, q_pick, q_rank, q_ohr, q_slot,
                 q_tab, q_bkt, q_bktout, q_row, q_rowout, q_rowdma0, q_rowdma1, q_stat) = (
                    sem("q_" + n) for n in
                    ("kk", "oh", "ohc", "vs", "vd", "cnt", "pick", "rank", "ohr", "slot",
                     "tab", "bkt", "bktout", "row", "rowout", "rowdma0", "rowdma1", "stat"))
                q_rowdma = (q_rowdma0, q_rowdma1)
                with nc.Block() as block:
                    @block.vector
                    def _(dve):
                        def encode(b, p):
                            t0 = dve.value_load(ctl[0:1, ds(b, 1)], min_val=0, max_val=NT - WIN)
                            wait(dve, q_slot, b - 1)
                            nc.vector.tensor_scalar(kk[p][:, :], keyC[:, ds(t0, WIN)], dbase[:, ds(b, 1)], None,
                                                    ALU.subtract).then_inc(q_kk, 1)
                            dve.wait_ge(q_kk, b + 1)
                            nc.vector.tensor_tensor(oh[p][:, :, :], iotaS[:, :, :],
                                                    kk[p][:, :].unsqueeze(1).to_broadcast([P, NB, WIN]),
                                                    ALU.is_equal).then_inc(q_oh, 1)
                            dve.wait_ge(q_oh, b + 1)
                            with nc.allow_low_precision("counts to 9"):
                                nc.vector.tensor_reduce(ohc[p][:, :, :],
                                                        oh[p][:, :, :].rearrange("p s (c j) -> p s c j", j=WC),
                                                        axis=AX.X, op=ALU.add).then_inc(q_ohc, 1)
                            nc.vector.tensor_tensor(val[p][:, 0], oh[p][:, :, :],
                                                    idS[:, ds(t0, WIN)].unsqueeze(1).to_broadcast([P, NB, WIN]),
                                                    ALU.mult).then_inc(q_vs, 1)

                        def place(b, p):
                            dve.wait_ge(q_cnt, b + 1)
                            nc.vector.tensor_tensor(
                                picked[:, :, :, :],
                                pC[:, :, 0:WC * NB].rearrange("p c (j s) -> p c j s", s=NB),
                                oh[p][:, :, :].rearrange("p s (c j) -> p c j s", j=WC),
                                ALU.mult).then_inc(q_pick, 1)
                            dve.wait_ge(q_pick, b + 1)
                            with nc.allow_low_precision("one term isn't zero; a rank over 255 rounds to over 127"):
                                nc.vector.tensor_reduce(rank[p][:, :],
                                                        picked[:, :, :, :].rearrange("p c j s -> p (c j) s"),
                                                        axis=AX.X, op=ALU.add).then_inc(q_rank, 1)
                            dve.wait_ge(q_rank, b + 1)
                            wait(dve, q_slot, b - 1)
                            nc.vector.tensor_tensor(ohr[p][:, :, :], iotaR[:, :, :],
                                                    rank[p][:, :].unsqueeze(1).to_broadcast([P, P, WIN]),
                                                    ALU.is_equal).then_inc(q_ohr, 1)

                        encode(0, 0)
                        encode(1, 1)
                        place(0, 0)

                        def two(b):
                            encode(b + 1, 0)
                            place(b, 1)
                            encode(b + 2, 1)
                            place(b + 1, 0)
                        two(1)
                        with dve.Fori(1, (NB - 3) // 2) as i:
                            two(i * 2 + 1)
                        encode(NB - 1, 0)
                        place(NB - 2, 1)
                        place(NB - 1, 0)
                        dve.wait_ge(q_bktout, NB)
                        nc.vector.tensor_reduce(stat[:, 0:1], cntB[:, :, :], axis=AX.XY,
                                                op=ALU.add).then_inc(q_stat, 1)
                        nc.vector.tensor_reduce(stat[:, 1:2], cntB[:, :, :], axis=AX.XY,
                                                op=ALU.max).then_inc(q_stat, 1)
                        dve.wait_ge(q_stat, 2)
                        nc.vector.tensor_scalar(stat[:, 2:3], stat[:, 1:2], float(P), None,
                                                ALU.is_le).then_inc(q_stat, 1)
                        dve.wait_ge(q_stat, 3)
                        nc.vector.scalar_tensor_tensor(out=ctl[0:1, FLAG:FLAG + 1], in0=stat[0:1, 0:1],
                                                       scalar=float(N_EDGES), in1=stat[0:1, 2:3],
                                                       op0=ALU.is_equal, op1=ALU.mult).then_inc(q_stat, 1)
                        dve.wait_ge(q_stat, 4)

                    @block.gpsimd
                    def _(pool):
                        def values(b, p):
                            t0 = pool.value_load(ctl[0:1, ds(b, 1)], min_val=0, max_val=NT - WIN)
                            pool.wait_ge(q_oh, b + 1)
                            nc.gpsimd.tensor_tensor(val[p][:, 1], oh[p][:, :, :],
                                                    idD[:, ds(t0, WIN)].unsqueeze(1).to_broadcast([P, NB, WIN]),
                                                    ALU.mult).then_inc(q_vd, 1)

                        with pool.Fori(0, NB // 2) as i:
                            values(i * 2, 0)
                            values(i * 2 + 1, 1)
                        values(NB - 1, 0)

                    @block.tensor
                    def _(pe):
                        def count(b, p):
                            pe.wait_ge(q_ohc, b + 1)
                            wait(pe, q_pick, b)
                            o = oh[p][:, :, :].rearrange("p s j -> p j s")
                            for c in range(NWC):
                                full = pC[:, c, 0:WC * NB].rearrange("p (j s) -> p j s", s=NB)
                                nc.tensor.matmul(full, tri[:, :], o[:, c * WC:(c + 1) * WC, :],
                                                 start=True, stop=True)
                                for e in range(c):
                                    nc.tensor.matmul(full, onesb[:, :], ohc[p][:, :, e].unsqueeze(1)
                                                     .to_broadcast([P, WC, NB]), start=False, stop=True,
                                                     skip_group_check=True)
                                for j in range(WC - 1):
                                    last = nc.tensor.matmul(
                                        full[:, j + 1:WC, :], onesb[:, :],
                                        o[:, c * WC + j:c * WC + j + 1, :].to_broadcast([P, WC - 1 - j, NB]),
                                        start=False, stop=True, skip_group_check=True)
                            last.then_inc(q_cnt, 1)
                            wait(pe, q_bktout, b)
                            for e in range(NWC):
                                last = nc.tensor.matmul(pB[:, 0:NB], onesb[:, :], ohc[p][:, :, e],
                                                        start=e == 0, stop=e == NWC - 1)
                            last.then_inc(q_bkt, 1)

                        def fill(b, p):
                            pe.wait_ge(q_ohr, b + 1)
                            pe.wait_ge(q_vs, b + 1)
                            pe.wait_ge(q_vd, b + 1)
                            wait(pe, q_tab, b - 1)
                            for j in range(WIN):
                                last = nc.tensor.matmul(
                                    pS[p][:, 0:2 * NB], ohr[p][:, :, j],
                                    val[p][:, :, :, j].rearrange("p v s -> p (v s)"),
                                    start=j == 0, stop=j == WIN - 1)
                            last.then_inc(q_slot, 1)
                            pe.wait_ge(q_tab, b + 1)
                            wait(pe, q_rowout, b)
                            nc.tensor.matmul(pR[0:2 * NB, 0:P], tab[:, ds(b, 1)].rearrange("p o v s -> p (o v s)"),
                                             identb[:, :], start=True, stop=True).then_inc(q_row, 1)

                        count(0, 0)
                        count(1, 1)
                        fill(0, 0)

                        def two(b):
                            count(b + 1, 0)
                            fill(b, 1)
                            count(b + 2, 1)
                            fill(b + 1, 0)
                        two(1)
                        with pe.Fori(1, (NB - 3) // 2) as i:
                            two(i * 2 + 1)
                        count(NB - 1, 0)
                        fill(NB - 2, 1)
                        fill(NB - 1, 0)

                    @block.scalar
                    def _(act):
                        def leave(b, p):
                            act.wait_ge(q_bkt, b + 1)
                            nc.scalar.activation(cntB[:, ds(b, 1), :], pB[:, 0:NB].unsqueeze(1),
                                                 ACT.Copy).then_inc(q_bktout, 1)
                            act.wait_ge(q_slot, b + 1)
                            nc.scalar.activation(tab[:, ds(b, 1)].rearrange("p o v s -> p (o v s)"),
                                                 pS[p][:, 0:2 * NB], ACT.Copy).then_inc(q_tab, 1)

                        def row(b, p):
                            act.wait_ge(q_row, b + 1)
                            wait(act, q_rowdma[p], (b - p) * 16)
                            nc.scalar.activation(rowS[p][:, :], pR[0:2 * NB, 0:P], ACT.Copy).then_inc(q_rowout, 1)

                        leave(0, 0)
                        row(0, 0)
                        leave(1, 1)
                        row(1, 1)
                        with act.Fori(1, NB // 2) as i:
                            leave(i * 2, 0)
                            row(i * 2, 0)
                            leave(i * 2 + 1, 1)
                            row(i * 2 + 1, 1)
                        leave(NB - 1, 0)
                        row(NB - 1, 0)

                    @block.sync
                    def _(sp):
                        def save(b, p):
                            sp.wait_ge(q_rowout, b + 1)
                            for v in range(2):
                                sp.dma_start(rows[v][:, ds(b, 1), :].rearrange("s o r -> s (o r)"),
                                             rowS[p][v * NB:(v + 1) * NB, :]).then_inc(q_rowdma[p], 16)

                        with sp.Fori(0, NB // 2) as i:
                            save(i * 2, 0)
                            save(i * 2 + 1, 1)
                        save(NB - 1, 0)
                        sp.wait_ge(q_rowdma0, 32 * (NB // 2 + 1))
                        sp.wait_ge(q_rowdma1, 32 * (NB // 2))

        def norm_block(name, add_hT):
            cn = ExitStack()
            with cn:
                st = sb(name + "_st", [P, NBP, 6], f32, cn)
                mv = sb(name + "_mv", [P, NBP, 2], f32, cn)
                std = sb(name + "_std", [P, NBP], f32, cn)
                rstd = sb(name + "_rstd", [P, NBP], f32, cn)
                xn = [sb(f"{name}_xn{i}", [P, G, D], f32, cn) for i in range(2)]
                pN = [ps(f"{name}_p{i}", [P, GC], cn) for i in range(2)]
                pH = [ps(f"{name}_h{i}", [P, GC], cn) for i in range(2)]
                n_ht, n_add, n_st, n_mv, n_std, n_rstd, n_xn, n_tr, n_out = (
                    sem(name + "_" + n) for n in ("ht", "add", "st", "mv", "std", "rstd", "xn", "tr", "out"))
                with nc.Block() as block:
                    @block.vector
                    def _(dve):
                        if add_hT:
                            def add(g, p):
                                dve.wait_ge(n_ht, g + 1)
                                nc.vector.tensor_tensor(
                                    xN[:, ds(g * G, G), :], xN[:, ds(g * G, G), :],
                                    pH[p][:, :].rearrange("p (k d) -> p k d", d=D), ALU.add).then_inc(n_add, 1)
                            with dve.Fori(0, NG // 2) as i:
                                add(i * 2, 0)
                                add(i * 2 + 1, 1)
                            add(NG - 1, 0)
                            dve.wait_ge(n_add, NG)
                        with dve.Fori(0, NBP) as b:
                            nc.vector.bn_stats(st[:, ds(b, 1), :].rearrange("p o s -> p (o s)"),
                                               xN[:, ds(b, 1), :].rearrange("p o d -> p (o d)")).then_inc(n_st, 1)
                        dve.wait_ge(n_st, NBP)
                        nc.vector.tensor_tensor(mv[:, :, 0], st[:, :, 1], st[:, :, 4], ALU.add).then_inc(n_mv, 1)
                        nc.vector.tensor_tensor(mv[:, :, 1], st[:, :, 1], st[:, :, 4], ALU.subtract).then_inc(n_mv, 1)
                        nc.vector.tensor_tensor(rstd[:, :], st[:, :, 2], st[:, :, 5], ALU.add).then_inc(n_mv, 1)
                        dve.wait_ge(n_mv, 3)
                        nc.vector.tensor_scalar(mv[:, :, 0], mv[:, :, 0], 0.5, None, ALU.mult).then_inc(n_mv, 1)
                        nc.vector.scalar_tensor_tensor(out=std[:, :], in0=mv[:, :, 1], scalar=0.25,
                                                       in1=mv[:, :, 1], op0=ALU.mult,
                                                       op1=ALU.mult).then_inc(n_mv, 1)
                        dve.wait_ge(n_mv, 5)
                        nc.vector.scalar_tensor_tensor(out=mv[:, :, 1], in0=rstd[:, :], scalar=1.0 / D,
                                                       in1=std[:, :], op0=ALU.mult,
                                                       op1=ALU.add).then_inc(n_mv, 1)
                        dve.wait_ge(n_std, 1)
                        nc.vector.reciprocal(rstd[:, :], std[:, :]).then_inc(n_rstd, 1)
                        dve.wait_ge(n_rstd, 1)

                        def scale(g, p):
                            wait(dve, n_tr, g - 1)
                            for k in range(G):
                                b = g * G + k
                                last = nc.vector.tensor_scalar(
                                    xn[p][:, k, :], xN[:, ds(b, 1), :].rearrange("p o d -> p (o d)"),
                                    mv[:, ds(b, 1), 0:1].rearrange("p o s -> p (o s)"), rstd[:, ds(b, 1)],
                                    ALU.subtract, ALU.mult)
                            last.then_inc(n_xn, 1)
                        scale(0, 0)
                        scale(1, 1)
                        with dve.Fori(1, NG // 2) as i:
                            scale(i * 2, 0)
                            scale(i * 2 + 1, 1)
                        scale(NG - 1, 0)

                    @block.tensor
                    def _(pe):
                        if add_hT:
                            def back(g, p):
                                wait(pe, n_add, g - 1)
                                for k in range(G):
                                    last = nc.tensor.transpose(pH[p][:, k * P:(k + 1) * P], hcopy(k, p),
                                                               ident[:, :])
                                last.then_inc(n_ht, 1)
                            def hcopy(k, p):
                                return xn[p][:, k, :]
                            def back_all(g, p):
                                pe.wait_ge(n_out, g + 1)
                                back(g, p)
                            back_all(0, 0)
                            back_all(1, 1)
                            with pe.Fori(1, NG // 2) as i:
                                back_all(i * 2, 0)
                                back_all(i * 2 + 1, 1)
                            back_all(NG - 1, 0)

                        def turn(g, p):
                            pe.wait_ge(n_xn, g + 1)
                            wait(pe, n_out, g - 1 + (NG if add_hT else 0))
                            for k in range(G):
                                last = nc.tensor.transpose(pN[p][:, k * P:(k + 1) * P], xn[p][:, k, :],
                                                           ident[:, :])
                            last.then_inc(n_tr, 1)
                        turn(0, 0)
                        turn(1, 1)
                        with pe.Fori(1, NG // 2) as i:
                            turn(i * 2, 0)
                            turn(i * 2 + 1, 1)
                        turn(NG - 1, 0)

                    @block.scalar
                    def _(act):
                        if add_hT:
                            def fetch(g, p):
                                wait(act, n_ht, g - 1)
                                nc.scalar.activation(xn[p][:, :, :].rearrange("p k d -> p (k d)"),
                                                     hT[:, ds(g * GC, GC)], ACT.Copy).then_inc(n_out, 1)
                            fetch(0, 0)
                            fetch(1, 1)
                            with act.Fori(1, NG // 2) as i:
                                fetch(i * 2, 0)
                                fetch(i * 2 + 1, 1)
                            fetch(NG - 1, 0)
                        act.wait_ge(n_mv, 6)
                        nc.scalar.activation(std[:, :], mv[:, :, 1], ACT.Sqrt, bias=epsC[:, 0:1]
                                             ).then_inc(n_std, 1)

                        def leave(g, p):
                            act.wait_ge(n_tr, g + 1)
                            nc.scalar.activation(hT[:, ds(g * GC, GC)], pN[p][:, :], ACT.Relu).then_inc(n_out, 1)
                        with act.Fori(0, NG // 2) as i:
                            leave(i * 2, 0)
                            leave(i * 2 + 1, 1)
                        leave(NG - 1, 0)

        norm_block("n1", False)

        ca = ExitStack()
        with ca:
            ohe = [sb(f"ohe{i}", [P, G, 2, P, CH], bf16, ca) for i in range(2)]
            blk = [sb(f"blk{i}", [P, CH, GC], bf16, ca) for i in range(2)]
            cntP = sb("cntP", [P, NG, NB], f32, ca)
            sroot = sb("sroot", [P, GC], f32, ca)
            pA = [ps(f"pA{i}", [P, GC], ca) for i in range(CH)]
            pD = ps("pD", [P, GC], ca)
            (a_oh, a_mm, a_ev, a_deg, a_dcopy, a_dma0, a_dma1, a_cnt, a_root, a_done) = (
                sem("a_" + n) for n in ("oh", "mm", "ev", "deg", "dcopy", "dma0", "dma1", "cnt", "root", "done"))
            a_dma = (a_dma0, a_dma1)
            cntT = gp[:, :, :, :].rearrange("p b k d -> p (b k d)").bitcast(f32)[:, 0:NBP * P]

            def steps(body):
                def pair(m):
                    for t in range(2 * NCH):
                        body(m * 2 + t // NCH, t % NCH, t % 2, G)
                return pair

            with nc.Block() as block:
                @block.vector
                def _(dve):
                    flag = dve.value_load(ctl[0:1, FLAG:FLAG + 1], min_val=0, max_val=1)

                    def hot(g, c, p, nj):
                        n = g * NCH + c
                        wait(dve, a_mm, (n - 1) * CH)
                        for j in range(nj):
                            for v in range(2):
                                last = nc.vector.tensor_tensor(
                                    ohe[p][:, j, v], iotaN[:, :, :],
                                    tab[:, ds(g * G + j, 1), v, c * CH:(c + 1) * CH].to_broadcast([P, P, CH]),
                                    ALU.is_equal)
                        last.then_inc(a_oh, 1)
                        if c == 2 and not (isinstance(g, int) and g == 0):
                            degrees(g - 1)

                    def degrees(g, cols=GC):
                        dve.wait_ge(a_deg, (g + 1) * NCH)
                        nc.vector.tensor_scalar(dinvT[:, ds(g * GC, cols)], pD[:, 0:cols], 1.0, None,
                                                ALU.add).then_inc(a_dcopy, 1)

                    with dve.If(flag > 0):
                        nc.vector.memset(dinvT[:, NB * P:NBP * P], 1.0).then_inc(a_cnt, 1)
                        pair = steps(hot)
                        pair(0)
                        with dve.Fori(1, NG // 2) as m:
                            pair(m)
                        for c in range(NCH):
                            hot(NG - 1, c, c % 2, 1)
                        degrees(NG - 1, P)
                        dve.wait_ge(a_ev, NG * NCH * CH)
                        nc.vector.tensor_reduce(cntN[:, :], cntP[:, :, :].rearrange("p g s -> p s g"), axis=AX.X,
                                                op=ALU.add).then_inc(a_cnt, 1)
                        dve.wait_ge(a_dcopy, NG)
                    with dve.Else():
                        nc.vector.memset(dinvT[:, :], 1.0)
                        nc.vector.memset(cntT, 0.0)
                        dve.drain()
                        with dve.Fori(0, N_EDGES) as e:
                            s = dve.value_load(src1[0:1, ds(e, 1)], min_val=0, max_val=N_NODES - 1)
                            d = dve.value_load(dst1[0:1, ds(e, 1)], min_val=0, max_val=N_NODES - 1)
                            nc.vector.tensor_scalar(dinvT[:, ds(d, 1)], dinvT[:, ds(d, 1)], 1.0, None, ALU.add)
                            nc.vector.tensor_scalar(cntT[:, ds(s, 1)], cntT[:, ds(s, 1)], 1.0, None, ALU.add)
                            dve.drain()
                        with dve.Fori(0, NB) as b:
                            nc.vector.tensor_tensor(sroot[:, 0:P], cntT[:, ds(b * P, P)], ident[:, :], ALU.mult)
                            dve.drain()
                            nc.vector.tensor_reduce(cntN[:, ds(b, 1)], sroot[:, 0:P], axis=AX.X, op=ALU.add)
                            dve.drain()
                    dve.drain().then_inc(a_done, 1)

                    def invert(g):
                        dve.wait_ge(a_root, g + 1)
                        nc.vector.reciprocal(dinvT[:, ds(g * GC, GC)], sroot[:, :]).then_inc(a_dcopy, 1)
                        dve.drain().then_inc(a_done, 1)
                    with dve.Fori(0, NG) as g:
                        invert(g)

                @block.tensor
                def _(pe):
                    flag = pe.value_load(ctl[0:1, FLAG:FLAG + 1], min_val=0, max_val=1)

                    def add_degrees(g, c, p, nj):
                        n = g * NCH + c
                        pe.wait_ge(a_ev, (n + 1) * CH)
                        if c == 0:
                            wait(pe, a_dcopy, g)
                        for i in range(CH):
                            last = nc.tensor.matmul(pD[:, 0:nj * P], onesb[:, :], blk[p][:, i, 0:nj * P],
                                                    start=c == 0 and i == 0, stop=c == NCH - 1 and i == CH - 1)
                        last.then_inc(a_deg, 1)

                    def count(g, c, p, nj):
                        n = g * NCH + c
                        pe.wait_ge(a_oh, n + 1)
                        for i in range(CH):
                            wait(pe, a_ev, (n - 1) * CH + i + 1)
                            for j in range(nj):
                                last = nc.tensor.matmul(pA[i][:, j * P:(j + 1) * P], ohe[p][:, j, 0, :, i],
                                                        ohe[p][:, j, 1, :, i], start=True, stop=True)
                            last.then_inc(a_mm, 1)
                        if not (isinstance(g, int) and g == 0 and c == 0):
                            if c:
                                add_degrees(g, c - 1, 1 - p, nj)
                            else:
                                add_degrees(g - 1, NCH - 1, 1 - p, G)

                    with pe.If(flag > 0):
                        pair = steps(count)
                        pair(0)
                        with pe.Fori(1, NG // 2) as m:
                            pair(m)
                        for c in range(NCH):
                            count(NG - 1, c, c % 2, 1)
                        add_degrees(NG - 1, NCH - 1, (NCH - 1) % 2, 1)

                @block.scalar
                def _(act):
                    flag = act.value_load(ctl[0:1, FLAG:FLAG + 1], min_val=0, max_val=1)

                    def leave(g, c, p, nj):
                        n = g * NCH + c
                        wait(act, a_dma[p], (n - p) * 8)
                        wait(act, a_deg, n - 1)
                        for i in range(CH):
                            act.wait_ge(a_mm, n * CH + i + 1)
                            nc.scalar.activation(blk[p][:, i, 0:nj * P], pA[i][:, 0:nj * P], ACT.Copy,
                                                 accum_out=cntP[:, ds(g, 1), c * CH + i]).then_inc(a_ev, 1)

                    with act.If(flag > 0):
                        pair = steps(leave)
                        pair(0)
                        with act.Fori(1, NG // 2) as m:
                            pair(m)
                        for c in range(NCH):
                            leave(NG - 1, c, c % 2, 1)
                    act.wait_ge(a_done, 1)
                    with act.Fori(0, NG) as g:
                        act.wait_ge(a_done, g + 1)
                        nc.scalar.activation(sroot[:, :], dinvT[:, ds(g * GC, GC)], ACT.Sqrt).then_inc(a_root, 1)

                @block.sync
                def _(sp):
                    flag = sp.value_load(ctl[0:1, FLAG:FLAG + 1], min_val=0, max_val=1)

                    def save(g, c, p, nj):
                        n = g * NCH + c
                        sp.wait_ge(a_ev, (n + 1) * CH)
                        sp.dma_start(adj[ds(g, 1), c, :, :, 0:nj * P].rearrange("o p i n -> (o p) i n"),
                                     blk[p][:, :, 0:nj * P]).then_inc(a_dma[p], 16)

                    with sp.If(flag > 0):
                        pair = steps(save)
                        pair(0)
                        with sp.Fori(1, NG // 2) as m:
                            pair(m)
                        for c in range(NCH):
                            save(NG - 1, c, c % 2, 1)
                        sp.wait_ge(a_dma0, 16 * ((NG * NCH + 1) // 2))
                        sp.wait_ge(a_dma1, 16 * (NG * NCH // 2))

        def table_block(name, W):
            ct = ExitStack()
            with ct:
                hs = [sb(f"{name}_hs{i}", [P, GC], f32, ct) for i in range(2)]
                rem = [sb(f"{name}_rem{i}", [P, GC], f32, ct) for i in range(2)]
                pG = [ps(f"{name}_p{i}", [P, GC], ct) for i in range(2)]
                t_hs, t_mm, t_hi, t_rem, t_mid, t_lo = (
                    sem(name + "_" + n) for n in ("hs", "mm", "hi", "rem", "mid", "lo"))

                def part(g, k):
                    return gp[:, ds(g * G, G), k, :]

                def rows4(t):
                    return t[:, :].rearrange("p (k d) -> p k d", d=D)

                def each(eng, body):
                    body(0, 0)
                    body(1, 1)
                    with eng.Fori(1, NG // 2) as i:
                        body(i * 2, 0)
                        body(i * 2 + 1, 1)
                    body(NG - 1, 0)

                with nc.Block() as block:
                    @block.vector
                    def _(dve):
                        def load(g, p):
                            wait(dve, t_mm, g - 1)
                            nc.vector.tensor_tensor(hs[p][:, :], hT[:, ds(g * GC, GC)],
                                                    dinvT[:, ds(g * GC, GC)], ALU.mult).then_inc(t_hs, 1)

                        def split(g, p):
                            dve.wait_ge(t_hi, g + 1)
                            wait(dve, t_mid, g - 1)
                            wait(dve, t_lo, g - 1)
                            nc.vector.tensor_tensor(rows4(rem[p]), rows4(pG[p]), part(g, 0),
                                                    ALU.subtract).then_inc(t_rem, 1)
                            dve.wait_ge(t_mid, g + 1)
                            nc.vector.tensor_tensor(part(g, 2), rows4(rem[p]), part(g, 1),
                                                    ALU.subtract).then_inc(t_lo, 1)
                        load(0, 0)
                        load(1, 1)
                        split(0, 0)

                        def two(g):
                            load(g + 1, 0)
                            split(g, 1)
                            load(g + 2, 1)
                            split(g + 1, 0)
                        two(1)
                        with dve.Fori(1, (NG - 3) // 2) as i:
                            two(i * 2 + 1)
                        load(NG - 1, 0)
                        split(NG - 2, 1)
                        split(NG - 1, 0)

                    @block.tensor
                    def _(pe):
                        def mul(g, p):
                            pe.wait_ge(t_hs, g + 1)
                            wait(pe, t_rem, g - 1)
                            for k in range(G):
                                last = nc.tensor.matmul(pG[p][:, k * D:(k + 1) * D],
                                                        hs[p][:, k * P:(k + 1) * P], W[:, :],
                                                        start=True, stop=True)
                            last.then_inc(t_mm, 1)
                        each(pe, mul)

                    @block.scalar
                    def _(act):
                        def take(g, p):
                            act.wait_ge(t_mm, g + 1)
                            nc.scalar.activation(part(g, 0), rows4(pG[p]), ACT.Copy).then_inc(t_hi, 1)
                            act.wait_ge(t_rem, g + 1)
                            nc.scalar.activation(part(g, 1), rows4(rem[p]), ACT.Copy).then_inc(t_mid, 1)
                        each(act, take)

        def gcn_block(name, bias):
            cg = ExitStack()
            with cg:
                ring = sb(name + "_ring", [P, NCH, CH, GC], bf16, cg)
                sc = [sb(f"{name}_sc{i}", [P, GC], f32, cg) for i in range(2)]
                pO = [ps(f"{name}_p{i}", [P, GC], cg) for i in range(2)]
                gT = ring[:, :, :, :].rearrange("p c i n -> p (c i n)").bitcast(f32)[:, 0:NBP * P]
                g_in = [sem(f"{name}_in{c}") for c in range(NCH)]
                g_chunk, g_mm, g_sc, g_out, g_self = (
                    sem(name + "_" + n) for n in ("chunk", "mm", "sc", "out", "self"))

                def each(eng, body):
                    body(0, 0, G)
                    body(1, 1, G)
                    with eng.Fori(1, NG // 2) as i:
                        body(i * 2, 0, G)
                        body(i * 2 + 1, 1, G)
                    body(NG - 1, 0, 1)

                with nc.Block() as block:
                    @block.sync
                    def _(sp):
                        flag = sp.value_load(ctl[0:1, FLAG:FLAG + 1], min_val=0, max_val=1)

                        def load(g, p, nj):
                            for c in range(NCH):
                                wait(sp, g_chunk, (g - 1) * NCH + c + 1)
                                sp.dma_start(ring[:, c, :, 0:nj * P],
                                             adj[ds(g, 1), c, :, :, 0:nj * P].rearrange("o p i n -> (o p) i n")
                                             ).then_inc(g_in[c], 16)
                        with sp.If(flag > 0):
                            each(sp, load)

                    @block.tensor
                    def _(pe):
                        flag = pe.value_load(ctl[0:1, FLAG:FLAG + 1], min_val=0, max_val=1)

                        def own(g, p, nj, start):
                            for k in range(nj):
                                for part in range(3):
                                    last = nc.tensor.matmul(
                                        pO[p][:, k * P:(k + 1) * P],
                                        gp[:, ds(g * G + k, 1), part, :].rearrange("p o d -> p (o d)"),
                                        identb[:, :], start=start and part == 0, stop=part == 2,
                                        skip_group_check=True)
                            return last

                        def add(g, p, nj):
                            wait(pe, g_sc, g - 1)
                            for c in range(NCH):
                                pe.wait_ge(g_in[c], g * 16 + 16)
                                for i in range(CH):
                                    for part in range(3):
                                        last = nc.tensor.matmul(
                                            pO[p][:, 0:nj * P], gp[:, c * CH + i, part, :],
                                            ring[:, c, i, 0:nj * P], start=c == 0 and i == 0 and part == 0,
                                            stop=c == NCH - 1 and i == CH - 1 and part == 2,
                                            skip_group_check=True)
                                last.then_inc(g_chunk, 1)
                            own(g, p, nj, False).then_inc(g_mm, 1)

                        with pe.If(flag > 0):
                            each(pe, add)
                        with pe.Else():
                            with pe.Fori(0, NG) as g:
                                pe.wait_ge(g_sc, g + 1)
                                own(g, 0, G, True).then_inc(g_self, 1)

                    @block.vector
                    def _(dve):
                        flag = dve.value_load(ctl[0:1, FLAG:FLAG + 1], min_val=0, max_val=1)

                        def scale(g, p, nj):
                            dve.wait_ge(g_mm, g + 1)
                            wait(dve, g_out, g - 1)
                            nc.vector.tensor_tensor(sc[p][:, 0:nj * P], pO[p][:, 0:nj * P],
                                                    dinvT[:, ds(g * GC, nj * P)], ALU.mult).then_inc(g_sc, 1)
                        with dve.If(flag > 0):
                            each(dve, scale)
                        with dve.Else():
                            nc.vector.memset(sc[0][:, :], 0.0).then_inc(g_sc, 1)
                            with dve.Fori(0, NG) as g:
                                dve.wait_ge(g_self, g + 1)
                                nc.vector.tensor_copy(gT[:, ds(g * GC, GC)], pO[0][:, :])
                                nc.vector.tensor_copy(hT[:, ds(g * GC, GC)], pO[0][:, :])
                                dve.drain().then_inc(g_sc, 1)
                            with dve.Fori(0, N_EDGES) as e:
                                s = dve.value_load(src1[0:1, ds(e, 1)], min_val=0, max_val=N_NODES - 1)
                                d = dve.value_load(dst1[0:1, ds(e, 1)], min_val=0, max_val=N_NODES - 1)
                                nc.vector.tensor_tensor(hT[:, ds(d, 1)], hT[:, ds(d, 1)], gT[:, ds(s, 1)],
                                                        ALU.add)
                                dve.drain()
                            with dve.Fori(0, NG) as g:
                                nc.vector.tensor_tensor(hT[:, ds(g * GC, GC)], hT[:, ds(g * GC, GC)],
                                                        dinvT[:, ds(g * GC, GC)], ALU.mult)
                                dve.drain()
                                nc.vector.tensor_scalar(hT[:, ds(g * GC, GC)], hT[:, ds(g * GC, GC)],
                                                        bias[:, 0:1], 0.0, ALU.add, ALU.max)
                                dve.drain()

                    @block.scalar
                    def _(act):
                        flag = act.value_load(ctl[0:1, FLAG:FLAG + 1], min_val=0, max_val=1)

                        def leave(g, p, nj):
                            act.wait_ge(g_sc, g + 1)
                            nc.scalar.activation(hT[:, ds(g * GC, nj * P)], sc[p][:, 0:nj * P], ACT.Relu,
                                                 bias=bias[:, 0:1]).then_inc(g_out, 1)
                        with act.If(flag > 0):
                            each(act, leave)

        table_block("t1", W1s)
        gcn_block("g1", b1c)
        table_block("t2", W2s)
        gcn_block("g2", b2c)
        norm_block("n2", True)

        hN = gp[:, :, :, :].rearrange("p b k d -> p (b k d)").bitcast(f32)[:, 0:NBP * P]
        ch = ExitStack()
        with ch:
            hs = [sb(f"h_hs{i}", [P, GC], f32, ch) for i in range(2)]
            zt = [sb(f"h_zt{i}", [P, GC], f32, ch) for i in range(2)]
            hT4 = hT[:, :].rearrange("p (b n) -> p b n", n=P)
            pG, pF, pZ = ([ps(f"h_{n}{i}", [P, GC], ch) for i in range(2)] for n in "gfz")
            h_hs, h_mm, h_n, h_t, h_z, h_zz = (sem("h_" + n) for n in ("hs", "mm", "n", "t", "z", "zz"))

            def each(eng, body):
                body(0, 0)
                body(1, 1)
                with eng.Fori(1, NG // 2) as i:
                    body(i * 2, 0)
                    body(i * 2 + 1, 1)
                body(NG - 1, 0)

            with nc.Block() as block:
                @block.scalar
                def _(act):
                    def copy(g, p):
                        wait(act, h_mm, g - 1)
                        nc.scalar.activation(hs[p][:, :], hT[:, ds(g * GC, GC)], ACT.Copy).then_inc(h_hs, 1)

                    def bias(g, p):
                        act.wait_ge(h_mm, g + 1)
                        nc.scalar.activation(hT4[:, ds(g * G, G), :], pF[p][:, :].rearrange(
                            "p (k n) -> p k n", n=P), ACT.Identity,
                                             bias=bnc[:, 0:1]).then_inc(h_t, 1)
                    copy(0, 0)
                    copy(1, 1)
                    bias(0, 0)
                    with act.Fori(0, (NG - 3) // 2) as i:
                        copy(i * 2 + 2, 0)
                        bias(i * 2 + 1, 1)
                        copy(i * 2 + 3, 1)
                        bias(i * 2 + 2, 0)
                    copy(NG - 1, 0)
                    bias(NG - 2, 1)
                    bias(NG - 1, 0)

                @block.tensor
                def _(pe):
                    def mul(g, p):
                        pe.wait_ge(h_hs, g + 1)
                        wait(pe, h_t, g - 1)
                        wait(pe, h_n, g - 1)
                        wait(pe, h_z, g - 1)
                        for k in range(G):
                            for o, W in ((pG, WnT), (pZ, Wl1T)):
                                nc.tensor.matmul(o[p][:, k * D:(k + 1) * D], hs[p][:, k * P:(k + 1) * P], W[:, :],
                                                 start=True, stop=True)
                        nc.tensor.matmul(pF[p][:, :], WnT[:, :], hs[p][:, :], start=True,
                                         stop=True).then_inc(h_mm, 1)
                    each(pe, mul)

                @block.vector
                def _(dve):
                    def four(t):
                        return t.rearrange("p (k d) -> p k d", d=D)

                    def leave(g, p):
                        dve.wait_ge(h_mm, g + 1)
                        nc.vector.tensor_tensor(four(hN[:, ds(g * GC, GC)]), four(pG[p][:, :]),
                                                bnr[:, :].unsqueeze(1).to_broadcast([P, G, D]),
                                                ALU.add).then_inc(h_n, 1)
                        wait(dve, h_zz, g - 1)
                        nc.vector.tensor_tensor(four(zt[p][:, :]), four(pZ[p][:, :]),
                                                blr[:, :].unsqueeze(1).to_broadcast([P, G, D]),
                                                ALU.add).then_inc(h_z, 1)
                        dve.wait_ge(h_z, g + 1)
                        nc.vector.tensor_tensor(xN[:, ds(g * G, G), :], xN[:, ds(g * G, G), :],
                                                four(zt[p][:, :]), ALU.add).then_inc(h_zz, 1)
                    each(dve, leave)

        absT = dinvT
        ce = ExitStack()
        with ce:
            difT = sb("difT", [P, NBP * P], f32, ce)
            agg = sb("agg", [P, 2, D], f32, ce)
            cr = ExitStack()
            COLS = CH * P
            idr = [sb(f"idr{c}", [P, 2, COLS], bf16, cr) for c in range(NCH)]
            UN = (4, 3)
            pick = [sb(f"pick{i}", [P, 2, G * P], f32, cr) for i in range(2)]
            put = [sb(f"put{i}", [P, G, P], f32, cr) for i in range(2)]
            dif = [sb(f"dif{i}", [P, G, 2, D], f32, cr) for i in range(2)]
            pE = [ps(f"pE{i}", [P, G, P], ce) for i in range(4)]
            pAg = ps("pAg", [P, 2, D], ce)
            pTr = ps("pTr", [P, 2, P], ce)
            e_in = [sem(f"e_in{c}") for c in range(NCH)]
            e_pick, e_put, e_gath, e_abs, e_dif, e_sum, e_agg, e_tr, e_out, e_zero, e_outD = (
                sem("e_" + n) for n in ("pick", "put", "gath", "abs", "dif", "sum", "agg", "tr", "out", "zero",
                                        "outd"))
            NU = 2 * NCH

            with nc.Block() as block:
                @block.sync
                def _(sp):
                    flag = sp.value_load(ctl[0:1, FLAG:FLAG + 1], min_val=0, max_val=1)

                    def load(a):
                        for c in range(NCH):
                            wait(sp, e_pick, (a - 1) * NU + 2 * c + 2)
                            for v in range(2):
                                sp.dma_start(idr[c][:, v, :], rows[v][ds(a, 1), c * CH:(c + 1) * CH, :].rearrange(
                                    "o b r -> (o b r)").partition_broadcast(P)).then_inc(e_in[c], 16)
                    with sp.If(flag > 0):
                        load(0)
                        with sp.Fori(1, NB) as a:
                            load(a)

                @block.vector
                def _(dve):
                    flag = dve.value_load(ctl[0:1, FLAG:FLAG + 1], min_val=0, max_val=1)

                    def hot(a):
                        for u in range(NU):
                            c, n, p = u // 2, UN[u % 2], u % 2
                            if u % 2 == 0:
                                dve.wait_ge(e_in[c], a * 32 + 32)
                            wait(dve, e_gath, a * NU + u - 1)
                            o = (u % 2) * UN[0] * P
                            nc.vector.tensor_scalar(pick[p][:, 0, 0:n * P], idr[c][:, 0, o:o + n * P],
                                                    idCol[:, 0:1], None, ALU.is_equal)
                            nc.vector.tensor_scalar(pick[p][:, 1, 0:n * P], idr[c][:, 1, o:o + n * P],
                                                    idCol[:, 0:1], -1.0, ALU.is_equal,
                                                    ALU.mult).then_inc(e_pick, 1)
                            wait(dve, e_sum, a * NU + u - 1)
                            b0 = c * CH + (u % 2) * UN[0]
                            for k in range(n):
                                last = nc.vector.tensor_scalar(
                                    put[p][:, k, :], iotaN[:, :, 0],
                                    tab[:, b0 + k, 0, ds(a, 1)], None, ALU.is_equal)
                            last.then_inc(e_put, 1)
                    with dve.If(flag > 0):
                        hot(0)
                        with dve.Fori(1, NB) as a:
                            hot(a)
                    with dve.Else():
                        nc.vector.memset(absT[:, :], 0.0)
                        nc.vector.memset(difT[:, :], 0.0)
                        dve.drain()
                        d1, d2 = agg[:, 0, 0:1], agg[:, 1, 0:1]
                        with dve.Fori(0, N_EDGES) as e:
                            s = dve.value_load(src1[0:1, ds(e, 1)], min_val=0, max_val=N_NODES - 1)
                            d = dve.value_load(dst1[0:1, ds(e, 1)], min_val=0, max_val=N_NODES - 1)
                            nc.vector.tensor_tensor(d1, hT[:, ds(s, 1)], hT[:, ds(d, 1)], ALU.subtract)
                            nc.vector.tensor_tensor(d2, hT[:, ds(d, 1)], hT[:, ds(s, 1)], ALU.subtract)
                            dve.drain()
                            nc.vector.tensor_tensor(difT[:, ds(s, 1)], difT[:, ds(s, 1)], d2, ALU.add)
                            dve.drain()
                            nc.vector.tensor_tensor(d1, d1, d2, ALU.max)
                            dve.drain()
                            nc.vector.tensor_tensor(absT[:, ds(s, 1)], absT[:, ds(s, 1)], d1, ALU.add)
                            dve.drain()

                @block.tensor
                def _(pe):
                    flag = pe.value_load(ctl[0:1, FLAG:FLAG + 1], min_val=0, max_val=1)

                    def gather(a, u):
                        c, n, p = u // 2, UN[u % 2], u % 2
                        pe.wait_ge(e_pick, a * NU + u + 1)
                        wait(pe, e_dif, a * NU + u - 1)
                        wait(pe, e_abs, a * NU + u - 1)
                        b0 = c * CH + (u % 2) * UN[0]
                        for k in range(n):
                            nc.tensor.matmul(pE[p][:, k, :], pick[p][:, 0, k * P:(k + 1) * P],
                                             hN[:, ds(a * P, P)], start=True, stop=False)
                            last = nc.tensor.matmul(pE[p][:, k, :], pick[p][:, 1, k * P:(k + 1) * P],
                                                    hN[:, (b0 + k) * P:(b0 + k + 1) * P], start=False, stop=True)
                        last.then_inc(e_gath, 1)

                    def total(a, u):
                        n, p = UN[u % 2], u % 2
                        pe.wait_ge(e_put, a * NU + u + 1)
                        pe.wait_ge(e_abs, a * NU + u + 1)
                        pe.wait_ge(e_dif, a * NU + u + 1)
                        if u == 0:
                            wait(pe, e_agg, a)
                        for k in range(n):
                            last = nc.tensor.matmul(pAg[:, :, :], put[p][:, k, :], dif[p][:, k, :, :],
                                                    start=u == 0 and k == 0, stop=u == NU - 1 and k == n - 1)
                        last.then_inc(e_sum, 1)

                    def turn(a):
                        pe.wait_ge(e_agg, a + 1)
                        wait(pe, e_outD, a)
                        for v in range(2):
                            last = nc.tensor.transpose(pTr[:, v, :], agg[:, v, :], ident[:, :])
                        last.then_inc(e_tr, 1)

                    def all_units(a):
                        gather(a, 0)
                        for u in range(NU):
                            if u + 1 < NU:
                                gather(a, u + 1)
                            total(a, u)
                        turn(a)
                    with pe.If(flag > 0):
                        all_units(0)
                        with pe.Fori(1, NB) as a:
                            all_units(a)

                @block.scalar
                def _(act):
                    flag = act.value_load(ctl[0:1, FLAG:FLAG + 1], min_val=0, max_val=1)

                    def leave(a):
                        for u in range(NU):
                            n, p = UN[u % 2], u % 2
                            act.wait_ge(e_gath, a * NU + u + 1)
                            wait(act, e_sum, a * NU + u - 1)
                            nc.scalar.activation(dif[p][:, 0:n, 0, :], pE[p][:, 0:n, :], ACT.Abs).then_inc(e_abs, 1)
                            nc.scalar.activation(dif[p][:, 0:n, 1, :], pE[p][:, 0:n, :], ACT.Copy,
                                                 scale=-1.0).then_inc(e_dif, 1)
                        act.wait_ge(e_sum, (a + 1) * NU)
                        wait(act, e_tr, a)
                        nc.scalar.activation(agg[:, :, :], pAg[:, :, :], ACT.Copy).then_inc(e_agg, 1)
                        act.wait_ge(e_tr, a + 1)
                        nc.scalar.activation(absT[:, ds(a * P, P)], pTr[:, 0, :], ACT.Copy)
                        nc.scalar.activation(difT[:, ds(a * P, P)], pTr[:, 1, :], ACT.Copy).then_inc(e_outD, 1)
                    with act.If(flag > 0):
                        leave(0)
                        with act.Fori(1, NB) as a:
                            leave(a)

            cr.close()
            hb = [sb(f"f_hb{i}", [P, 3, P], f32, ce) for i in range(2)]
            cnt1 = sb("f_cnt1", [P, NB], f32, ce)
            rcnt = sb("f_rcnt", [P, NB], f32, ce)
            u1, u2, u3 = ([sb(f"f_{n}{i}", [P, D], f32, ce) for i in range(2)] for n in ("u", "v", "w"))
            f_in, f_mm, f_u1, f_u2, f_u3, f_dma0, f_dma1, f_c = (
                sem("f_" + n) for n in ("in", "mm", "u1", "u2", "u3", "dma0", "dma1", "c"))
            f_dma = (f_dma0, f_dma1)

            def each(eng, body):
                body(0, 0)
                body(1, 1)
                with eng.Fori(1, NB // 2) as i:
                    body(i * 2, 0)
                    body(i * 2 + 1, 1)
                body(NB - 1, 0)

            with nc.Block() as block:
                @block.scalar
                def _(act):
                    def load(b, p):
                        wait(act, f_mm, b - 1)
                        for k, t in enumerate((hT, absT, difT)):
                            last = nc.scalar.activation(hb[p][:, k, :], t[:, ds(b * P, P)], ACT.Copy)
                        last.then_inc(f_in, 1)
                    each(act, load)

                @block.tensor
                def _(pe):
                    def mul(b, p):
                        pe.wait_ge(f_in, b + 1)
                        wait(pe, f_u2, b - 1)
                        wait(pe, f_u1, b - 1)
                        nc.tensor.matmul(pE[2 + p][:, 0, :], hb[p][:, 0, :], Wl2T[:, :], start=True, stop=False)
                        nc.tensor.matmul(pE[2 + p][:, 0, :], hb[p][:, 1, :], W22[:, :], start=False, stop=False)
                        nc.tensor.matmul(pE[2 + p][:, 0, :], hb[p][:, 2, :], W12[:, :], start=False, stop=True)
                        nc.tensor.matmul(pE[2 + p][:, 1, :], hb[p][:, 0, :], W12[:, :], start=True,
                                         stop=True).then_inc(f_mm, 1)
                    each(pe, mul)

                @block.vector
                def _(dve):
                    nc.vector.tensor_scalar(cnt1[:, :], cntN[:, :], 1.0, None, ALU.max).then_inc(f_c, 1)
                    dve.wait_ge(f_c, 1)
                    nc.vector.reciprocal(rcnt[:, :], cnt1[:, :]).then_inc(f_c, 1)
                    dve.wait_ge(f_c, 2)

                    def leave(b, p):
                        dve.wait_ge(f_mm, b + 1)
                        wait(dve, f_u2, b - 1)
                        nc.vector.tensor_tensor(u1[p][:, :], pE[2 + p][:, 1, :], ber[:, :],
                                                ALU.add).then_inc(f_u1, 1)
                        dve.wait_ge(f_u1, b + 1)
                        wait(dve, f_u3, b - 1)
                        nc.vector.scalar_tensor_tensor(out=u2[p][:, :], in0=u1[p][:, :], scalar=cntN[:, ds(b, 1)],
                                                       in1=pE[2 + p][:, 0, :], op0=ALU.mult,
                                                       op1=ALU.add).then_inc(f_u2, 1)
                        dve.wait_ge(f_u2, b + 1)
                        wait(dve, f_dma[p], (b - p) * 8)
                        nc.vector.scalar_tensor_tensor(out=u3[p][:, :], in0=u2[p][:, :], scalar=rcnt[:, ds(b, 1)],
                                                       in1=xN[:, ds(b, 1), :].rearrange("p o d -> p (o d)"),
                                                       op0=ALU.mult, op1=ALU.add).then_inc(f_u3, 1)
                    each(dve, leave)

                @block.sync
                def _(sp):
                    def save(b, p, n=P):
                        sp.wait_ge(f_u3, b + 1)
                        sp.dma_start(out[ds(b * P, n), :], u3[p][0:n, :]).then_inc(f_dma[p], 16)
                    with sp.Fori(0, NB // 2) as i:
                        save(i * 2, 0)
                        save(i * 2 + 1, 1)
                    save(NB - 1, 0, LAST)
                    sp.wait_ge(f_dma0, 16 * (NB // 2 + 1))
                    sp.wait_ge(f_dma1, 16 * (NB // 2))


_NAMES = ("x", "src", "dst", "L0_gnn_W1", "L0_gnn_b1", "L0_gnn_W2", "L0_gnn_b2", "L1_gnn_W_neigh",
          "L1_gnn_b_neigh", "L1_gnn_W_edge", "L1_gnn_b_edge", "L1_gnn_W_lin", "L1_gnn_b_lin")


def kernel(**inputs):
    import numpy as np
    import concourse.bacc as bacc
    from concourse.bass_utils import run_bass_kernel_spmd

    nc = bacc.Bacc("TRN2", target_bir_lowering=False, num_devices=1)
    arrays, args = {}, []
    for name in _NAMES:
        a = np.ascontiguousarray(inputs[name])
        arrays["in_" + name] = a
        args.append(nc.dram_tensor("in_" + name, a.shape, mybir.dt.from_np(a.dtype), kind="ExternalInput").ap())
    out = nc.dram_tensor("out", (N_NODES, D), mybir.dt.float32, kind="ExternalOutput").ap()
    gnn(nc, *args, out)
    got = run_bass_kernel_spmd(nc, [arrays], core_ids=[0])
    return got.results[0]["out"]
```

```python
from contextlib import ExitStack

import concourse.bass as bass
from concourse import mybir

P = 128
N_NODES, N_EDGES, D = 6250, 200000, 128
NB = -(-N_NODES // P)
LAST = N_NODES - (NB - 1) * P
G = 4
NG = -(-NB // G)
NBP = NG * G
GC = G * P
CH = 7
NCH = NB // CH
WIN, WC = 36, 9
NWC = WIN // WC
FULL_G = N_EDGES // (P * P)
TAIL = N_EDGES - FULL_G * P * P
TAIL_ROWS, TAIL_EDGES = TAIL // P, TAIL % P
EG = FULL_G + 1
NT = EG * P
PAD_DST = 200 * P
EPS = 1e-5


def gnn(nc, x, src, dst, W1, b1, W2, b2, Wn, bn, We, be, Wl, bl, out):
    f32, bf16, i32, u8 = mybir.dt.float32, mybir.dt.bfloat16, mybir.dt.int32, mybir.dt.uint8
    u16 = mybir.dt.uint16
    f32r = mybir.dt.float32r
    ALU = mybir.AluOpType
    ACT = mybir.ActivationFunctionType
    AX = mybir.AxisListType
    ds = bass.ds

    adj = nc.dram_tensor("adj", (NG, NCH, P, CH, GC), bf16, kind="Internal").ap()
    rows = nc.dram_tensor("slot_rows", (2, NB, NB, P // 2), u16, kind="Internal").ap()

    src1 = src.rearrange("(o e) -> o e", o=1)
    dst1 = dst.rearrange("(o e) -> o e", o=1)

    ctx = ExitStack()
    with ctx:
        def sb(name, shape, dt, c=ctx):
            return c.enter_context(nc.sbuf_tensor(name, shape, dt))

        def ps(name, shape, c):
            return c.enter_context(nc.psum_tensor(name, shape, f32))

        def sem(name):
            return ctx.enter_context(nc.semaphore(name))

        def wait(eng, s, value):
            if not isinstance(value, int) or value > 0:
                eng.wait_ge(s, value)

        xN = sb("xN", [P, NBP, D], f32)
        hT = sb("hT", [P, NBP * P], f32)
        dinvT = sb("dinvT", [P, NBP * P], f32)
        tab = sb("tab", [P, NB, 2, NB], bf16)
        cntN = sb("cntN", [P, NB], f32)
        ident = sb("ident", [P, P], f32)
        identb = sb("identb", [P, P], bf16)
        onesf = sb("onesf", [P, P], f32)
        iotaN = sb("iotaN", [P, P, CH], bf16)
        idCol = sb("idCol", [P, 1], f32)
        idColF = sb("idColF", [P, 1], i32)
        WnT, Wl1T = (sb(n, [P, D], f32) for n in ("WnT", "Wl1T"))
        Wout = sb("Wout", [P, 4, D], f32)
        Wl2T, W12, W22, WD = (Wout[:, i, :] for i in range(4))
        b1c, b2c, bec, bnc = (sb(n, [P, 1], f32) for n in ("b1c", "b2c", "bec", "bnc"))
        bnr, blr, ber = (sb(n, [P, D], f32) for n in ("bnr", "blr", "ber"))
        epsC = sb("epsC", [P, 1], f32)
        ctl = sb("ctl", [1, 64], i32)
        FLAG = 60

        W1s, W2s = sb("W1s", [P, D], f32), sb("W2s", [P, D], f32)
        onesb = sb("onesb", [P, P], bf16)
        tri = sb("tri", [P, P], bf16)
        gp = sb("gp", [P, NBP, 3, D], bf16)

        c0 = ExitStack()
        with c0:
            keyC = sb("keyC", [P, NT], f32, c0)
            idS = sb("idS", [P, NT], bf16, c0)
            idD = sb("idD", [P, NT], bf16, c0)
            iotaS = sb("iotaS", [P, NB, WIN], bf16, c0)
            iotaR = sb("iotaR", [P, P, WIN], bf16, c0)
            dbase = sb("dbase", [P, NB], f32, c0)
            c1 = ExitStack()
            with c1:
                eD = sb("eD", [P, EG, P], i32, c1)
                eS = sb("eS", [P, EG, P], i32, c1)
                blkD = sb("blkD", [P, EG, P], i32, c1)
                blkS = sb("blkS", [P, EG, P], i32, c1)
                keyR = sb("keyR", [P, EG, P], f32, c1)
                tmax = sb("tmax", [P, EG], f32, c1)
                less = sb("less", [P, NB, EG], f32, c1)
                lessN = sb("lessN", [P, NB], f32, c1)
                dbN = sb("dbN", [P, NB], f32, c1)
                wld = sb("wld", [P, 5, D], f32, c1)
                pT = [ps(f"pT{i}", [P, GC], c1) for i in range(4)]
                pW = [ps(f"pW{i}", [P, GC], c1) for i in range(3)]
                s_pre, s_edge, s_w, s_x, s_b = (sem(n) for n in ("s_pre", "s_edge", "s_w", "s_x", "s_b"))
                s_const, s_dvec, s_col, s_colps, s_colout = (
                    sem(n) for n in ("s_const", "s_dvec", "s_col", "s_colps", "s_colout"))
                s_wt, s_wtout, s_win, s_w2, s_w2out = (
                    sem(n) for n in ("s_wt", "s_wtout", "s_win", "s_w2", "s_w2out"))
                s_pool = sem("s_pool")
                with nc.Block() as block:
                    @block.sync
                    def _(sp):
                        sp.wait_ge(s_pre, 2)
                        for e, a in ((eD, dst), (eS, src)):
                            sp.dma_start(e[:, 0:FULL_G, :], a[0:FULL_G * P * P].rearrange(
                                "(g p e) -> p g e", p=P, e=P)).then_inc(s_edge, 16)
                            sp.dma_start(e[0:TAIL_ROWS, FULL_G, :], a[FULL_G * P * P:N_EDGES - TAIL_EDGES]
                                         .rearrange("(p e) -> p e", e=P)).then_inc(s_edge, 16)
                            sp.dma_start(e[TAIL_ROWS:TAIL_ROWS + 1, FULL_G, 0:TAIL_EDGES],
                                         a[N_EDGES - TAIL_EDGES:N_EDGES].rearrange("(p e) -> p e", p=1)
                                         ).then_inc(s_edge, 16)
                        sp.wait_ge(s_pre, 3)
                        sp.dma_start(xN[:, 0:NB - 1, :], x[0:(NB - 1) * P, :].rearrange(
                            "(n p) d -> p n d", p=P)).then_inc(s_x, 16)
                        sp.dma_start(xN[0:LAST, NB - 1, :], x[(NB - 1) * P:N_NODES, :]).then_inc(s_x, 16)
                        sp.wait_ge(s_x, 32)

                    @block.scalar
                    def _(act):
                        for t, w in ((0, Wn), (1, We[:, 0:D]), (2, We[:, D:2 * D]),
                                     (3, Wl[:, 0:D]), (4, Wl[:, D:2 * D])):
                            act.dma_start(wld[:, t, :], w).then_inc(s_w, 16)
                        act.dma_start(W1s[:, :], W1).then_inc(s_b, 16)
                        act.dma_start(W2s[:, :], W2).then_inc(s_b, 16)
                        for c, b in ((b1c, b1), (b2c, b2), (bec, be), (bnc, bn)):
                            act.dma_start(c[:, :], b.rearrange("(p a) -> p a", a=1)).then_inc(s_b, 16)
                        act.dma_start(bnr[:, :], bn.partition_broadcast(P)).then_inc(s_b, 16)
                        act.dma_start(blr[:, :], bl.partition_broadcast(P)).then_inc(s_b, 16)
                        for t, w in enumerate((WnT, Wl1T, Wl2T)):
                            act.wait_ge(s_wt, t + 1)
                            nc.scalar.activation(w[:, :], pW[t][:, 0:D], ACT.Copy).then_inc(s_wtout, 1)
                        act.wait_ge(s_w2, 1)
                        for t, (w, scale) in enumerate(((W12, 1.0), (W22, 2.0), (ber, 1.0))):
                            nc.scalar.activation(w[:, :], pW[0][:, t * D:(t + 1) * D], ACT.Copy,
                                                 scale=scale).then_inc(s_w2out, 1)
                        act.wait_ge(s_w2out, 3)
                        act.wait_ge(s_b, 8 * 16)

                    @block.gpsimd
                    def _(pool):
                        nc.gpsimd.memset(ident[:, :], 0.0).then_inc(s_pool, 1)
                        nc.gpsimd.memset(onesf[:, :], 1.0).then_inc(s_const, 1)
                        nc.gpsimd.memset(onesb[:, :], 1.0).then_inc(s_const, 1)
                        nc.gpsimd.memset(epsC[:, :], EPS).then_inc(s_const, 1)
                        pool.wait_ge(s_pool, 1)
                        nc.gpsimd.affine_select(out=ident[:, :], in_=ident[:, :], compare_op=ALU.not_equal,
                                                fill=1.0, base=0, pattern=[[-1, P]],
                                                channel_multiplier=1).then_inc(s_const, 1)
                        pool.wait_ge(s_const, 3)
                        nc.gpsimd.affine_select(out=tri[:, :], in_=onesb[:, :], compare_op=ALU.is_gt,
                                                fill=0.0, base=0, pattern=[[1, P]],
                                                channel_multiplier=-1).then_inc(s_const, 1)
                        nc.gpsimd.iota(idColF[:, :], pattern=[[0, 1]], base=1,
                                       channel_multiplier=1).then_inc(s_const, 1)
                        for t, step, off in ((dbN, 1, 0), (dbase, NB, 0)):
                            nc.gpsimd.iota(t[:, :], pattern=[[step, NB]], base=off, channel_multiplier=0,
                                           allow_small_or_imprecise_dtypes=True).then_inc(s_const, 1)
                        for t, n, rep, off in ((iotaS, NB, WIN, 0), (iotaN, P, CH, 1), (iotaR, P, WIN, 0)):
                            nc.gpsimd.iota(t[:, :, :], pattern=[[1, n], [0, rep]], base=off,
                                           channel_multiplier=0,
                                           allow_small_or_imprecise_dtypes=True).then_inc(s_const, 1)
                        pool.wait_ge(s_const, 11)

                    @block.vector
                    def _(dve):
                        nc.vector.memset(eD[:, FULL_G, :], PAD_DST).then_inc(s_pre, 1)
                        nc.vector.memset(eS[:, FULL_G, :], 0).then_inc(s_pre, 1)
                        nc.vector.memset(xN[:, NB - 1:NBP, :], 0.0).then_inc(s_pre, 1)
                        dve.wait_ge(s_const, 7)
                        nc.vector.tensor_copy(idCol[:, :], idColF[:, :]).then_inc(s_dvec, 1)
                        nc.vector.tensor_copy(identb[:, :], ident[:, :]).then_inc(s_dvec, 1)
                        dve.wait_ge(s_edge, 6 * 16)
                        nc.vector.tensor_scalar(blkD[:, :, :], eD[:, :, :], 7, None,
                                                ALU.arith_shift_right).then_inc(s_dvec, 1)
                        nc.vector.tensor_scalar(blkS[:, :, :], eS[:, :, :], 7, None,
                                                ALU.arith_shift_right).then_inc(s_dvec, 1)
                        nc.vector.tensor_scalar(eD[:, :, :], eD[:, :, :], P - 1, None,
                                                ALU.bitwise_and).then_inc(s_dvec, 1)
                        nc.vector.tensor_scalar(eS[:, :, :], eS[:, :, :], P - 1, None,
                                                ALU.bitwise_and).then_inc(s_dvec, 1)
                        dve.wait_ge(s_dvec, 6)
                        nc.vector.scalar_tensor_tensor(out=keyR[:, :, :], in0=blkD[:, :, :], scalar=float(NB),
                                                       in1=blkS[:, :, :], op0=ALU.mult,
                                                       op1=ALU.add).then_inc(s_dvec, 1)
                        nc.vector.tensor_reduce(tmax[:, :], blkD[:, :, :], axis=AX.X,
                                                op=ALU.max).then_inc(s_dvec, 1)
                        dve.wait_ge(s_dvec, 8)
                        nc.vector.tensor_scalar(blkS[:, :, :].bitcast(f32), eS[:, :, :], 1.0, None,
                                                ALU.add).then_inc(s_dvec, 1)
                        nc.vector.tensor_scalar(blkD[:, :, :].bitcast(f32), eD[:, :, :], 1.0, None,
                                                ALU.add).then_inc(s_dvec, 1)
                        dve.wait_ge(s_const, 8)
                        nc.vector.tensor_tensor(less[:, :, :], tmax[:, :].unsqueeze(1).to_broadcast([P, NB, EG]),
                                                dbN[:, :].unsqueeze(2).to_broadcast([P, NB, EG]),
                                                ALU.is_lt).then_inc(s_dvec, 1)
                        dve.wait_ge(s_dvec, 11)
                        nc.vector.tensor_reduce(lessN[:, :], less[:, :, :], axis=AX.X,
                                                op=ALU.add).then_inc(s_dvec, 1)
                        n = 0
                        for t in (keyC, idS, idD):
                            for g in range(0, EG, 4):
                                k = min(4, EG - g) * P
                                dve.wait_ge(s_colps, n + 1)
                                nc.vector.tensor_copy(t[:, g * P:g * P + k],
                                                      pT[n % 4][:, 0:k]).then_inc(s_colout, 1)
                                n += 1
                        dve.wait_ge(s_win, 1)
                        nc.vector.tensor_copy(ctl[0:1, 0:NB], pW[1][0:1, 0:NB]).then_inc(s_dvec, 1)
                        dve.wait_ge(s_w2out, 2)
                        nc.vector.scalar_tensor_tensor(out=WD[:, :], in0=W22[:, :], scalar=-0.5, in1=W12[:, :],
                                                       op0=ALU.mult, op1=ALU.add).then_inc(s_dvec, 1)
                        dve.wait_ge(s_dvec, 14)
                        dve.wait_ge(s_colout, n)

                    @block.tensor
                    def _(pe):
                        pe.wait_ge(s_const, 4)
                        pe.wait_ge(s_w, 5 * 16)
                        for t, k in enumerate((0, 3, 4)):
                            nc.tensor.transpose(pW[t][:, 0:D], wld[:, k, :], ident[:, :]).then_inc(s_wt, 1)
                        pe.wait_ge(s_wtout, 3)
                        pe.wait_ge(s_b, 8 * 16)
                        nc.tensor.matmul(pW[0][:, 0:D], wld[:, 1, :], Wl2T[:, :], start=True, stop=True)
                        nc.tensor.matmul(pW[0][:, D:2 * D], wld[:, 2, :], Wl2T[:, :], start=True, stop=True)
                        nc.tensor.matmul(pW[0][:, 2 * D:3 * D], bec[:, 0:1].to_broadcast([P, P]), Wl2T[:, :],
                                         start=True, stop=True).then_inc(s_w2, 1)
                        n = 0
                        for t, r in enumerate((keyR[:, :, :], blkS[:, :, :].bitcast(f32),
                                               blkD[:, :, :].bitcast(f32))):
                            pe.wait_ge(s_dvec, 10)
                            for g in range(0, EG, 4):
                                if n >= 4:
                                    pe.wait_ge(s_colout, n - 3)
                                for k in range(min(4, EG - g)):
                                    last = nc.tensor.transpose(pT[n % 4][:, k * P:(k + 1) * P], r[:, g + k, :],
                                                               ident[:, :])
                                last.then_inc(s_colps, 1)
                                n += 1
                        pe.wait_ge(s_dvec, 12)
                        nc.tensor.matmul(pW[1][0:1, 0:NB], onesf[:, 0:1], lessN[:, :], start=True,
                                         stop=True).then_inc(s_win, 1)

            c1 = ExitStack()
            with c1:
                kk = [sb(f"kk{i}", [P, WIN], bf16, c1) for i in range(2)]
                oh = [sb(f"oh{i}", [P, NB, WIN], bf16, c1) for i in range(2)]
                ohc = [sb(f"ohc{i}", [P, NB, NWC], bf16, c1) for i in range(2)]
                room = gp[:, :, :, :].rearrange("p b k d -> p (b k d)")
                nv, nr = 2 * NB * WIN, P * WIN
                val = [room[:, i * nv:(i + 1) * nv].rearrange("p (v s j) -> p v s j", v=2, s=NB)
                       for i in range(2)]
                ohr = [room[:, 2 * nv + i * nr:2 * nv + (i + 1) * nr].rearrange("p (r j) -> p r j", r=P)
                       for i in range(2)]
                picked = sb("picked", [P, NWC, WC, NB], bf16, c1)
                rank = [sb(f"rank{i}", [P, WIN], bf16, c1) for i in range(2)]
                cntB = sb("cntB", [P, NB, NB], f32, c1)
                rowS = [sb(f"rowS{i}", [2 * NB, P], u8, c1) for i in range(2)]
                stat = sb("stat", [P, 4], f32, c1)
                pC = ps("pC", [P, NWC, GC], c1)
                pS = [ps(f"pS{i}", [P, GC], c1) for i in range(2)]
                pB = ps("pB", [P, GC], c1)
                pR = ps("pR", [P, GC], c1)
                (q_kk, q_oh, q_ohc, q_vs, q_vd, q_cnt, q_pick, q_rank, q_ohr, q_slot,
                 q_tab, q_bkt, q_bktout, q_row, q_rowout, q_rowdma0, q_rowdma1, q_stat) = (
                    sem("q_" + n) for n in
                    ("kk", "oh", "ohc", "vs", "vd", "cnt", "pick", "rank", "ohr", "slot",
                     "tab", "bkt", "bktout", "row", "rowout", "rowdma0", "rowdma1", "stat"))
                q_rowdma = (q_rowdma0, q_rowdma1)
                with nc.Block() as block:
                    @block.vector
                    def _(dve):
                        def encode(b, p):
                            t0 = dve.value_load(ctl[0:1, ds(b, 1)], min_val=0, max_val=NT - WIN)
                            wait(dve, q_slot, b - 1)
                            nc.vector.tensor_scalar(kk[p][:, :], keyC[:, ds(t0, WIN)], dbase[:, ds(b, 1)], None,
                                                    ALU.subtract).then_inc(q_kk, 1)
                            dve.wait_ge(q_kk, b + 1)
                            nc.vector.tensor_tensor(oh[p][:, :, :], iotaS[:, :, :],
                                                    kk[p][:, :].unsqueeze(1).to_broadcast([P, NB, WIN]),
                                                    ALU.is_equal).then_inc(q_oh, 1)
                            dve.wait_ge(q_oh, b + 1)
                            with nc.allow_low_precision("counts to 9"):
                                nc.vector.tensor_reduce(ohc[p][:, :, :],
                                                        oh[p][:, :, :].rearrange("p s (c j) -> p s c j", j=WC),
                                                        axis=AX.X, op=ALU.add).then_inc(q_ohc, 1)
                            nc.vector.tensor_tensor(val[p][:, 0], oh[p][:, :, :],
                                                    idS[:, ds(t0, WIN)].unsqueeze(1).to_broadcast([P, NB, WIN]),
                                                    ALU.mult).then_inc(q_vs, 1)

                        def place(b, p):
                            dve.wait_ge(q_cnt, b + 1)
                            nc.vector.tensor_tensor(
                                picked[:, :, :, :],
                                pC[:, :, 0:WC * NB].rearrange("p c (j s) -> p c j s", s=NB),
                                oh[p][:, :, :].rearrange("p s (c j) -> p c j s", j=WC),
                                ALU.mult).then_inc(q_pick, 1)
                            dve.wait_ge(q_pick, b + 1)
                            with nc.allow_low_precision("one term isn't zero; a rank over 255 rounds to over 127"):
                                nc.vector.tensor_reduce(rank[p][:, :],
                                                        picked[:, :, :, :].rearrange("p c j s -> p (c j) s"),
                                                        axis=AX.X, op=ALU.add).then_inc(q_rank, 1)
                            dve.wait_ge(q_rank, b + 1)
                            wait(dve, q_slot, b - 1)
                            nc.vector.tensor_tensor(ohr[p][:, :, :], iotaR[:, :, :],
                                                    rank[p][:, :].unsqueeze(1).to_broadcast([P, P, WIN]),
                                                    ALU.is_equal).then_inc(q_ohr, 1)

                        encode(0, 0)
                        encode(1, 1)
                        place(0, 0)

                        def two(b):
                            encode(b + 1, 0)
                            place(b, 1)
                            encode(b + 2, 1)
                            place(b + 1, 0)
                        two(1)
                        with dve.Fori(1, (NB - 3) // 2) as i:
                            two(i * 2 + 1)
                        encode(NB - 1, 0)
                        place(NB - 2, 1)
                        place(NB - 1, 0)
                        dve.wait_ge(q_bktout, NB)
                        nc.vector.tensor_reduce(stat[:, 0:1], cntB[:, :, :], axis=AX.XY,
                                                op=ALU.add).then_inc(q_stat, 1)
                        nc.vector.tensor_reduce(stat[:, 1:2], cntB[:, :, :], axis=AX.XY,
                                                op=ALU.max).then_inc(q_stat, 1)
                        dve.wait_ge(q_stat, 2)
                        nc.vector.tensor_scalar(stat[:, 2:3], stat[:, 1:2], float(P), None,
                                                ALU.is_le).then_inc(q_stat, 1)
                        dve.wait_ge(q_stat, 3)
                        nc.vector.scalar_tensor_tensor(out=ctl[0:1, FLAG:FLAG + 1], in0=stat[0:1, 0:1],
                                                       scalar=float(N_EDGES), in1=stat[0:1, 2:3],
                                                       op0=ALU.is_equal, op1=ALU.mult).then_inc(q_stat, 1)
                        dve.wait_ge(q_stat, 4)

                    @block.gpsimd
                    def _(pool):
                        def values(b, p):
                            t0 = pool.value_load(ctl[0:1, ds(b, 1)], min_val=0, max_val=NT - WIN)
                            pool.wait_ge(q_oh, b + 1)
                            nc.gpsimd.tensor_tensor(val[p][:, 1], oh[p][:, :, :],
                                                    idD[:, ds(t0, WIN)].unsqueeze(1).to_broadcast([P, NB, WIN]),
                                                    ALU.mult).then_inc(q_vd, 1)

                        with pool.Fori(0, NB // 2) as i:
                            values(i * 2, 0)
                            values(i * 2 + 1, 1)
                        values(NB - 1, 0)

                    @block.tensor
                    def _(pe):
                        def count(b, p):
                            pe.wait_ge(q_ohc, b + 1)
                            wait(pe, q_pick, b)
                            o = oh[p][:, :, :].rearrange("p s j -> p j s")
                            for c in range(NWC):
                                full = pC[:, c, 0:WC * NB].rearrange("p (j s) -> p j s", s=NB)
                                nc.tensor.matmul(full, tri[:, :], o[:, c * WC:(c + 1) * WC, :],
                                                 start=True, stop=True)
                                for e in range(c):
                                    nc.tensor.matmul(full, onesb[:, :], ohc[p][:, :, e].unsqueeze(1)
                                                     .to_broadcast([P, WC, NB]), start=False, stop=True,
                                                     skip_group_check=True)
                                for j in range(WC - 1):
                                    last = nc.tensor.matmul(
                                        full[:, j + 1:WC, :], onesb[:, :],
                                        o[:, c * WC + j:c * WC + j + 1, :].to_broadcast([P, WC - 1 - j, NB]),
                                        start=False, stop=True, skip_group_check=True)
                            last.then_inc(q_cnt, 1)
                            wait(pe, q_bktout, b)
                            for e in range(NWC):
                                last = nc.tensor.matmul(pB[:, 0:NB], onesb[:, :], ohc[p][:, :, e],
                                                        start=e == 0, stop=e == NWC - 1)
                            last.then_inc(q_bkt, 1)

                        def fill(b, p):
                            pe.wait_ge(q_ohr, b + 1)
                            pe.wait_ge(q_vs, b + 1)
                            pe.wait_ge(q_vd, b + 1)
                            wait(pe, q_tab, b - 1)
                            for j in range(WIN):
                                last = nc.tensor.matmul(
                                    pS[p][:, 0:2 * NB], ohr[p][:, :, j],
                                    val[p][:, :, :, j].rearrange("p v s -> p (v s)"),
                                    start=j == 0, stop=j == WIN - 1)
                            last.then_inc(q_slot, 1)
                            pe.wait_ge(q_tab, b + 1)
                            wait(pe, q_rowout, b)
                            nc.tensor.matmul(pR[0:2 * NB, 0:P], tab[:, ds(b, 1)].rearrange("p o v s -> p (o v s)"),
                                             identb[:, :], start=True, stop=True).then_inc(q_row, 1)

                        count(0, 0)
                        count(1, 1)
                        fill(0, 0)

                        def two(b):
                            count(b + 1, 0)
                            fill(b, 1)
                            count(b + 2, 1)
                            fill(b + 1, 0)
                        two(1)
                        with pe.Fori(1, (NB - 3) // 2) as i:
                            two(i * 2 + 1)
                        count(NB - 1, 0)
                        fill(NB - 2, 1)
                        fill(NB - 1, 0)

                    @block.scalar
                    def _(act):
                        def leave(b, p):
                            act.wait_ge(q_bkt, b + 1)
                            nc.scalar.activation(cntB[:, ds(b, 1), :], pB[:, 0:NB].unsqueeze(1),
                                                 ACT.Copy).then_inc(q_bktout, 1)
                            act.wait_ge(q_slot, b + 1)
                            nc.scalar.activation(tab[:, ds(b, 1)].rearrange("p o v s -> p (o v s)"),
                                                 pS[p][:, 0:2 * NB], ACT.Copy).then_inc(q_tab, 1)

                        def row(b, p):
                            act.wait_ge(q_row, b + 1)
                            wait(act, q_rowdma[p], (b - p) * 16)
                            nc.scalar.activation(rowS[p][:, :], pR[0:2 * NB, 0:P], ACT.Copy).then_inc(q_rowout, 1)

                        leave(0, 0)
                        row(0, 0)
                        leave(1, 1)
                        row(1, 1)
                        with act.Fori(1, NB // 2) as i:
                            leave(i * 2, 0)
                            row(i * 2, 0)
                            leave(i * 2 + 1, 1)
                            row(i * 2 + 1, 1)
                        leave(NB - 1, 0)
                        row(NB - 1, 0)

                    @block.sync
                    def _(sp):
                        def save(b, p):
                            sp.wait_ge(q_rowout, b + 1)
                            for v in range(2):
                                sp.dma_start(rows[v][:, ds(b, 1), :].rearrange("s o r -> s (o r)"),
                                             rowS[p][v * NB:(v + 1) * NB, :].bitcast(u16)).then_inc(q_rowdma[p], 16)

                        with sp.Fori(0, NB // 2) as i:
                            save(i * 2, 0)
                            save(i * 2 + 1, 1)
                        save(NB - 1, 0)
                        sp.wait_ge(q_rowdma0, 32 * (NB // 2 + 1))
                        sp.wait_ge(q_rowdma1, 32 * (NB // 2))

        def norm_block(name, add_hT):
            cn = ExitStack()
            with cn:
                st = sb(name + "_st", [P, NBP, 6], f32, cn)
                mv = sb(name + "_mv", [P, NBP, 2], f32, cn)
                std = sb(name + "_std", [P, NBP], f32, cn)
                rstd = sb(name + "_rstd", [P, NBP], f32, cn)
                xn = [sb(f"{name}_xn{i}", [P, G, D], f32, cn) for i in range(2)]
                pN = [ps(f"{name}_p{i}", [P, GC], cn) for i in range(2)]
                pH = [ps(f"{name}_h{i}", [P, GC], cn) for i in range(2)]
                n_ht, n_add, n_st, n_mv, n_std, n_rstd, n_xn, n_tr, n_out = (
                    sem(name + "_" + n) for n in ("ht", "add", "st", "mv", "std", "rstd", "xn", "tr", "out"))
                with nc.Block() as block:
                    @block.vector
                    def _(dve):
                        if add_hT:
                            def add(g, p):
                                dve.wait_ge(n_ht, g + 1)
                                nc.vector.tensor_tensor(
                                    xN[:, ds(g * G, G), :], xN[:, ds(g * G, G), :],
                                    pH[p][:, :].rearrange("p (k d) -> p k d", d=D), ALU.add).then_inc(n_add, 1)
                            with dve.Fori(0, NG // 2) as i:
                                add(i * 2, 0)
                                add(i * 2 + 1, 1)
                            add(NG - 1, 0)
                            dve.wait_ge(n_add, NG)
                        with dve.Fori(0, NBP) as b:
                            nc.vector.bn_stats(st[:, ds(b, 1), :].rearrange("p o s -> p (o s)"),
                                               xN[:, ds(b, 1), :].rearrange("p o d -> p (o d)")).then_inc(n_st, 1)
                        dve.wait_ge(n_st, NBP)
                        nc.vector.tensor_tensor(mv[:, :, 0], st[:, :, 1], st[:, :, 4], ALU.add).then_inc(n_mv, 1)
                        nc.vector.tensor_tensor(mv[:, :, 1], st[:, :, 1], st[:, :, 4], ALU.subtract).then_inc(n_mv, 1)
                        nc.vector.tensor_tensor(rstd[:, :], st[:, :, 2], st[:, :, 5], ALU.add).then_inc(n_mv, 1)
                        dve.wait_ge(n_mv, 3)
                        nc.vector.tensor_scalar(mv[:, :, 0], mv[:, :, 0], 0.5, None, ALU.mult).then_inc(n_mv, 1)
                        nc.vector.scalar_tensor_tensor(out=std[:, :], in0=mv[:, :, 1], scalar=0.25,
                                                       in1=mv[:, :, 1], op0=ALU.mult,
                                                       op1=ALU.mult).then_inc(n_mv, 1)
                        dve.wait_ge(n_mv, 5)
                        nc.vector.scalar_tensor_tensor(out=mv[:, :, 1], in0=rstd[:, :], scalar=1.0 / D,
                                                       in1=std[:, :], op0=ALU.mult,
                                                       op1=ALU.add).then_inc(n_mv, 1)
                        dve.wait_ge(n_std, 1)
                        nc.vector.reciprocal(rstd[:, :], std[:, :]).then_inc(n_rstd, 1)
                        dve.wait_ge(n_rstd, 1)

                        def scale(g, p):
                            wait(dve, n_tr, g - 1)
                            for k in range(G):
                                b = g * G + k
                                last = nc.vector.tensor_scalar(
                                    xn[p][:, k, :], xN[:, ds(b, 1), :].rearrange("p o d -> p (o d)"),
                                    mv[:, ds(b, 1), 0:1].rearrange("p o s -> p (o s)"), rstd[:, ds(b, 1)],
                                    ALU.subtract, ALU.mult)
                            last.then_inc(n_xn, 1)
                        scale(0, 0)
                        scale(1, 1)
                        with dve.Fori(1, NG // 2) as i:
                            scale(i * 2, 0)
                            scale(i * 2 + 1, 1)
                        scale(NG - 1, 0)

                    @block.tensor
                    def _(pe):
                        if add_hT:
                            def back(g, p):
                                wait(pe, n_add, g - 1)
                                for k in range(G):
                                    last = nc.tensor.transpose(pH[p][:, k * P:(k + 1) * P], hcopy(k, p),
                                                               ident[:, :])
                                last.then_inc(n_ht, 1)
                            def hcopy(k, p):
                                return xn[p][:, k, :]
                            def back_all(g, p):
                                pe.wait_ge(n_out, g + 1)
                                back(g, p)
                            back_all(0, 0)
                            back_all(1, 1)
                            with pe.Fori(1, NG // 2) as i:
                                back_all(i * 2, 0)
                                back_all(i * 2 + 1, 1)
                            back_all(NG - 1, 0)

                        def turn(g, p):
                            pe.wait_ge(n_xn, g + 1)
                            wait(pe, n_out, g - 1 + (NG if add_hT else 0))
                            for k in range(G):
                                last = nc.tensor.transpose(pN[p][:, k * P:(k + 1) * P], xn[p][:, k, :],
                                                           ident[:, :])
                            last.then_inc(n_tr, 1)
                        turn(0, 0)
                        turn(1, 1)
                        with pe.Fori(1, NG // 2) as i:
                            turn(i * 2, 0)
                            turn(i * 2 + 1, 1)
                        turn(NG - 1, 0)

                    @block.scalar
                    def _(act):
                        if add_hT:
                            def fetch(g, p):
                                wait(act, n_ht, g - 1)
                                nc.scalar.activation(xn[p][:, :, :].rearrange("p k d -> p (k d)"),
                                                     hT[:, ds(g * GC, GC)], ACT.Copy).then_inc(n_out, 1)
                            fetch(0, 0)
                            fetch(1, 1)
                            with act.Fori(1, NG // 2) as i:
                                fetch(i * 2, 0)
                                fetch(i * 2 + 1, 1)
                            fetch(NG - 1, 0)
                        act.wait_ge(n_mv, 6)
                        nc.scalar.activation(std[:, :], mv[:, :, 1], ACT.Sqrt, bias=epsC[:, 0:1]
                                             ).then_inc(n_std, 1)

                        def leave(g, p):
                            act.wait_ge(n_tr, g + 1)
                            nc.scalar.activation(hT[:, ds(g * GC, GC)], pN[p][:, :], ACT.Relu).then_inc(n_out, 1)
                        with act.Fori(0, NG // 2) as i:
                            leave(i * 2, 0)
                            leave(i * 2 + 1, 1)
                        leave(NG - 1, 0)

        norm_block("n1", False)

        ca = ExitStack()
        with ca:
            ohe = [sb(f"ohe{i}", [P, G, 2, P, CH], bf16, ca) for i in range(2)]
            blk = [sb(f"blk{i}", [P, CH, GC], bf16, ca) for i in range(2)]
            cntP = sb("cntP", [P, NG, NB], f32, ca)
            sroot = sb("sroot", [P, GC], f32, ca)
            pA = [ps(f"pA{i}", [P, GC], ca) for i in range(CH)]
            pD = ps("pD", [P, GC], ca)
            (a_oh, a_mm, a_ev, a_deg, a_dcopy, a_dma0, a_dma1, a_cnt, a_root, a_done) = (
                sem("a_" + n) for n in ("oh", "mm", "ev", "deg", "dcopy", "dma0", "dma1", "cnt", "root", "done"))
            a_dma = (a_dma0, a_dma1)
            cntT = gp[:, :, :, :].rearrange("p b k d -> p (b k d)").bitcast(f32)[:, 0:NBP * P]

            def steps(body):
                def pair(m):
                    for t in range(2 * NCH):
                        body(m * 2 + t // NCH, t % NCH, t % 2, G)
                return pair

            with nc.Block() as block:
                @block.vector
                def _(dve):
                    flag = dve.value_load(ctl[0:1, FLAG:FLAG + 1], min_val=0, max_val=1)

                    def hot(g, c, p, nj):
                        n = g * NCH + c
                        wait(dve, a_mm, (n - 1) * CH)
                        for j in range(nj):
                            for v in range(2):
                                last = nc.vector.tensor_tensor(
                                    ohe[p][:, j, v], iotaN[:, :, :],
                                    tab[:, ds(g * G + j, 1), v, c * CH:(c + 1) * CH].to_broadcast([P, P, CH]),
                                    ALU.is_equal)
                        last.then_inc(a_oh, 1)
                        if c == 2 and not (isinstance(g, int) and g == 0):
                            degrees(g - 1)

                    def degrees(g, cols=GC):
                        dve.wait_ge(a_deg, (g + 1) * NCH)
                        nc.vector.tensor_scalar(dinvT[:, ds(g * GC, cols)], pD[:, 0:cols], 1.0, None,
                                                ALU.add).then_inc(a_dcopy, 1)

                    with dve.If(flag > 0):
                        nc.vector.memset(dinvT[:, NB * P:NBP * P], 1.0).then_inc(a_cnt, 1)
                        pair = steps(hot)
                        pair(0)
                        with dve.Fori(1, NG // 2) as m:
                            pair(m)
                        for c in range(NCH):
                            hot(NG - 1, c, c % 2, 1)
                        degrees(NG - 1, P)
                        dve.wait_ge(a_ev, NG * NCH * CH)
                        nc.vector.tensor_reduce(cntN[:, :], cntP[:, :, :].rearrange("p g s -> p s g"), axis=AX.X,
                                                op=ALU.add).then_inc(a_cnt, 1)
                        dve.wait_ge(a_dcopy, NG)
                    with dve.Else():
                        nc.vector.memset(dinvT[:, :], 1.0)
                        nc.vector.memset(cntT, 0.0)
                        dve.drain()
                        with dve.Fori(0, N_EDGES) as e:
                            s = dve.value_load(src1[0:1, ds(e, 1)], min_val=0, max_val=N_NODES - 1)
                            d = dve.value_load(dst1[0:1, ds(e, 1)], min_val=0, max_val=N_NODES - 1)
                            nc.vector.tensor_scalar(dinvT[:, ds(d, 1)], dinvT[:, ds(d, 1)], 1.0, None, ALU.add)
                            nc.vector.tensor_scalar(cntT[:, ds(s, 1)], cntT[:, ds(s, 1)], 1.0, None, ALU.add)
                            dve.drain()
                        with dve.Fori(0, NB) as b:
                            nc.vector.tensor_tensor(sroot[:, 0:P], cntT[:, ds(b * P, P)], ident[:, :], ALU.mult)
                            dve.drain()
                            nc.vector.tensor_reduce(cntN[:, ds(b, 1)], sroot[:, 0:P], axis=AX.X, op=ALU.add)
                            dve.drain()
                    dve.drain().then_inc(a_done, 1)

                    def invert(g):
                        dve.wait_ge(a_root, g + 1)
                        nc.vector.reciprocal(dinvT[:, ds(g * GC, GC)], sroot[:, :]).then_inc(a_dcopy, 1)
                        dve.drain().then_inc(a_done, 1)
                    with dve.Fori(0, NG) as g:
                        invert(g)

                @block.tensor
                def _(pe):
                    flag = pe.value_load(ctl[0:1, FLAG:FLAG + 1], min_val=0, max_val=1)

                    def add_degrees(g, c, p, nj):
                        n = g * NCH + c
                        pe.wait_ge(a_ev, (n + 1) * CH)
                        if c == 0:
                            wait(pe, a_dcopy, g)
                        for i in range(CH):
                            last = nc.tensor.matmul(pD[:, 0:nj * P], onesb[:, :], blk[p][:, i, 0:nj * P],
                                                    start=c == 0 and i == 0, stop=c == NCH - 1 and i == CH - 1)
                        last.then_inc(a_deg, 1)

                    def count(g, c, p, nj):
                        n = g * NCH + c
                        pe.wait_ge(a_oh, n + 1)
                        for i in range(CH):
                            wait(pe, a_ev, (n - 1) * CH + i + 1)
                            for j in range(nj):
                                last = nc.tensor.matmul(pA[i][:, j * P:(j + 1) * P], ohe[p][:, j, 0, :, i],
                                                        ohe[p][:, j, 1, :, i], start=True, stop=True)
                            last.then_inc(a_mm, 1)
                        if not (isinstance(g, int) and g == 0 and c == 0):
                            if c:
                                add_degrees(g, c - 1, 1 - p, nj)
                            else:
                                add_degrees(g - 1, NCH - 1, 1 - p, G)

                    with pe.If(flag > 0):
                        pair = steps(count)
                        pair(0)
                        with pe.Fori(1, NG // 2) as m:
                            pair(m)
                        for c in range(NCH):
                            count(NG - 1, c, c % 2, 1)
                        add_degrees(NG - 1, NCH - 1, (NCH - 1) % 2, 1)

                @block.scalar
                def _(act):
                    flag = act.value_load(ctl[0:1, FLAG:FLAG + 1], min_val=0, max_val=1)

                    def leave(g, c, p, nj):
                        n = g * NCH + c
                        wait(act, a_dma[p], (n - p) * 8)
                        wait(act, a_deg, n - 1)
                        for i in range(CH):
                            act.wait_ge(a_mm, n * CH + i + 1)
                            nc.scalar.activation(blk[p][:, i, 0:nj * P], pA[i][:, 0:nj * P], ACT.Copy,
                                                 accum_out=cntP[:, ds(g, 1), c * CH + i]).then_inc(a_ev, 1)

                    with act.If(flag > 0):
                        pair = steps(leave)
                        pair(0)
                        with act.Fori(1, NG // 2) as m:
                            pair(m)
                        for c in range(NCH):
                            leave(NG - 1, c, c % 2, 1)
                    act.wait_ge(a_done, 1)
                    with act.Fori(0, NG) as g:
                        act.wait_ge(a_done, g + 1)
                        nc.scalar.activation(sroot[:, :], dinvT[:, ds(g * GC, GC)], ACT.Sqrt).then_inc(a_root, 1)

                @block.sync
                def _(sp):
                    flag = sp.value_load(ctl[0:1, FLAG:FLAG + 1], min_val=0, max_val=1)

                    def save(g, c, p, nj):
                        n = g * NCH + c
                        sp.wait_ge(a_ev, (n + 1) * CH)
                        sp.dma_start(adj[ds(g, 1), c, :, :, 0:nj * P].rearrange("o p i n -> (o p) i n"),
                                     blk[p][:, :, 0:nj * P]).then_inc(a_dma[p], 16)

                    with sp.If(flag > 0):
                        pair = steps(save)
                        pair(0)
                        with sp.Fori(1, NG // 2) as m:
                            pair(m)
                        for c in range(NCH):
                            save(NG - 1, c, c % 2, 1)
                        sp.wait_ge(a_dma0, 16 * ((NG * NCH + 1) // 2))
                        sp.wait_ge(a_dma1, 16 * (NG * NCH // 2))

        def table_block(name, W):
            ct = ExitStack()
            with ct:
                hs = [sb(f"{name}_hs{i}", [P, GC], f32, ct) for i in range(2)]
                rem = [sb(f"{name}_rem{i}", [P, GC], f32, ct) for i in range(2)]
                pG = [ps(f"{name}_p{i}", [P, GC], ct) for i in range(2)]
                t_hs, t_mm, t_hi, t_rem, t_mid, t_lo = (
                    sem(name + "_" + n) for n in ("hs", "mm", "hi", "rem", "mid", "lo"))

                def part(g, k):
                    return gp[:, ds(g * G, G), k, :]

                def rows4(t):
                    return t[:, :].rearrange("p (k d) -> p k d", d=D)

                def each(eng, body):
                    body(0, 0)
                    body(1, 1)
                    with eng.Fori(1, NG // 2) as i:
                        body(i * 2, 0)
                        body(i * 2 + 1, 1)
                    body(NG - 1, 0)

                with nc.Block() as block:
                    @block.vector
                    def _(dve):
                        def load(g, p):
                            wait(dve, t_mm, g - 1)
                            nc.vector.tensor_tensor(hs[p][:, :], hT[:, ds(g * GC, GC)],
                                                    dinvT[:, ds(g * GC, GC)], ALU.mult).then_inc(t_hs, 1)

                        def split(g, p):
                            dve.wait_ge(t_hi, g + 1)
                            wait(dve, t_mid, g - 1)
                            wait(dve, t_lo, g - 1)
                            nc.vector.tensor_tensor(rows4(rem[p]), rows4(pG[p]), part(g, 0),
                                                    ALU.subtract).then_inc(t_rem, 1)
                            dve.wait_ge(t_mid, g + 1)
                            nc.vector.tensor_tensor(part(g, 2), rows4(rem[p]), part(g, 1),
                                                    ALU.subtract).then_inc(t_lo, 1)
                        load(0, 0)
                        load(1, 1)
                        split(0, 0)

                        def two(g):
                            load(g + 1, 0)
                            split(g, 1)
                            load(g + 2, 1)
                            split(g + 1, 0)
                        two(1)
                        with dve.Fori(1, (NG - 3) // 2) as i:
                            two(i * 2 + 1)
                        load(NG - 1, 0)
                        split(NG - 2, 1)
                        split(NG - 1, 0)

                    @block.tensor
                    def _(pe):
                        def mul(g, p):
                            pe.wait_ge(t_hs, g + 1)
                            wait(pe, t_rem, g - 1)
                            for k in range(G):
                                last = nc.tensor.matmul(pG[p][:, k * D:(k + 1) * D],
                                                        hs[p][:, k * P:(k + 1) * P], W[:, :],
                                                        start=True, stop=True)
                            last.then_inc(t_mm, 1)
                        each(pe, mul)

                    @block.scalar
                    def _(act):
                        def take(g, p):
                            act.wait_ge(t_mm, g + 1)
                            nc.scalar.activation(part(g, 0), rows4(pG[p]), ACT.Copy).then_inc(t_hi, 1)
                            act.wait_ge(t_rem, g + 1)
                            nc.scalar.activation(part(g, 1), rows4(rem[p]), ACT.Copy).then_inc(t_mid, 1)
                        each(act, take)

        def gcn_block(name, bias):
            cg = ExitStack()
            with cg:
                ring = sb(name + "_ring", [P, NCH, CH, GC], bf16, cg)
                sc = [sb(f"{name}_sc{i}", [P, GC], f32, cg) for i in range(2)]
                pO = [ps(f"{name}_p{i}", [P, GC], cg) for i in range(2)]
                gT = ring[:, :, :, :].rearrange("p c i n -> p (c i n)").bitcast(f32)[:, 0:NBP * P]
                g_in = [sem(f"{name}_in{c}") for c in range(NCH)]
                g_chunk, g_mm, g_sc, g_out, g_self = (
                    sem(name + "_" + n) for n in ("chunk", "mm", "sc", "out", "self"))

                def each(eng, body):
                    body(0, 0, G)
                    body(1, 1, G)
                    with eng.Fori(1, NG // 2) as i:
                        body(i * 2, 0, G)
                        body(i * 2 + 1, 1, G)
                    body(NG - 1, 0, 1)

                with nc.Block() as block:
                    @block.sync
                    def _(sp):
                        flag = sp.value_load(ctl[0:1, FLAG:FLAG + 1], min_val=0, max_val=1)

                        def load(g, p, nj):
                            for c in range(NCH):
                                wait(sp, g_chunk, (g - 1) * NCH + c + 1)
                                sp.dma_start(ring[:, c, :, 0:nj * P],
                                             adj[ds(g, 1), c, :, :, 0:nj * P].rearrange("o p i n -> (o p) i n")
                                             ).then_inc(g_in[c], 16)
                        with sp.If(flag > 0):
                            each(sp, load)

                    @block.tensor
                    def _(pe):
                        flag = pe.value_load(ctl[0:1, FLAG:FLAG + 1], min_val=0, max_val=1)

                        def own(g, p, nj, start):
                            for k in range(nj):
                                for part in range(3):
                                    last = nc.tensor.matmul(
                                        pO[p][:, k * P:(k + 1) * P],
                                        gp[:, ds(g * G + k, 1), part, :].rearrange("p o d -> p (o d)"),
                                        identb[:, :], start=start and part == 0, stop=part == 2,
                                        skip_group_check=True)
                            return last

                        def add(g, p, nj):
                            wait(pe, g_sc, g - 1)
                            for c in range(NCH):
                                pe.wait_ge(g_in[c], g * 16 + 16)
                                for i in range(CH):
                                    for part in range(3):
                                        last = nc.tensor.matmul(
                                            pO[p][:, 0:nj * P], gp[:, c * CH + i, part, :],
                                            ring[:, c, i, 0:nj * P], start=c == 0 and i == 0 and part == 0,
                                            stop=c == NCH - 1 and i == CH - 1 and part == 2,
                                            skip_group_check=True)
                                last.then_inc(g_chunk, 1)
                            own(g, p, nj, False).then_inc(g_mm, 1)

                        with pe.If(flag > 0):
                            each(pe, add)
                        with pe.Else():
                            with pe.Fori(0, NG) as g:
                                pe.wait_ge(g_sc, g + 1)
                                own(g, 0, G, True).then_inc(g_self, 1)

                    @block.vector
                    def _(dve):
                        flag = dve.value_load(ctl[0:1, FLAG:FLAG + 1], min_val=0, max_val=1)

                        def scale(g, p, nj):
                            dve.wait_ge(g_mm, g + 1)
                            wait(dve, g_out, g - 1)
                            nc.vector.tensor_tensor(sc[p][:, 0:nj * P], pO[p][:, 0:nj * P],
                                                    dinvT[:, ds(g * GC, nj * P)], ALU.mult).then_inc(g_sc, 1)
                        with dve.If(flag > 0):
                            each(dve, scale)
                        with dve.Else():
                            nc.vector.memset(sc[0][:, :], 0.0).then_inc(g_sc, 1)
                            with dve.Fori(0, NG) as g:
                                dve.wait_ge(g_self, g + 1)
                                nc.vector.tensor_copy(gT[:, ds(g * GC, GC)], pO[0][:, :])
                                nc.vector.tensor_copy(hT[:, ds(g * GC, GC)], pO[0][:, :])
                                dve.drain().then_inc(g_sc, 1)
                            with dve.Fori(0, N_EDGES) as e:
                                s = dve.value_load(src1[0:1, ds(e, 1)], min_val=0, max_val=N_NODES - 1)
                                d = dve.value_load(dst1[0:1, ds(e, 1)], min_val=0, max_val=N_NODES - 1)
                                nc.vector.tensor_tensor(hT[:, ds(d, 1)], hT[:, ds(d, 1)], gT[:, ds(s, 1)],
                                                        ALU.add)
                                dve.drain()
                            with dve.Fori(0, NG) as g:
                                nc.vector.tensor_tensor(hT[:, ds(g * GC, GC)], hT[:, ds(g * GC, GC)],
                                                        dinvT[:, ds(g * GC, GC)], ALU.mult)
                                dve.drain()
                                nc.vector.tensor_scalar(hT[:, ds(g * GC, GC)], hT[:, ds(g * GC, GC)],
                                                        bias[:, 0:1], 0.0, ALU.add, ALU.max)
                                dve.drain()

                    @block.scalar
                    def _(act):
                        flag = act.value_load(ctl[0:1, FLAG:FLAG + 1], min_val=0, max_val=1)

                        def leave(g, p, nj):
                            act.wait_ge(g_sc, g + 1)
                            nc.scalar.activation(hT[:, ds(g * GC, nj * P)], sc[p][:, 0:nj * P], ACT.Relu,
                                                 bias=bias[:, 0:1]).then_inc(g_out, 1)
                        with act.If(flag > 0):
                            each(act, leave)

        table_block("t1", W1s)
        gcn_block("g1", b1c)
        table_block("t2", W2s)
        gcn_block("g2", b2c)
        norm_block("n2", True)

        ch = ExitStack()
        with ch:
            cnt1 = sb("cnt1", [P, NBP], f32, ch)
            has = sb("has", [P, NBP], f32, ch)
            rcnt = sb("rcnt", [P, NBP], f32, ch)
            ci = ExitStack()
            with ci:
                hs, hv, hw, zt = ([sb(f"h_{n}{i}", [P, GC], f32, ci) for i in range(2)]
                                  for n in ("hs", "hv", "hw", "zt"))
                pF = [ps(f"h_pf{i}", [P, GC], ci) for i in range(2)]
                pG, pZ = ps("h_pg", [P, GC], ci), ps("h_pz", [P, GC], ci)
                pY = [ps(f"h_py{i}", [P, G, 2, D], ci) for i in range(2)]
                (h_c, h_hs, h_mm, h_y, h_v, h_hi, h_rem, h_mid, h_lo, h_t, h_t2, h_z, h_zz, h_yy, h_w) = (
                    sem("h_" + n) for n in ("c", "hs", "mm", "y", "v", "hi", "rem", "mid", "lo", "t", "t2", "z",
                                            "zz", "yy", "w"))

                def four(t):
                    return t.rearrange("p (k d) -> p k d", d=D)

                with nc.Block() as block:
                    @block.scalar
                    def _(act):
                        def copy(g, p):
                            wait(act, h_mm, g - 1)
                            nc.scalar.activation(hs[p][:, :], hT[:, ds(g * GC, GC)], ACT.Copy).then_inc(h_hs, 1)

                        def bias(g, p):
                            act.wait_ge(h_mm, g + 1)
                            wait(act, h_y, g - 1)
                            nc.scalar.activation(hw[p][:, :], pF[p][:, :], ACT.Identity,
                                                 bias=bnc[:, 0:1]).then_inc(h_t, 1)
                            act.wait_ge(h_v, g + 1)
                            nc.scalar.activation(gp[:, ds(g * G, G), 0, :], four(hv[p][:, :]),
                                                 ACT.Copy).then_inc(h_hi, 1)
                            act.wait_ge(h_t, g + 1)
                            nc.scalar.activation(hT.rearrange("p (n c) -> p n c", c=P)[:, ds(g * G, G), :],
                                                 four(hw[p][:, :]), ACT.Copy).then_inc(h_t2, 1)
                            act.wait_ge(h_rem, g + 1)
                            nc.scalar.activation(gp[:, ds(g * G, G), 1, :], four(hv[p][:, :]),
                                                 ACT.Copy).then_inc(h_mid, 1)
                        copy(0, 0)
                        copy(1, 1)
                        bias(0, 0)

                        def two(g):
                            copy(g + 1, 0)
                            bias(g, 1)
                            copy(g + 2, 1)
                            bias(g + 1, 0)
                        two(1)
                        with act.Fori(1, (NG - 3) // 2) as i:
                            two(i * 2 + 1)
                        copy(NG - 1, 0)
                        bias(NG - 2, 1)
                        bias(NG - 1, 0)

                    @block.tensor
                    def _(pe):
                        def mul(g, p):
                            pe.wait_ge(h_hs, g + 1)
                            wait(pe, h_t, g - 1)
                            wait(pe, h_v, g)
                            wait(pe, h_z, g)
                            nc.tensor.matmul(pF[p][:, :], WnT[:, :], hs[p][:, :], start=True, stop=True)
                            for k in range(G):
                                for o, W in ((pG, WnT), (pZ, Wl1T)):
                                    last = nc.tensor.matmul(o[:, k * D:(k + 1) * D],
                                                            hs[p][:, k * P:(k + 1) * P], W[:, :],
                                                            start=True, stop=True)
                            last.then_inc(h_mm, 1)

                        def through(g, p):
                            pe.wait_ge(h_t, g + 1)
                            wait(pe, h_w, 2 * g - 2)
                            for k in range(G):
                                last = nc.tensor.matmul(pY[p][:, k, :, :], hw[p][:, k * P:(k + 1) * P],
                                                        Wout[:, 0:2, :], start=True, stop=True)
                            last.then_inc(h_y, 1)
                        mul(0, 0)
                        mul(1, 1)
                        through(0, 0)

                        def two(g):
                            mul(g + 1, 0)
                            through(g, 1)
                            mul(g + 2, 1)
                            through(g + 1, 0)
                        two(1)
                        with pe.Fori(1, (NG - 3) // 2) as i:
                            two(i * 2 + 1)
                        mul(NG - 1, 0)
                        through(NG - 2, 1)
                        through(NG - 1, 0)

                    @block.vector
                    def _(dve):
                        nc.vector.memset(cnt1[:, :], 0.0).then_inc(h_c, 1)
                        dve.wait_ge(h_c, 1)
                        nc.vector.tensor_copy(cnt1[:, 0:NB], cntN[:, :]).then_inc(h_c, 1)
                        dve.wait_ge(h_c, 2)
                        nc.vector.tensor_scalar(has[:, :], cnt1[:, :], 1.0, None, ALU.min).then_inc(h_c, 1)
                        dve.wait_ge(h_c, 3)
                        nc.vector.tensor_scalar(cnt1[:, :], cnt1[:, :], 1.0, None, ALU.max).then_inc(h_c, 1)
                        dve.wait_ge(h_c, 4)
                        nc.vector.reciprocal(rcnt[:, :], cnt1[:, :]).then_inc(h_c, 1)
                        dve.wait_ge(h_c, 5)

                        def add(g, p, added):
                            nc.vector.tensor_tensor(xN[:, ds(g * G, G), :], xN[:, ds(g * G, G), :],
                                                    four(zt[p][:, :]), ALU.add).then_inc(added, 1)

                        def first(g, p):
                            dve.wait_ge(h_mm, g + 1)
                            wait(dve, h_mid, g - 1)
                            wait(dve, h_lo, g - 1)
                            nc.vector.tensor_tensor(four(hv[p][:, :]), four(pG[:, :]),
                                                    bnr[:, :].unsqueeze(1).to_broadcast([P, G, D]),
                                                    ALU.add).then_inc(h_v, 1)
                            wait(dve, h_yy, 2 * g - 2)
                            nc.vector.tensor_tensor(four(zt[p][:, :]), four(pZ[:, :]),
                                                    blr[:, :].unsqueeze(1).to_broadcast([P, G, D]),
                                                    ALU.add).then_inc(h_z, 1)
                            dve.wait_ge(h_z, g + 1)
                            add(g, p, h_zz)

                        def second(g, p):
                            dve.wait_ge(h_hi, g + 1)
                            dve.wait_ge(h_v, g + 1)
                            nc.vector.tensor_tensor(four(hv[p][:, :]), four(hv[p][:, :]),
                                                    gp[:, ds(g * G, G), 0, :], ALU.subtract).then_inc(h_rem, 1)
                            dve.wait_ge(h_y, g + 1)
                            for k, f in enumerate((rcnt, has)):
                                if k == 0:
                                    dve.wait_ge(h_zz, g + 1)
                                else:
                                    dve.wait_ge(h_yy, 2 * g + 1)
                                nc.vector.tensor_tensor(four(zt[p][:, :]), pY[p][:, :, k, :],
                                                        f[:, ds(g * G, G)].unsqueeze(2).to_broadcast([P, G, D]),
                                                        ALU.mult).then_inc(h_w, 1)
                                dve.wait_ge(h_w, 2 * g + k + 1)
                                add(g, p, h_yy)
                            dve.wait_ge(h_mid, g + 1)
                            dve.wait_ge(h_rem, g + 1)
                            nc.vector.tensor_tensor(gp[:, ds(g * G, G), 2, :], four(hv[p][:, :]),
                                                    gp[:, ds(g * G, G), 1, :], ALU.subtract).then_inc(h_lo, 1)
                        first(0, 0)

                        def two(g):
                            first(g + 1, 1)
                            second(g, 0)
                            first(g + 2, 0)
                            second(g + 1, 1)
                        two(0)
                        with dve.Fori(1, NG // 2) as i:
                            two(i * 2)
                        second(NG - 1, 0)

            posT = dinvT
            cr = ExitStack()
            with cr:
                COLS = CH * P
                sumT = sb("sumT", [P, NBP * P], f32, cr)
                idr = [sumT[:, :].bitcast(u8)[:, c * 2 * COLS:(c + 1) * 2 * COLS] for c in range(NCH)]
                agg0 = NCH * 2 * COLS // 4
                agg = sumT[:, agg0:agg0 + 2 * D].rearrange("p (v d) -> p v d", v=2)
                dif = sb("dif", [P, 1], f32, cr)
                pick = [sb(f"pick{i}", [P, 2 * COLS], bf16, cr) for i in range(2)]
                put = [sb(f"put{i}", [P, P, CH], f32r, cr) for i in range(2)]
                msg = [sb(f"msg{i}", [P, CH, 2, 2, D], f32r, cr) for i in range(2)]
                nega = [sb(f"nega{i}", [P, 3, D], bf16, cr) for i in range(2)]
                pD = [ps(f"pD{i}", [P, 2 * G, P], cr) for i in range(2)]
                pAg = ps("pAg", [P, 2, D], cr)
                pTr = ps("pTr", [P, 2, P], cr)
                e_in = [sem(f"e_in{c}") for c in range(NCH)]
                e_pick, e_put, e_neg, e_gath, e_hi, e_low, e_sum, e_agg, e_tr, e_out = (
                    sem("e_" + n) for n in ("pick", "put", "neg", "gath", "hi", "low", "sum", "agg", "tr", "out"))

                def each(eng, body):
                    body(0, 0, True, False)
                    body(1, 1, False, False)
                    with eng.Fori(1, NB // 2) as i:
                        body(i * 2, 0, False, False)
                        body(i * 2 + 1, 1, False, False)
                    body(NB - 1, 0, False, True)

                with nc.Block() as block:
                    @block.sync
                    def _(sp):
                        flag = sp.value_load(ctl[0:1, FLAG:FLAG + 1], min_val=0, max_val=1)

                        def load(a):
                            for c in range(NCH):
                                wait(sp, e_pick, (a - 1) * NCH + c + 1)
                                for v in range(2):
                                    sp.dma_start(idr[c][:, v * COLS:(v + 1) * COLS].bitcast(u16),
                                                 rows[v][ds(a, 1), c * CH:(c + 1) * CH, :]
                                                 .rearrange("o b r -> (o b r)").partition_broadcast(P)
                                                 ).then_inc(e_in[c], 16)
                        with sp.If(flag > 0):
                            load(0)
                            with sp.Fori(1, NB) as a:
                                load(a)

                    @block.vector
                    def _(dve):
                        flag = dve.value_load(ctl[0:1, FLAG:FLAG + 1], min_val=0, max_val=1)

                        def one_hot_nodes(a, c, q):
                            p = (q + c) % 2
                            dve.wait_ge(e_in[c], a * 32 + 32)
                            wait(dve, e_gath, a * NCH + c - 1)
                            nc.vector.tensor_scalar(pick[p][:, :], idr[c], idCol[:, 0:1], None,
                                                    ALU.is_equal).then_inc(e_pick, 1)

                        def one_hot_slots(a, c, q):
                            p = (q + c) % 2
                            wait(dve, e_sum, a * NCH + c - 1)
                            nc.vector.tensor_tensor(
                                put[p][:, :, :], iotaN[:, :, :],
                                tab[:, c * CH:(c + 1) * CH, 0, ds(a, 1)].rearrange("p b o -> p (b o)")
                                .unsqueeze(1).to_broadcast([P, P, CH]), ALU.is_equal).then_inc(e_put, 1)

                        def low(a, c, q):
                            p = (q + c) % 2
                            dve.wait_ge(e_hi, (a * NCH + c) * 2 + 1)
                            nc.vector.tensor_tensor(msg[p][:, :, 1, 1, :], pD[p][:, 0:CH, :],
                                                    msg[p][:, :, 0, 1, :].bitcast(f32),
                                                    ALU.subtract).then_inc(e_low, 1)
                            dve.wait_ge(e_hi, (a * NCH + c) * 2 + 2)
                            nc.vector.scalar_tensor_tensor(
                                out=msg[p][:, :, 1, 0, :], in0=pD[p][:, 0:CH, :], scalar=0.0,
                                in1=msg[p][:, :, 0, 0, :].bitcast(f32), op0=ALU.max,
                                op1=ALU.subtract).then_inc(e_low, 1)

                        def block_of(a, q, first, last):
                            def ahead(make, c):
                                if c < NCH:
                                    make(a, c, q)
                                elif not last:
                                    make(a + 1, c - NCH, 1 - q)
                            if first:
                                one_hot_nodes(0, 0, 0)
                                one_hot_nodes(0, 1, 0)
                                one_hot_slots(0, 0, 0)
                            for c in range(NCH):
                                low(a, c, q)
                                ahead(one_hot_nodes, c + 2)
                                ahead(one_hot_slots, c + 1)
                        with dve.If(flag > 0):
                            each(dve, block_of)
                        with dve.Else():
                            nc.vector.memset(posT[:, :], 0.0)
                            nc.vector.memset(sumT[:, :], 0.0)
                            dve.drain()
                            with dve.Fori(0, N_EDGES) as e:
                                s = dve.value_load(src1[0:1, ds(e, 1)], min_val=0, max_val=N_NODES - 1)
                                d = dve.value_load(dst1[0:1, ds(e, 1)], min_val=0, max_val=N_NODES - 1)
                                nc.vector.tensor_tensor(dif[:, :], hT[:, ds(d, 1)], hT[:, ds(s, 1)],
                                                        ALU.subtract)
                                dve.drain()
                                nc.vector.tensor_tensor(sumT[:, ds(s, 1)], sumT[:, ds(s, 1)], dif[:, :], ALU.add)
                                nc.vector.scalar_tensor_tensor(out=posT[:, ds(s, 1)], in0=dif[:, :], scalar=0.0,
                                                               in1=posT[:, ds(s, 1)], op0=ALU.max,
                                                               op1=ALU.add)
                                dve.drain()
                            nc.vector.tensor_copy(hT[:, :], sumT[:, :])

                    @block.tensor
                    def _(pe):
                        flag = pe.value_load(ctl[0:1, FLAG:FLAG + 1], min_val=0, max_val=1)

                        def gather(a, c, q):
                            p = (q + c) % 2
                            pe.wait_ge(e_pick, a * NCH + c + 1)
                            wait(pe, e_low, (a * NCH + c - 1) * 2)
                            if c == 0:
                                pe.wait_ge(e_neg, a + 1)
                            for k in range(CH):
                                for t in range(3):
                                    nc.tensor.matmul(pD[p][:, k, :], pick[p][:, k * P:(k + 1) * P],
                                                     nega[q][:, t, :], start=t == 0, stop=False)
                                for t in range(3):
                                    last = nc.tensor.matmul(pD[p][:, k, :],
                                                            pick[p][:, COLS + k * P:COLS + (k + 1) * P],
                                                            gp[:, c * CH + k, t, :], start=False, stop=t == 2)
                            last.then_inc(e_gath, 1)

                        def total(a, c, q):
                            p = (q + c) % 2
                            pe.wait_ge(e_put, a * NCH + c + 1)
                            pe.wait_ge(e_hi, (a * NCH + c + 1) * 2)
                            pe.wait_ge(e_low, (a * NCH + c + 1) * 2)
                            if c == 0:
                                wait(pe, e_agg, a)
                            for k in range(CH):
                                for t in range(2):
                                    last = nc.tensor.matmul(
                                        pAg[:, :, :], put[p][:, :, k], msg[p][:, k, t, :, :],
                                        start=c == 0 and k == 0 and t == 0,
                                        stop=c == NCH - 1 and k == CH - 1 and t == 1)
                            last.then_inc(e_sum, 1)

                        def turn(a):
                            pe.wait_ge(e_agg, a + 1)
                            wait(pe, e_out, a * 2)
                            for v in range(2):
                                last = nc.tensor.transpose(pTr[:, v, :], agg[:, v, :], ident[:, :])
                            last.then_inc(e_tr, 1)

                        def block_of(a, q, first, last):
                            if first:
                                gather(0, 0, 0)
                            for c in range(NCH):
                                if c + 1 < NCH:
                                    gather(a, c + 1, q)
                                elif not last:
                                    gather(a + 1, 0, 1 - q)
                                total(a, c, q)
                                if c == 1 and not first:
                                    turn(a - 1)
                            if last:
                                turn(a)
                        with pe.If(flag > 0):
                            each(pe, block_of)

                    @block.scalar
                    def _(act):
                        flag = act.value_load(ctl[0:1, FLAG:FLAG + 1], min_val=0, max_val=1)

                        def negate(a, q):
                            wait(act, e_sum, (a - 1) * NCH)
                            nc.scalar.activation(nega[q][:, :, :], gp[:, ds(a, 1), :, :].rearrange(
                                "p o t d -> p (o t) d"), ACT.Copy, scale=-1.0).then_inc(e_neg, 1)

                        def first_parts(a, c, q):
                            p = (q + c) % 2
                            act.wait_ge(e_gath, a * NCH + c + 1)
                            wait(act, e_sum, a * NCH + c - 1)
                            nc.scalar.activation(msg[p][:, :, 0, 1, :], pD[p][:, 0:CH, :],
                                                 ACT.Copy).then_inc(e_hi, 1)
                            act.wait_ge(e_hi, (a * NCH + c) * 2 + 1)
                            nc.scalar.activation(msg[p][:, :, 0, 0, :], msg[p][:, :, 0, 1, :].bitcast(f32),
                                                 ACT.Relu).then_inc(e_hi, 1)

                        def sums(a):
                            act.wait_ge(e_sum, (a + 1) * NCH)
                            wait(act, e_tr, a)
                            nc.scalar.activation(agg[:, :, :], pAg[:, :, :], ACT.Copy).then_inc(e_agg, 1)

                        def save(a):
                            act.wait_ge(e_tr, a + 1)
                            nc.scalar.activation(posT[:, ds(a * P, P)], pTr[:, 0, :], ACT.Copy).then_inc(e_out, 1)
                            nc.scalar.activation(hT[:, ds(a * P, P)], pTr[:, 1, :], ACT.Copy).then_inc(e_out, 1)

                        def block_of(a, q, first, last):
                            if first:
                                negate(0, 0)
                            for c in range(NCH):
                                first_parts(a, c, q)
                                if c == 0 and not first:
                                    sums(a - 1)
                                if c == 2 and not first:
                                    save(a - 1)
                                if c == 3 and not last:
                                    negate(a + 1, 1 - q)
                            if last:
                                sums(a)
                                save(a)
                        with act.If(flag > 0):
                            each(act, block_of)

            hb = [sb(f"f_hb{i}", [P, 2, P], f32, ch) for i in range(2)]
            u2, u3 = ([sb(f"f_{n}{i}", [P, D], f32, ch) for i in range(2)] for n in ("v", "w"))
            cb = [sb(f"f_cb{i}", [P, D], f32, ch) for i in range(2)]
            pO = [ps(f"f_p{i}", [P, GC], ch) for i in range(2)]
            f_in, f_mm, f_cb, f_u2, f_u3, f_dma0, f_dma1 = (
                sem("f_" + n) for n in ("in", "mm", "cb", "u2", "u3", "dma0", "dma1"))
            f_dma = (f_dma0, f_dma1)

            def each(eng, body):
                body(0, 0)
                body(1, 1)
                with eng.Fori(1, NB // 2) as i:
                    body(i * 2, 0)
                    body(i * 2 + 1, 1)
                body(NB - 1, 0)

            with nc.Block() as block:
                @block.scalar
                def _(act):
                    def load(b, p):
                        wait(act, f_mm, b - 1)
                        for k, t in enumerate((posT, hT)):
                            last = nc.scalar.activation(hb[p][:, k, :], t[:, ds(b * P, P)], ACT.Copy)
                        last.then_inc(f_in, 1)
                    each(act, load)

                @block.tensor
                def _(pe):
                    def mul(b, p):
                        pe.wait_ge(f_in, b + 1)
                        wait(pe, f_u2, b - 1)
                        nc.tensor.matmul(pO[p][:, 0:D], hb[p][:, 0, :], W22[:, :], start=True, stop=False)
                        nc.tensor.matmul(pO[p][:, 0:D], hb[p][:, 1, :], WD[:, :], start=False,
                                         stop=True).then_inc(f_mm, 1)
                    each(pe, mul)

                @block.vector
                def _(dve):
                    def leave(b, p):
                        dve.wait_ge(f_mm, b + 1)
                        wait(dve, f_u3, b - 1)
                        nc.vector.scalar_tensor_tensor(out=u2[p][:, :], in0=ber[:, :], scalar=cntN[:, ds(b, 1)],
                                                       in1=pO[p][:, 0:D], op0=ALU.mult,
                                                       op1=ALU.add).then_inc(f_u2, 1)
                        dve.wait_ge(f_u2, b + 1)
                        wait(dve, f_dma[p], (b - p) * 8)
                        nc.vector.scalar_tensor_tensor(out=u3[p][:, :], in0=u2[p][:, :], scalar=rcnt[:, ds(b, 1)],
                                                       in1=xN[:, ds(b, 1), :].rearrange("p o d -> p (o d)"),
                                                       op0=ALU.mult, op1=ALU.add).then_inc(f_u3, 1)
                    each(dve, leave)

                @block.sync
                def _(sp):
                    def save(b, p, n=P):
                        sp.wait_ge(f_u3, b + 1)
                        sp.dma_start(out[ds(b * P, n), :], u3[p][0:n, :]).then_inc(f_dma[p], 16)
                    with sp.Fori(0, NB // 2) as i:
                        save(i * 2, 0)
                        save(i * 2 + 1, 1)
                    save(NB - 1, 0, LAST)
                    sp.wait_ge(f_dma0, 16 * (NB // 2 + 1))
                    sp.wait_ge(f_dma1, 16 * (NB // 2))


_NAMES = ("x", "src", "dst", "L0_gnn_W1", "L0_gnn_b1", "L0_gnn_W2", "L0_gnn_b2", "L1_gnn_W_neigh",
          "L1_gnn_b_neigh", "L1_gnn_W_edge", "L1_gnn_b_edge", "L1_gnn_W_lin", "L1_gnn_b_lin")


def kernel(**inputs):
    import numpy as np
    import concourse.bacc as bacc
    from concourse.bass_utils import run_bass_kernel_spmd

    nc = bacc.Bacc("TRN2", target_bir_lowering=False, num_devices=1)
    arrays, args = {}, []
    for name in _NAMES:
        a = np.ascontiguousarray(inputs[name])
        arrays["in_" + name] = a
        args.append(nc.dram_tensor("in_" + name, a.shape, mybir.dt.from_np(a.dtype), kind="ExternalInput").ap())
    out = nc.dram_tensor("out", (N_NODES, D), mybir.dt.float32, kind="ExternalOutput").ap()
    gnn(nc, *args, out)
    got = run_bass_kernel_spmd(nc, [arrays], core_ids=[0])
    return got.results[0]["out"]
```

```python
from contextlib import ExitStack

import concourse.bass as bass
from concourse import mybir

P = 128
N_NODES, N_EDGES, D = 6250, 200000, 128
NB = -(-N_NODES // P)
LAST = N_NODES - (NB - 1) * P
G = 4
NG = -(-NB // G)
NBP = NG * G
GC = G * P
CH = 7
NCH = NB // CH
WIN, WC = 36, 9
NWC = WIN // WC
FULL_G = N_EDGES // (P * P)
TAIL = N_EDGES - FULL_G * P * P
TAIL_ROWS, TAIL_EDGES = TAIL // P, TAIL % P
EG = FULL_G + 1
NT = EG * P
PAD_DST = 200 * P
EPS = 1e-5


def gnn(nc, x, src, dst, W1, b1, W2, b2, Wn, bn, We, be, Wl, bl, out):
    f32, bf16, i32, u8 = mybir.dt.float32, mybir.dt.bfloat16, mybir.dt.int32, mybir.dt.uint8
    u16 = mybir.dt.uint16
    f32r = mybir.dt.float32r
    ALU = mybir.AluOpType
    ACT = mybir.ActivationFunctionType
    AX = mybir.AxisListType
    ds = bass.ds

    adj = nc.dram_tensor("adj", (NG, NCH, P, CH, GC), bf16, kind="Internal").ap()
    rows = nc.dram_tensor("slot_rows", (2, NB, NB, P // 2), u16, kind="Internal").ap()

    src1 = src.rearrange("(o e) -> o e", o=1)
    dst1 = dst.rearrange("(o e) -> o e", o=1)

    ctx = ExitStack()
    with ctx:
        def sb(name, shape, dt, c=ctx):
            return c.enter_context(nc.sbuf_tensor(name, shape, dt))

        def ps(name, shape, c):
            return c.enter_context(nc.psum_tensor(name, shape, f32))

        def sem(name):
            return ctx.enter_context(nc.semaphore(name))

        def wait(eng, s, value):
            if not isinstance(value, int) or value > 0:
                eng.wait_ge(s, value)

        xN = sb("xN", [P, NBP, D], f32)
        hT = sb("hT", [P, NBP * P], f32)
        dinvT = sb("dinvT", [P, NBP * P], f32)
        tab = sb("tab", [P, NB, 2, NB], bf16)
        cntN = sb("cntN", [P, NB], f32)
        ident = sb("ident", [P, P], f32)
        identb = sb("identb", [P, P], bf16)
        onesf = sb("onesf", [P, P], f32)
        iotaN = sb("iotaN", [P, P, CH], bf16)
        idCol = sb("idCol", [P, 1], f32)
        idColF = sb("idColF", [P, 1], i32)
        WnT, Wl1T = (sb(n, [P, D], f32) for n in ("WnT", "Wl1T"))
        Wout = sb("Wout", [P, 4, D], f32)
        Wl2T, W12, W22, WD = (Wout[:, i, :] for i in range(4))
        b1c, b2c, bec, bnc = (sb(n, [P, 1], f32) for n in ("b1c", "b2c", "bec", "bnc"))
        bnr, blr, ber = (sb(n, [P, D], f32) for n in ("bnr", "blr", "ber"))
        epsC = sb("epsC", [P, 1], f32)
        ctl = sb("ctl", [1, 64], i32)
        FLAG = 60

        W1s, W2s = sb("W1s", [P, D], f32), sb("W2s", [P, D], f32)
        onesb = sb("onesb", [P, P], bf16)
        tri = sb("tri", [P, P], bf16)

        cw = ExitStack()
        work = sb("work", [P, NBP * 3 * D], bf16, cw)

        c0 = ExitStack()
        with c0:
            keyC = sb("keyC", [P, NT], f32, c0)
            idS = sb("idS", [P, NT], bf16, c0)
            idD = sb("idD", [P, NT], bf16, c0)
            iotaS = sb("iotaS", [P, NB, WIN], bf16, c0)
            iotaR = sb("iotaR", [P, P, WIN], bf16, c0)
            dbase = sb("dbase", [P, NB], f32, c0)
            c1 = ExitStack()
            with c1:
                eD = sb("eD", [P, EG, P], i32, c1)
                eS = sb("eS", [P, EG, P], i32, c1)
                blkD = sb("blkD", [P, EG, P], i32, c1)
                blkS = sb("blkS", [P, EG, P], i32, c1)
                keyR = sb("keyR", [P, EG, P], f32, c1)
                tmax = sb("tmax", [P, EG], f32, c1)
                less = sb("less", [P, NB, EG], f32, c1)
                lessN = sb("lessN", [P, NB], f32, c1)
                dbN = sb("dbN", [P, NB], f32, c1)
                wld = sb("wld", [P, 5, D], f32, c1)
                pT = [ps(f"pT{i}", [P, GC], c1) for i in range(4)]
                pW = [ps(f"pW{i}", [P, GC], c1) for i in range(3)]
                s_pre, s_edge, s_w, s_x, s_b = (sem(n) for n in ("s_pre", "s_edge", "s_w", "s_x", "s_b"))
                s_const, s_dvec, s_col, s_colps, s_colout = (
                    sem(n) for n in ("s_const", "s_dvec", "s_col", "s_colps", "s_colout"))
                s_wt, s_wtout, s_win, s_w2, s_w2out = (
                    sem(n) for n in ("s_wt", "s_wtout", "s_win", "s_w2", "s_w2out"))
                s_pool = sem("s_pool")
                with nc.Block() as block:
                    @block.sync
                    def _(sp):
                        sp.wait_ge(s_pre, 2)
                        for e, a in ((eD, dst), (eS, src)):
                            sp.dma_start(e[:, 0:FULL_G, :], a[0:FULL_G * P * P].rearrange(
                                "(g p e) -> p g e", p=P, e=P)).then_inc(s_edge, 16)
                            sp.dma_start(e[0:TAIL_ROWS, FULL_G, :], a[FULL_G * P * P:N_EDGES - TAIL_EDGES]
                                         .rearrange("(p e) -> p e", e=P)).then_inc(s_edge, 16)
                            sp.dma_start(e[TAIL_ROWS:TAIL_ROWS + 1, FULL_G, 0:TAIL_EDGES],
                                         a[N_EDGES - TAIL_EDGES:N_EDGES].rearrange("(p e) -> p e", p=1)
                                         ).then_inc(s_edge, 16)
                        sp.wait_ge(s_pre, 3)
                        sp.dma_start(xN[:, 0:NB - 1, :], x[0:(NB - 1) * P, :].rearrange(
                            "(n p) d -> p n d", p=P)).then_inc(s_x, 16)
                        sp.dma_start(xN[0:LAST, NB - 1, :], x[(NB - 1) * P:N_NODES, :]).then_inc(s_x, 16)
                        sp.wait_ge(s_x, 32)

                    @block.scalar
                    def _(act):
                        for t, w in ((0, Wn), (1, We[:, 0:D]), (2, We[:, D:2 * D]),
                                     (3, Wl[:, 0:D]), (4, Wl[:, D:2 * D])):
                            act.dma_start(wld[:, t, :], w).then_inc(s_w, 16)
                        act.dma_start(W1s[:, :], W1).then_inc(s_b, 16)
                        act.dma_start(W2s[:, :], W2).then_inc(s_b, 16)
                        for c, b in ((b1c, b1), (b2c, b2), (bec, be), (bnc, bn)):
                            act.dma_start(c[:, :], b.rearrange("(p a) -> p a", a=1)).then_inc(s_b, 16)
                        act.dma_start(bnr[:, :], bn.partition_broadcast(P)).then_inc(s_b, 16)
                        act.dma_start(blr[:, :], bl.partition_broadcast(P)).then_inc(s_b, 16)
                        for t, w in enumerate((WnT, Wl1T, Wl2T)):
                            act.wait_ge(s_wt, t + 1)
                            nc.scalar.activation(w[:, :], pW[t][:, 0:D], ACT.Copy).then_inc(s_wtout, 1)
                        act.wait_ge(s_w2, 1)
                        for t, (w, scale) in enumerate(((W12, 1.0), (W22, 2.0), (ber, 1.0))):
                            nc.scalar.activation(w[:, :], pW[0][:, t * D:(t + 1) * D], ACT.Copy,
                                                 scale=scale).then_inc(s_w2out, 1)
                        act.wait_ge(s_w2out, 3)
                        act.wait_ge(s_b, 8 * 16)

                    @block.gpsimd
                    def _(pool):
                        nc.gpsimd.memset(ident[:, :], 0.0).then_inc(s_pool, 1)
                        nc.gpsimd.memset(onesf[:, :], 1.0).then_inc(s_const, 1)
                        nc.gpsimd.memset(onesb[:, :], 1.0).then_inc(s_const, 1)
                        nc.gpsimd.memset(epsC[:, :], EPS).then_inc(s_const, 1)
                        pool.wait_ge(s_pool, 1)
                        nc.gpsimd.affine_select(out=ident[:, :], in_=ident[:, :], compare_op=ALU.not_equal,
                                                fill=1.0, base=0, pattern=[[-1, P]],
                                                channel_multiplier=1).then_inc(s_const, 1)
                        pool.wait_ge(s_const, 3)
                        nc.gpsimd.affine_select(out=tri[:, :], in_=onesb[:, :], compare_op=ALU.is_gt,
                                                fill=0.0, base=0, pattern=[[1, P]],
                                                channel_multiplier=-1).then_inc(s_const, 1)
                        nc.gpsimd.iota(idColF[:, :], pattern=[[0, 1]], base=1,
                                       channel_multiplier=1).then_inc(s_const, 1)
                        for t, step, off in ((dbN, 1, 0), (dbase, NB, 0)):
                            nc.gpsimd.iota(t[:, :], pattern=[[step, NB]], base=off, channel_multiplier=0,
                                           allow_small_or_imprecise_dtypes=True).then_inc(s_const, 1)
                        for t, n, rep, off in ((iotaS, NB, WIN, 0), (iotaN, P, CH, 1), (iotaR, P, WIN, 0)):
                            nc.gpsimd.iota(t[:, :, :], pattern=[[1, n], [0, rep]], base=off,
                                           channel_multiplier=0,
                                           allow_small_or_imprecise_dtypes=True).then_inc(s_const, 1)
                        pool.wait_ge(s_const, 11)

                    @block.vector
                    def _(dve):
                        nc.vector.memset(eD[:, FULL_G, :], PAD_DST).then_inc(s_pre, 1)
                        nc.vector.memset(eS[:, FULL_G, :], 0).then_inc(s_pre, 1)
                        nc.vector.memset(xN[:, NB - 1:NBP, :], 0.0).then_inc(s_pre, 1)
                        dve.wait_ge(s_const, 7)
                        nc.vector.tensor_copy(idCol[:, :], idColF[:, :]).then_inc(s_dvec, 1)
                        nc.vector.tensor_copy(identb[:, :], ident[:, :]).then_inc(s_dvec, 1)
                        dve.wait_ge(s_edge, 6 * 16)
                        nc.vector.tensor_scalar(blkD[:, :, :], eD[:, :, :], 7, None,
                                                ALU.arith_shift_right).then_inc(s_dvec, 1)
                        nc.vector.tensor_scalar(blkS[:, :, :], eS[:, :, :], 7, None,
                                                ALU.arith_shift_right).then_inc(s_dvec, 1)
                        nc.vector.tensor_scalar(eD[:, :, :], eD[:, :, :], P - 1, None,
                                                ALU.bitwise_and).then_inc(s_dvec, 1)
                        nc.vector.tensor_scalar(eS[:, :, :], eS[:, :, :], P - 1, None,
                                                ALU.bitwise_and).then_inc(s_dvec, 1)
                        dve.wait_ge(s_dvec, 6)
                        nc.vector.scalar_tensor_tensor(out=keyR[:, :, :], in0=blkD[:, :, :], scalar=float(NB),
                                                       in1=blkS[:, :, :], op0=ALU.mult,
                                                       op1=ALU.add).then_inc(s_dvec, 1)
                        nc.vector.tensor_reduce(tmax[:, :], blkD[:, :, :], axis=AX.X,
                                                op=ALU.max).then_inc(s_dvec, 1)
                        dve.wait_ge(s_dvec, 8)
                        nc.vector.tensor_scalar(blkS[:, :, :].bitcast(f32), eS[:, :, :], 1.0, None,
                                                ALU.add).then_inc(s_dvec, 1)
                        nc.vector.tensor_scalar(blkD[:, :, :].bitcast(f32), eD[:, :, :], 1.0, None,
                                                ALU.add).then_inc(s_dvec, 1)
                        dve.wait_ge(s_const, 8)
                        nc.vector.tensor_tensor(less[:, :, :], tmax[:, :].unsqueeze(1).to_broadcast([P, NB, EG]),
                                                dbN[:, :].unsqueeze(2).to_broadcast([P, NB, EG]),
                                                ALU.is_lt).then_inc(s_dvec, 1)
                        dve.wait_ge(s_dvec, 11)
                        nc.vector.tensor_reduce(lessN[:, :], less[:, :, :], axis=AX.X,
                                                op=ALU.add).then_inc(s_dvec, 1)
                        n = 0
                        for t in (keyC, idS, idD):
                            for g in range(0, EG, 4):
                                k = min(4, EG - g) * P
                                dve.wait_ge(s_colps, n + 1)
                                nc.vector.tensor_copy(t[:, g * P:g * P + k],
                                                      pT[n % 4][:, 0:k]).then_inc(s_colout, 1)
                                n += 1
                        dve.wait_ge(s_win, 1)
                        nc.vector.tensor_copy(ctl[0:1, 0:NB], pW[1][0:1, 0:NB]).then_inc(s_dvec, 1)
                        dve.wait_ge(s_w2out, 2)
                        nc.vector.scalar_tensor_tensor(out=WD[:, :], in0=W22[:, :], scalar=-0.5, in1=W12[:, :],
                                                       op0=ALU.mult, op1=ALU.add).then_inc(s_dvec, 1)
                        dve.wait_ge(s_dvec, 14)
                        dve.wait_ge(s_colout, n)

                    @block.tensor
                    def _(pe):
                        pe.wait_ge(s_const, 4)
                        pe.wait_ge(s_w, 5 * 16)
                        for t, k in enumerate((0, 3, 4)):
                            nc.tensor.transpose(pW[t][:, 0:D], wld[:, k, :], ident[:, :]).then_inc(s_wt, 1)
                        pe.wait_ge(s_wtout, 3)
                        pe.wait_ge(s_b, 8 * 16)
                        nc.tensor.matmul(pW[0][:, 0:D], wld[:, 1, :], Wl2T[:, :], start=True, stop=True)
                        nc.tensor.matmul(pW[0][:, D:2 * D], wld[:, 2, :], Wl2T[:, :], start=True, stop=True)
                        nc.tensor.matmul(pW[0][:, 2 * D:3 * D], bec[:, 0:1].to_broadcast([P, P]), Wl2T[:, :],
                                         start=True, stop=True).then_inc(s_w2, 1)
                        n = 0
                        for t, r in enumerate((keyR[:, :, :], blkS[:, :, :].bitcast(f32),
                                               blkD[:, :, :].bitcast(f32))):
                            pe.wait_ge(s_dvec, 10)
                            for g in range(0, EG, 4):
                                if n >= 4:
                                    pe.wait_ge(s_colout, n - 3)
                                for k in range(min(4, EG - g)):
                                    last = nc.tensor.transpose(pT[n % 4][:, k * P:(k + 1) * P], r[:, g + k, :],
                                                               ident[:, :])
                                last.then_inc(s_colps, 1)
                                n += 1
                        pe.wait_ge(s_dvec, 12)
                        nc.tensor.matmul(pW[1][0:1, 0:NB], onesf[:, 0:1], lessN[:, :], start=True,
                                         stop=True).then_inc(s_win, 1)

            c1 = ExitStack()
            with c1:
                kk = [sb(f"kk{i}", [P, WIN], bf16, c1) for i in range(2)]
                oh = [sb(f"oh{i}", [P, NB, WIN], bf16, c1) for i in range(2)]
                upto = [sb(f"upto{i}", [P, NWC, NB], bf16, c1) for i in range(2)]
                nv, nr = 2 * NB * WIN, P * WIN
                val = [work[:, i * nv:(i + 1) * nv].rearrange("p (v s j) -> p v s j", v=2, s=NB)
                       for i in range(2)]
                ohr = [work[:, 2 * nv + i * nr:2 * nv + (i + 1) * nr].rearrange("p (r j) -> p r j", r=P)
                       for i in range(2)]
                picked = sb("picked", [P, NWC, WC, NB], bf16, c1)
                rank = [sb(f"rank{i}", [P, WIN], bf16, c1) for i in range(2)]
                cntB = sb("cntB", [P, NB, NB], f32, c1)
                rowS = [sb(f"rowS{i}", [2 * NB, P], u8, c1) for i in range(2)]
                stat = sb("stat", [P, 4], f32, c1)
                pC = ps("pC", [P, NWC, GC], c1)
                pS = [ps(f"pS{i}", [P, GC], c1) for i in range(2)]
                pB = ps("pB", [P, GC], c1)
                pR = ps("pR", [P, GC], c1)
                (q_kk, q_oh, q_upto, q_vs, q_vd, q_cnt, q_pick, q_rank, q_ohr, q_slot,
                 q_tab, q_bkt, q_bktout, q_row, q_rowout, q_rowdma0, q_rowdma1, q_stat) = (
                    sem("q_" + n) for n in
                    ("kk", "oh", "upto", "vs", "vd", "cnt", "pick", "rank", "ohr", "slot",
                     "tab", "bkt", "bktout", "row", "rowout", "rowdma0", "rowdma1", "stat"))
                q_rowdma = (q_rowdma0, q_rowdma1)
                with nc.Block() as block:
                    @block.vector
                    def _(dve):
                        def encode(b, p):
                            t0 = dve.value_load(ctl[0:1, ds(b, 1)], min_val=0, max_val=NT - WIN)
                            wait(dve, q_cnt, b - 1)
                            wait(dve, q_vd, b - 1)
                            nc.vector.tensor_scalar(kk[p][:, :], keyC[:, ds(t0, WIN)], dbase[:, ds(b, 1)], None,
                                                    ALU.subtract).then_inc(q_kk, 1)
                            dve.wait_ge(q_kk, b + 1)
                            nc.vector.tensor_tensor(oh[p][:, :, :], iotaS[:, :, :],
                                                    kk[p][:, :].unsqueeze(1).to_broadcast([P, NB, WIN]),
                                                    ALU.is_equal).then_inc(q_oh, 1)

                        def values(b, p):
                            t0 = dve.value_load(ctl[0:1, ds(b, 1)], min_val=0, max_val=NT - WIN)
                            wait(dve, q_slot, b - 1)
                            dve.wait_ge(q_oh, b + 1)
                            nc.vector.tensor_tensor(val[p][:, 0], oh[p][:, :, :],
                                                    idS[:, ds(t0, WIN)].unsqueeze(1).to_broadcast([P, NB, WIN]),
                                                    ALU.mult).then_inc(q_vs, 1)

                        def place(b, p):
                            dve.wait_ge(q_cnt, b + 1)
                            nc.vector.tensor_tensor(
                                picked[:, :, :, :],
                                pC[:, :, 0:WC * NB].rearrange("p c (j s) -> p c j s", s=NB),
                                oh[p][:, :, :].rearrange("p s (c j) -> p c j s", j=WC),
                                ALU.mult).then_inc(q_pick, 1)
                            dve.wait_ge(q_pick, b + 1)
                            with nc.allow_low_precision("one term isn't zero; a rank over 255 rounds to over 127"):
                                nc.vector.tensor_reduce(rank[p][:, :],
                                                        picked[:, :, :, :].rearrange("p c j s -> p (c j) s"),
                                                        axis=AX.X, op=ALU.add).then_inc(q_rank, 1)
                            dve.wait_ge(q_rank, b + 1)
                            wait(dve, q_slot, b - 1)
                            nc.vector.tensor_tensor(ohr[p][:, :, :], iotaR[:, :, :],
                                                    rank[p][:, :].unsqueeze(1).to_broadcast([P, P, WIN]),
                                                    ALU.is_equal).then_inc(q_ohr, 1)

                        encode(0, 0)
                        encode(1, 1)
                        values(0, 0)
                        place(0, 0)

                        def two(b):
                            encode(b + 1, 0)
                            values(b, 1)
                            place(b, 1)
                            encode(b + 2, 1)
                            values(b + 1, 0)
                            place(b + 1, 0)
                        two(1)
                        with dve.Fori(1, (NB - 3) // 2) as i:
                            two(i * 2 + 1)
                        encode(NB - 1, 0)
                        values(NB - 2, 1)
                        place(NB - 2, 1)
                        values(NB - 1, 0)
                        place(NB - 1, 0)
                        dve.wait_ge(q_bktout, NB)
                        nc.vector.tensor_reduce(stat[:, 0:1], cntB[:, :, :], axis=AX.XY,
                                                op=ALU.add).then_inc(q_stat, 1)
                        nc.vector.tensor_reduce(stat[:, 1:2], cntB[:, :, :], axis=AX.XY,
                                                op=ALU.max).then_inc(q_stat, 1)
                        dve.wait_ge(q_stat, 2)
                        nc.vector.tensor_scalar(stat[:, 2:3], stat[:, 1:2], float(P), None,
                                                ALU.is_le).then_inc(q_stat, 1)
                        dve.wait_ge(q_stat, 3)
                        nc.vector.scalar_tensor_tensor(out=ctl[0:1, FLAG:FLAG + 1], in0=stat[0:1, 0:1],
                                                       scalar=float(N_EDGES), in1=stat[0:1, 2:3],
                                                       op0=ALU.is_equal, op1=ALU.mult).then_inc(q_stat, 1)
                        dve.wait_ge(q_stat, 4)

                    @block.gpsimd
                    def _(pool):
                        def values(b, p):
                            t0 = pool.value_load(ctl[0:1, ds(b, 1)], min_val=0, max_val=NT - WIN)
                            pool.wait_ge(q_oh, b + 1)
                            wait(pool, q_slot, b - 1)
                            nc.gpsimd.tensor_tensor(val[p][:, 1], oh[p][:, :, :],
                                                    idD[:, ds(t0, WIN)].unsqueeze(1).to_broadcast([P, NB, WIN]),
                                                    ALU.mult).then_inc(q_vd, 1)

                        values(0, 0)
                        values(1, 1)
                        with pool.Fori(1, NB // 2) as i:
                            values(i * 2, 0)
                            values(i * 2 + 1, 1)
                        values(NB - 1, 0)

                    @block.tensor
                    def _(pe):
                        def count(b, p):
                            pe.wait_ge(q_oh, b + 1)
                            wait(pe, q_upto, b)
                            wait(pe, q_bktout, b)
                            o = oh[p][:, :, :].rearrange("p s j -> p j s")
                            sums = pB[:, 0:NWC * NB].rearrange("p (c s) -> p c s", s=NB)
                            for j in range(WIN):
                                c = j // WC
                                last = nc.tensor.matmul(sums[:, c:NWC, :], onesb[:, :],
                                                        o[:, j:j + 1, :].to_broadcast([P, NWC - c, NB]),
                                                        start=j == 0, stop=j == WIN - 1, skip_group_check=True)
                            last.then_inc(q_bkt, 1)
                            wait(pe, q_pick, b)
                            for c in range(NWC):
                                full = pC[:, c, 0:WC * NB].rearrange("p (j s) -> p j s", s=NB)
                                nc.tensor.matmul(full, tri[:, :], o[:, c * WC:(c + 1) * WC, :],
                                                 start=True, stop=True)
                                for j in range(WC - 1):
                                    last = nc.tensor.matmul(
                                        full[:, j + 1:WC, :], onesb[:, :],
                                        o[:, c * WC + j:c * WC + j + 1, :].to_broadcast([P, WC - 1 - j, NB]),
                                        start=False, stop=True, skip_group_check=True)
                            pe.wait_ge(q_upto, b + 1)
                            for c in range(1, NWC):
                                full = pC[:, c, 0:WC * NB].rearrange("p (j s) -> p j s", s=NB)
                                last = nc.tensor.matmul(full, identb[:, :], upto[p][:, c - 1:c, :]
                                                        .to_broadcast([P, WC, NB]), start=False, stop=True,
                                                        skip_group_check=True)
                            last.then_inc(q_cnt, 1)

                        def fill(b, p):
                            pe.wait_ge(q_ohr, b + 1)
                            pe.wait_ge(q_vs, b + 1)
                            pe.wait_ge(q_vd, b + 1)
                            wait(pe, q_tab, b - 1)
                            for j in range(WIN):
                                last = nc.tensor.matmul(
                                    pS[p][:, 0:2 * NB], ohr[p][:, :, j],
                                    val[p][:, :, :, j].rearrange("p v s -> p (v s)"),
                                    start=j == 0, stop=j == WIN - 1)
                            last.then_inc(q_slot, 1)
                            pe.wait_ge(q_tab, b + 1)
                            wait(pe, q_rowout, b)
                            nc.tensor.matmul(pR[0:2 * NB, 0:P], tab[:, ds(b, 1)].rearrange("p o v s -> p (o v s)"),
                                             identb[:, :], start=True, stop=True).then_inc(q_row, 1)

                        count(0, 0)
                        count(1, 1)
                        fill(0, 0)

                        def two(b):
                            count(b + 1, 0)
                            fill(b, 1)
                            count(b + 2, 1)
                            fill(b + 1, 0)
                        two(1)
                        with pe.Fori(1, (NB - 3) // 2) as i:
                            two(i * 2 + 1)
                        count(NB - 1, 0)
                        fill(NB - 2, 1)
                        fill(NB - 1, 0)

                    @block.scalar
                    def _(act):
                        def sums(b, p):
                            act.wait_ge(q_bkt, b + 1)
                            wait(act, q_cnt, b - 1)
                            nc.scalar.activation(upto[p][:, :, :].rearrange("p c s -> p (c s)"),
                                                 pB[:, 0:NWC * NB], ACT.Copy).then_inc(q_upto, 1)
                            nc.scalar.activation(cntB[:, ds(b, 1), :], pB[:, (NWC - 1) * NB:NWC * NB].unsqueeze(1),
                                                 ACT.Copy).then_inc(q_bktout, 1)

                        def leave(b, p):
                            act.wait_ge(q_slot, b + 1)
                            nc.scalar.activation(tab[:, ds(b, 1)].rearrange("p o v s -> p (o v s)"),
                                                 pS[p][:, 0:2 * NB], ACT.Copy).then_inc(q_tab, 1)

                        def row(b, p):
                            act.wait_ge(q_row, b + 1)
                            wait(act, q_rowdma[p], (b - p) * 16)
                            nc.scalar.activation(rowS[p][:, :], pR[0:2 * NB, 0:P], ACT.Copy).then_inc(q_rowout, 1)

                        def both(b, p):
                            sums(b + 1, 1 - p)
                            leave(b, p)
                            row(b, p)
                        sums(0, 0)
                        both(0, 0)
                        both(1, 1)
                        with act.Fori(1, NB // 2) as i:
                            both(i * 2, 0)
                            both(i * 2 + 1, 1)
                        leave(NB - 1, 0)
                        row(NB - 1, 0)

                    @block.sync
                    def _(sp):
                        def save(b, p):
                            sp.wait_ge(q_rowout, b + 1)
                            for v in range(2):
                                sp.dma_start(rows[v][:, ds(b, 1), :].rearrange("s o r -> s (o r)"),
                                             rowS[p][v * NB:(v + 1) * NB, :].bitcast(u16)).then_inc(q_rowdma[p], 16)

                        with sp.Fori(0, NB // 2) as i:
                            save(i * 2, 0)
                            save(i * 2 + 1, 1)
                        save(NB - 1, 0)
                        sp.wait_ge(q_rowdma0, 32 * (NB // 2 + 1))
                        sp.wait_ge(q_rowdma1, 32 * (NB // 2))

        def norm_block(name, add_hT):
            cn = ExitStack()
            with cn:
                st = sb(name + "_st", [P, NBP, 6], f32, cn)
                mv = sb(name + "_mv", [P, NBP, 2], f32, cn)
                std = sb(name + "_std", [P, NBP], f32, cn)
                rstd = sb(name + "_rstd", [P, NBP], f32, cn)
                xn = [sb(f"{name}_xn{i}", [P, G, D], f32, cn) for i in range(2)]
                pN = [ps(f"{name}_p{i}", [P, GC], cn) for i in range(2)]
                pH = [ps(f"{name}_h{i}", [P, GC], cn) for i in range(2)]
                n_ht, n_add, n_st, n_mv, n_std, n_rstd, n_xn, n_tr, n_out = (
                    sem(name + "_" + n) for n in ("ht", "add", "st", "mv", "std", "rstd", "xn", "tr", "out"))
                with nc.Block() as block:
                    @block.vector
                    def _(dve):
                        if add_hT:
                            def add(g, p):
                                dve.wait_ge(n_ht, g + 1)
                                nc.vector.tensor_tensor(
                                    xN[:, ds(g * G, G), :], xN[:, ds(g * G, G), :],
                                    pH[p][:, :].rearrange("p (k d) -> p k d", d=D), ALU.add).then_inc(n_add, 1)
                            with dve.Fori(0, NG // 2) as i:
                                add(i * 2, 0)
                                add(i * 2 + 1, 1)
                            add(NG - 1, 0)
                            dve.wait_ge(n_add, NG)
                        with dve.Fori(0, G) as i:
                            for k in range(NG):
                                b = i * NG + k
                                nc.vector.bn_stats(st[:, ds(b, 1), :].rearrange("p o s -> p (o s)"),
                                                   xN[:, ds(b, 1), :].rearrange("p o d -> p (o d)")
                                                   ).then_inc(n_st, 1)
                        dve.wait_ge(n_st, NBP)
                        nc.vector.tensor_tensor(mv[:, :, 0], st[:, :, 1], st[:, :, 4], ALU.add).then_inc(n_mv, 1)
                        nc.vector.tensor_tensor(mv[:, :, 1], st[:, :, 1], st[:, :, 4], ALU.subtract).then_inc(n_mv, 1)
                        nc.vector.tensor_tensor(rstd[:, :], st[:, :, 2], st[:, :, 5], ALU.add).then_inc(n_mv, 1)
                        dve.wait_ge(n_mv, 3)
                        nc.vector.tensor_scalar(mv[:, :, 0], mv[:, :, 0], 0.5, None, ALU.mult).then_inc(n_mv, 1)
                        nc.vector.scalar_tensor_tensor(out=std[:, :], in0=mv[:, :, 1], scalar=0.25,
                                                       in1=mv[:, :, 1], op0=ALU.mult,
                                                       op1=ALU.mult).then_inc(n_mv, 1)
                        dve.wait_ge(n_mv, 5)
                        nc.vector.scalar_tensor_tensor(out=mv[:, :, 1], in0=rstd[:, :], scalar=1.0 / D,
                                                       in1=std[:, :], op0=ALU.mult,
                                                       op1=ALU.add).then_inc(n_mv, 1)
                        dve.wait_ge(n_std, 1)
                        nc.vector.reciprocal(rstd[:, :], std[:, :]).then_inc(n_rstd, 1)
                        dve.wait_ge(n_rstd, 1)

                        def scale(g, p):
                            wait(dve, n_tr, g - 1)
                            for k in range(G):
                                b = g * G + k
                                last = nc.vector.tensor_scalar(
                                    xn[p][:, k, :], xN[:, ds(b, 1), :].rearrange("p o d -> p (o d)"),
                                    mv[:, ds(b, 1), 0:1].rearrange("p o s -> p (o s)"), rstd[:, ds(b, 1)],
                                    ALU.subtract, ALU.mult)
                            last.then_inc(n_xn, 1)
                        scale(0, 0)
                        scale(1, 1)
                        with dve.Fori(1, NG // 2) as i:
                            scale(i * 2, 0)
                            scale(i * 2 + 1, 1)
                        scale(NG - 1, 0)

                    @block.tensor
                    def _(pe):
                        if add_hT:
                            def back(g, p):
                                wait(pe, n_add, g - 1)
                                for k in range(G):
                                    last = nc.tensor.transpose(pH[p][:, k * P:(k + 1) * P], hcopy(k, p),
                                                               ident[:, :])
                                last.then_inc(n_ht, 1)
                            def hcopy(k, p):
                                return xn[p][:, k, :]
                            def back_all(g, p):
                                pe.wait_ge(n_out, g + 1)
                                back(g, p)
                            back_all(0, 0)
                            back_all(1, 1)
                            with pe.Fori(1, NG // 2) as i:
                                back_all(i * 2, 0)
                                back_all(i * 2 + 1, 1)
                            back_all(NG - 1, 0)

                        def turn(g, p):
                            pe.wait_ge(n_xn, g + 1)
                            wait(pe, n_out, g - 1 + (NG if add_hT else 0))
                            for k in range(G):
                                last = nc.tensor.transpose(pN[p][:, k * P:(k + 1) * P], xn[p][:, k, :],
                                                           ident[:, :])
                            last.then_inc(n_tr, 1)
                        turn(0, 0)
                        turn(1, 1)
                        with pe.Fori(1, NG // 2) as i:
                            turn(i * 2, 0)
                            turn(i * 2 + 1, 1)
                        turn(NG - 1, 0)

                    @block.scalar
                    def _(act):
                        if add_hT:
                            def fetch(g, p):
                                wait(act, n_ht, g - 1)
                                nc.scalar.activation(xn[p][:, :, :].rearrange("p k d -> p (k d)"),
                                                     hT[:, ds(g * GC, GC)], ACT.Copy).then_inc(n_out, 1)
                            fetch(0, 0)
                            fetch(1, 1)
                            with act.Fori(1, NG // 2) as i:
                                fetch(i * 2, 0)
                                fetch(i * 2 + 1, 1)
                            fetch(NG - 1, 0)
                        act.wait_ge(n_mv, 6)
                        nc.scalar.activation(std[:, :], mv[:, :, 1], ACT.Sqrt, bias=epsC[:, 0:1]
                                             ).then_inc(n_std, 1)

                        def leave(g, p):
                            act.wait_ge(n_tr, g + 1)
                            nc.scalar.activation(hT[:, ds(g * GC, GC)], pN[p][:, :], ACT.Relu).then_inc(n_out, 1)
                        with act.Fori(0, NG // 2) as i:
                            leave(i * 2, 0)
                            leave(i * 2 + 1, 1)
                        leave(NG - 1, 0)

        norm_block("n1", False)

        ca = ExitStack()
        with ca:
            ohe = [sb(f"ohe{i}", [P, G, 2, P, CH], bf16, ca) for i in range(2)]
            blk = [sb(f"blk{i}", [P, CH, GC], bf16, ca) for i in range(2)]
            cntP = sb("cntP", [P, NG, NB], f32, ca)
            own = sb("own", [P, P], f32, ca)
            pA = [ps(f"pA{i}", [P, GC], ca) for i in range(CH)]
            pD = ps("pD", [P, GC], ca)
            a_oh, a_mm, a_ev, a_deg, a_dcopy, a_dma0, a_dma1, a_cnt = (
                sem("a_" + n) for n in ("oh", "mm", "ev", "deg", "dcopy", "dma0", "dma1", "cnt"))
            a_dma = (a_dma0, a_dma1)
            cntT = work[:, :].bitcast(f32)[:, 0:NBP * P]

            def steps(body):
                def pair(m):
                    for t in range(2 * NCH):
                        body(m * 2 + t // NCH, t % NCH, t % 2, G)
                return pair

            with nc.Block() as block:
                @block.vector
                def _(dve):
                    flag = dve.value_load(ctl[0:1, FLAG:FLAG + 1], min_val=0, max_val=1)

                    def hot(g, c, p, nj):
                        n = g * NCH + c
                        wait(dve, a_mm, (n - 1) * CH)
                        for j in range(nj):
                            for v in range(2):
                                last = nc.vector.tensor_tensor(
                                    ohe[p][:, j, v], iotaN[:, :, :],
                                    tab[:, ds(g * G + j, 1), v, c * CH:(c + 1) * CH].to_broadcast([P, P, CH]),
                                    ALU.is_equal)
                        last.then_inc(a_oh, 1)
                        if c == 2 and not (isinstance(g, int) and g == 0):
                            degrees(g - 1)

                    def degrees(g, cols=GC):
                        dve.wait_ge(a_deg, (g + 1) * NCH)
                        nc.vector.tensor_scalar(dinvT[:, ds(g * GC, cols)], pD[:, 0:cols], 1.0, None,
                                                ALU.add).then_inc(a_dcopy, 1)

                    with dve.If(flag > 0):
                        nc.vector.memset(dinvT[:, NB * P:NBP * P], 1.0).then_inc(a_cnt, 1)
                        pair = steps(hot)
                        pair(0)
                        with dve.Fori(1, NG // 2) as m:
                            pair(m)
                        for c in range(NCH):
                            hot(NG - 1, c, c % 2, 1)
                        degrees(NG - 1, P)
                        dve.wait_ge(a_ev, NG * NCH * CH)
                        nc.vector.tensor_reduce(cntN[:, :], cntP[:, :, :].rearrange("p g s -> p s g"), axis=AX.X,
                                                op=ALU.add).then_inc(a_cnt, 1)
                        dve.wait_ge(a_dcopy, NG)
                    with dve.Else():
                        nc.vector.memset(dinvT[:, :], 1.0)
                        nc.vector.memset(cntT, 0.0)
                        dve.drain()
                        with dve.Fori(0, N_EDGES) as e:
                            s = dve.value_load(src1[0:1, ds(e, 1)], min_val=0, max_val=N_NODES - 1)
                            d = dve.value_load(dst1[0:1, ds(e, 1)], min_val=0, max_val=N_NODES - 1)
                            nc.vector.tensor_scalar(dinvT[:, ds(d, 1)], dinvT[:, ds(d, 1)], 1.0, None, ALU.add)
                            nc.vector.tensor_scalar(cntT[:, ds(s, 1)], cntT[:, ds(s, 1)], 1.0, None, ALU.add)
                            dve.drain()
                        with dve.Fori(0, NB) as b:
                            nc.vector.tensor_tensor(own[:, :], cntT[:, ds(b * P, P)], ident[:, :], ALU.mult)
                            dve.drain()
                            nc.vector.tensor_reduce(cntN[:, ds(b, 1)], own[:, :], axis=AX.X, op=ALU.add)
                            dve.drain()

                @block.tensor
                def _(pe):
                    flag = pe.value_load(ctl[0:1, FLAG:FLAG + 1], min_val=0, max_val=1)

                    def add_degrees(g, c, p, nj):
                        n = g * NCH + c
                        pe.wait_ge(a_ev, (n + 1) * CH)
                        if c == 0:
                            wait(pe, a_dcopy, g)
                        for i in range(CH):
                            last = nc.tensor.matmul(pD[:, 0:nj * P], onesb[:, :], blk[p][:, i, 0:nj * P],
                                                    start=c == 0 and i == 0, stop=c == NCH - 1 and i == CH - 1)
                        last.then_inc(a_deg, 1)

                    def count(g, c, p, nj):
                        n = g * NCH + c
                        pe.wait_ge(a_oh, n + 1)
                        for i in range(CH):
                            wait(pe, a_ev, (n - 1) * CH + i + 1)
                            for j in range(nj):
                                last = nc.tensor.matmul(pA[i][:, j * P:(j + 1) * P], ohe[p][:, j, 0, :, i],
                                                        ohe[p][:, j, 1, :, i], start=True, stop=True)
                            last.then_inc(a_mm, 1)
                        if not (isinstance(g, int) and g == 0 and c == 0):
                            if c:
                                add_degrees(g, c - 1, 1 - p, nj)
                            else:
                                add_degrees(g - 1, NCH - 1, 1 - p, G)

                    with pe.If(flag > 0):
                        pair = steps(count)
                        pair(0)
                        with pe.Fori(1, NG // 2) as m:
                            pair(m)
                        for c in range(NCH):
                            count(NG - 1, c, c % 2, 1)
                        add_degrees(NG - 1, NCH - 1, (NCH - 1) % 2, 1)

                @block.scalar
                def _(act):
                    flag = act.value_load(ctl[0:1, FLAG:FLAG + 1], min_val=0, max_val=1)

                    def leave(g, c, p, nj):
                        n = g * NCH + c
                        wait(act, a_dma[p], (n - p) * 8)
                        wait(act, a_deg, n - 1)
                        for i in range(CH):
                            act.wait_ge(a_mm, n * CH + i + 1)
                            nc.scalar.activation(blk[p][:, i, 0:nj * P], pA[i][:, 0:nj * P], ACT.Copy,
                                                 accum_out=cntP[:, ds(g, 1), c * CH + i]).then_inc(a_ev, 1)

                    with act.If(flag > 0):
                        pair = steps(leave)
                        pair(0)
                        with act.Fori(1, NG // 2) as m:
                            pair(m)
                        for c in range(NCH):
                            leave(NG - 1, c, c % 2, 1)

                @block.sync
                def _(sp):
                    flag = sp.value_load(ctl[0:1, FLAG:FLAG + 1], min_val=0, max_val=1)

                    def save(g, c, p, nj):
                        n = g * NCH + c
                        sp.wait_ge(a_ev, (n + 1) * CH)
                        sp.dma_start(adj[ds(g, 1), c, :, :, 0:nj * P].rearrange("o p i n -> (o p) i n"),
                                     blk[p][:, :, 0:nj * P]).then_inc(a_dma[p], 16)

                    with sp.If(flag > 0):
                        pair = steps(save)
                        pair(0)
                        with sp.Fori(1, NG // 2) as m:
                            pair(m)
                        for c in range(NCH):
                            save(NG - 1, c, c % 2, 1)
                        sp.wait_ge(a_dma0, 16 * ((NG * NCH + 1) // 2))
                        sp.wait_ge(a_dma1, 16 * (NG * NCH // 2))

        cv = ExitStack()
        with cv:
            root = sb("root", [P, NBP], f32, cv)
            inv = sb("inv", [P, NBP], f32, cv)
            diag = [sb(f"diag{i}", [P, G, P], f32, cv) for i in range(2)]
            pV = ps("pV", [P, GC], cv)
            pW = [ps(f"pV{i}", [P, GC], cv) for i in range(2)]
            v_deg, v_root, v_inv, v_diag, v_mm, v_out = (
                sem("v_" + n) for n in ("deg", "root", "inv", "diag", "mm", "out"))

            def each(eng, body):
                body(0, 0)
                body(1, 1)
                with eng.Fori(1, NG // 2) as i:
                    body(i * 2, 0)
                    body(i * 2 + 1, 1)
                body(NG - 1, 0)

            with nc.Block() as block:
                @block.tensor
                def _(pe):
                    for b in range(NBP):
                        last = nc.tensor.matmul(pV[:, b:b + 1], dinvT[:, b * P:(b + 1) * P], ident[:, 0:1],
                                                start=True, stop=True)
                    last.then_inc(v_deg, 1)

                    def spread(g, p):
                        pe.wait_ge(v_diag, g + 1)
                        wait(pe, v_out, g - 1)
                        nc.tensor.matmul(pW[p][:, :], onesf[:, :], diag[p][:, :, :].rearrange("p k n -> p (k n)"),
                                         start=True, stop=True).then_inc(v_mm, 1)
                    each(pe, spread)

                @block.scalar
                def _(act):
                    act.wait_ge(v_deg, 1)
                    nc.scalar.activation(root[:, :], pV[:, 0:NBP], ACT.Sqrt).then_inc(v_root, 1)

                    def leave(g, p):
                        act.wait_ge(v_mm, g + 1)
                        nc.scalar.activation(dinvT[:, ds(g * GC, GC)], pW[p][:, :], ACT.Copy).then_inc(v_out, 1)
                    each(act, leave)

                @block.vector
                def _(dve):
                    dve.wait_ge(v_root, 1)
                    nc.vector.reciprocal(inv[:, :], root[:, :]).then_inc(v_inv, 1)
                    dve.wait_ge(v_inv, 1)

                    def place(g, p):
                        wait(dve, v_mm, g - 1)
                        nc.vector.tensor_tensor(diag[p][:, :, :],
                                                ident[:, :].unsqueeze(1).to_broadcast([P, G, P]),
                                                inv[:, ds(g * G, G)].unsqueeze(2).to_broadcast([P, G, P]),
                                                ALU.mult).then_inc(v_diag, 1)
                    each(dve, place)

        cw.close()
        cgr = ExitStack()
        gr = sb("gr", [P, NBP, 2, D], f32r, cgr)

        def table_block(name, W):
            ct = ExitStack()
            with ct:
                hs = [sb(f"{name}_hs{i}", [P, GC], f32, ct) for i in range(2)]
                pG = [ps(f"{name}_p{i}", [P, GC], ct) for i in range(2)]
                t_hs, t_mm, t_hi, t_lo = (sem(name + "_" + n) for n in ("hs", "mm", "hi", "lo"))

                def rows4(t):
                    return t[:, :].rearrange("p (k d) -> p k d", d=D)

                def each(eng, body):
                    body(0, 0)
                    body(1, 1)
                    with eng.Fori(1, NG // 2) as i:
                        body(i * 2, 0)
                        body(i * 2 + 1, 1)
                    body(NG - 1, 0)

                with nc.Block() as block:
                    @block.vector
                    def _(dve):
                        def load(g, p):
                            wait(dve, t_mm, g - 1)
                            nc.vector.tensor_tensor(hs[p][:, :], hT[:, ds(g * GC, GC)],
                                                    dinvT[:, ds(g * GC, GC)], ALU.mult).then_inc(t_hs, 1)

                        def split(g, p):
                            dve.wait_ge(t_hi, g + 1)
                            nc.vector.tensor_tensor(gr[:, ds(g * G, G), 1, :], rows4(pG[p]),
                                                    gr[:, ds(g * G, G), 0, :].bitcast(f32),
                                                    ALU.subtract).then_inc(t_lo, 1)
                        load(0, 0)
                        load(1, 1)
                        split(0, 0)

                        def two(g):
                            load(g + 1, 0)
                            split(g, 1)
                            load(g + 2, 1)
                            split(g + 1, 0)
                        two(1)
                        with dve.Fori(1, (NG - 3) // 2) as i:
                            two(i * 2 + 1)
                        load(NG - 1, 0)
                        split(NG - 2, 1)
                        split(NG - 1, 0)

                    @block.tensor
                    def _(pe):
                        def mul(g, p):
                            pe.wait_ge(t_hs, g + 1)
                            wait(pe, t_lo, g - 1)
                            for k in range(G):
                                last = nc.tensor.matmul(pG[p][:, k * D:(k + 1) * D],
                                                        hs[p][:, k * P:(k + 1) * P], W[:, :],
                                                        start=True, stop=True)
                            last.then_inc(t_mm, 1)
                        each(pe, mul)

                    @block.scalar
                    def _(act):
                        def take(g, p):
                            act.wait_ge(t_mm, g + 1)
                            nc.scalar.activation(gr[:, ds(g * G, G), 0, :], rows4(pG[p]),
                                                 ACT.Copy).then_inc(t_hi, 1)
                        each(act, take)

        def gcn_block(name, W, bias):
            cg = ExitStack()
            with cg:
                NU, SLOTS = 2 * NCH, NCH
                UN = (G, CH - G)
                ring = sb(name + "_ring", [P, SLOTS, G, GC], bf16, cg)
                cnt4 = [sb(f"{name}_cnt4{i}", [P, G, GC], f32r, cg) for i in range(2)]
                cnt3 = sb(f"{name}_cnt3", [P, CH - G, GC], f32r, cg)
                hs = [sb(f"{name}_hs{i}", [P, GC], f32, cg) for i in range(2)]
                sc = [sb(f"{name}_sc{i}", [P, GC], f32, cg) for i in range(2)]
                pO = [ps(f"{name}_p{i}", [P, GC], cg) for i in range(2)]
                gT = ring[:, :, :, :].rearrange("p c i n -> p (c i n)").bitcast(f32)[:, 0:NBP * P]
                g_in = [sem(f"{name}_in{c}") for c in range(SLOTS)]
                g_cast, g_unit, g_mm, g_hs, g_sc, g_out, g_self = (
                    sem(name + "_" + n) for n in ("cast", "unit", "mm", "hs", "sc", "out", "self"))

                def each(eng, body):
                    body(0, 0, G)
                    body(1, 1, G)
                    with eng.Fori(1, NG // 2) as i:
                        body(i * 2, 0, G)
                        body(i * 2 + 1, 1, G)
                    body(NG - 1, 0, 1)

                def counts(p, u):
                    return cnt3 if u % 2 else cnt4[(p + u // 2) % 2]

                with nc.Block() as block:
                    @block.sync
                    def _(sp):
                        flag = sp.value_load(ctl[0:1, FLAG:FLAG + 1], min_val=0, max_val=1)

                        def load(g, p, nj):
                            for u in range(NU):
                                wait(sp, g_cast, g * NU + u - SLOTS + 1)
                                n, i0 = UN[u % 2], u % 2 * G
                                sp.dma_start(ring[:, u % SLOTS, 0:n, 0:nj * P],
                                             adj[ds(g, 1), u // 2, :, i0:i0 + n, 0:nj * P].rearrange(
                                                 "o p i n -> (o p) i n")).then_inc(g_in[u % SLOTS], 16)
                        with sp.If(flag > 0):
                            each(sp, load)

                    @block.tensor
                    def _(pe):
                        flag = pe.value_load(ctl[0:1, FLAG:FLAG + 1], min_val=0, max_val=1)

                        def own(p, nj, start):
                            return nc.tensor.matmul(pO[p][:, 0:nj * P], W[:, :], hs[p][:, 0:nj * P],
                                                    start=start, stop=True, skip_group_check=True)

                        def add(g, p, nj):
                            wait(pe, g_sc, g - 1)
                            for u in range(NU):
                                pe.wait_ge(g_cast, g * NU + u + 1)
                                for i in range(UN[u % 2]):
                                    for part in range(2):
                                        last = nc.tensor.matmul(
                                            pO[p][:, 0:nj * P], gr[:, u // 2 * CH + u % 2 * G + i, part, :],
                                            counts(p, u)[:, i, 0:nj * P], start=u == 0 and i == 0 and part == 0,
                                            stop=False, skip_group_check=True)
                                last.then_inc(g_unit, 1)
                            pe.wait_ge(g_hs, g + 1)
                            own(p, nj, False).then_inc(g_mm, 1)

                        with pe.If(flag > 0):
                            each(pe, add)
                        with pe.Else():
                            with pe.Fori(0, NG) as g:
                                pe.wait_ge(g_hs, g + 1)
                                own(0, G, True).then_inc(g_self, 1)

                    @block.vector
                    def _(dve):
                        flag = dve.value_load(ctl[0:1, FLAG:FLAG + 1], min_val=0, max_val=1)

                        def scaled(g, p, nj):
                            wait(dve, g_mm, g - 1)
                            nc.vector.tensor_tensor(hs[p][:, 0:nj * P], hT[:, ds(g * GC, nj * P)],
                                                    dinvT[:, ds(g * GC, nj * P)], ALU.mult).then_inc(g_hs, 1)

                        def scale_sum(g, p, nj):
                            dve.wait_ge(g_mm, g + 1)
                            wait(dve, g_out, g - 1)
                            nc.vector.tensor_tensor(sc[p][:, 0:nj * P], pO[p][:, 0:nj * P],
                                                    dinvT[:, ds(g * GC, nj * P)], ALU.mult).then_inc(g_sc, 1)

                        def cast(g, p, nj):
                            scaled(g, p, nj)
                            for u in range(NU):
                                dve.wait_ge(g_in[u % SLOTS], (g * 2 + u // SLOTS) * 16 + 16)
                                wait(dve, g_unit, g * NU + u - (1 if u % 2 else 3))
                                n = UN[u % 2]
                                nc.vector.tensor_copy(counts(p, u)[:, 0:n, 0:nj * P],
                                                      ring[:, u % SLOTS, 0:n, 0:nj * P]).then_inc(g_cast, 1)
                                if u == 1 and not (isinstance(g, int) and g == 0):
                                    scale_sum(g - 1, 1 - p, G)
                        with dve.If(flag > 0):
                            each(dve, cast)
                            scale_sum(NG - 1, 0, 1)
                        with dve.Else():
                            with dve.Fori(0, NG) as g:
                                nc.vector.tensor_tensor(hs[0][:, :], hT[:, ds(g * GC, GC)],
                                                        dinvT[:, ds(g * GC, GC)], ALU.mult)
                                dve.drain().then_inc(g_hs, 1)
                                dve.wait_ge(g_self, g + 1)
                                nc.vector.tensor_copy(gT[:, ds(g * GC, GC)], pO[0][:, :])
                                nc.vector.tensor_copy(hT[:, ds(g * GC, GC)], pO[0][:, :])
                                dve.drain()
                            with dve.Fori(0, N_EDGES) as e:
                                s = dve.value_load(src1[0:1, ds(e, 1)], min_val=0, max_val=N_NODES - 1)
                                d = dve.value_load(dst1[0:1, ds(e, 1)], min_val=0, max_val=N_NODES - 1)
                                nc.vector.tensor_tensor(hT[:, ds(d, 1)], hT[:, ds(d, 1)], gT[:, ds(s, 1)],
                                                        ALU.add)
                                dve.drain()
                            with dve.Fori(0, NG) as g:
                                nc.vector.tensor_tensor(hT[:, ds(g * GC, GC)], hT[:, ds(g * GC, GC)],
                                                        dinvT[:, ds(g * GC, GC)], ALU.mult)
                                dve.drain()
                                nc.vector.tensor_scalar(hT[:, ds(g * GC, GC)], hT[:, ds(g * GC, GC)],
                                                        bias[:, 0:1], 0.0, ALU.add, ALU.max)
                                dve.drain()

                    @block.scalar
                    def _(act):
                        flag = act.value_load(ctl[0:1, FLAG:FLAG + 1], min_val=0, max_val=1)

                        def leave(g, p, nj):
                            act.wait_ge(g_sc, g + 1)
                            nc.scalar.activation(hT[:, ds(g * GC, nj * P)], sc[p][:, 0:nj * P], ACT.Relu,
                                                 bias=bias[:, 0:1]).then_inc(g_out, 1)
                        with act.If(flag > 0):
                            each(act, leave)

        table_block("t1", W1s)
        gcn_block("g1", W1s, b1c)
        table_block("t2", W2s)
        gcn_block("g2", W2s, b2c)
        cgr.close()
        norm_block("n2", True)

        ch = ExitStack()
        with ch:
            gp = sb("gp", [P, NBP, 3, D], bf16, ch)
            cnt1 = sb("cnt1", [P, NBP], f32, ch)
            has = sb("has", [P, NBP], f32, ch)
            rcnt = sb("rcnt", [P, NBP], f32, ch)
            ci = ExitStack()
            with ci:
                hs, hv, hw, zt = ([sb(f"h_{n}{i}", [P, GC], f32, ci) for i in range(2)]
                                  for n in ("hs", "hv", "hw", "zt"))
                pF = [ps(f"h_pf{i}", [P, GC], ci) for i in range(2)]
                pG, pZ = ps("h_pg", [P, GC], ci), ps("h_pz", [P, GC], ci)
                pY = [ps(f"h_py{i}", [P, G, 2, D], ci) for i in range(2)]
                (h_c, h_hs, h_mm, h_y, h_v, h_hi, h_rem, h_mid, h_lo, h_t, h_t2, h_z, h_zz, h_yy, h_w) = (
                    sem("h_" + n) for n in ("c", "hs", "mm", "y", "v", "hi", "rem", "mid", "lo", "t", "t2", "z",
                                            "zz", "yy", "w"))

                def four(t):
                    return t.rearrange("p (k d) -> p k d", d=D)

                with nc.Block() as block:
                    @block.scalar
                    def _(act):
                        def copy(g, p):
                            wait(act, h_mm, g - 1)
                            nc.scalar.activation(hs[p][:, :], hT[:, ds(g * GC, GC)], ACT.Copy).then_inc(h_hs, 1)

                        def bias(g, p):
                            act.wait_ge(h_mm, g + 1)
                            wait(act, h_y, g - 1)
                            nc.scalar.activation(hw[p][:, :], pF[p][:, :], ACT.Identity,
                                                 bias=bnc[:, 0:1]).then_inc(h_t, 1)
                            act.wait_ge(h_v, g + 1)
                            nc.scalar.activation(gp[:, ds(g * G, G), 0, :], four(hv[p][:, :]),
                                                 ACT.Copy).then_inc(h_hi, 1)
                            act.wait_ge(h_t, g + 1)
                            nc.scalar.activation(hT.rearrange("p (n c) -> p n c", c=P)[:, ds(g * G, G), :],
                                                 four(hw[p][:, :]), ACT.Copy).then_inc(h_t2, 1)
                            act.wait_ge(h_rem, g + 1)
                            nc.scalar.activation(gp[:, ds(g * G, G), 1, :], four(hv[p][:, :]),
                                                 ACT.Copy).then_inc(h_mid, 1)
                        copy(0, 0)
                        copy(1, 1)
                        bias(0, 0)

                        def two(g):
                            copy(g + 1, 0)
                            bias(g, 1)
                            copy(g + 2, 1)
                            bias(g + 1, 0)
                        two(1)
                        with act.Fori(1, (NG - 3) // 2) as i:
                            two(i * 2 + 1)
                        copy(NG - 1, 0)
                        bias(NG - 2, 1)
                        bias(NG - 1, 0)

                    @block.tensor
                    def _(pe):
                        def mul(g, p):
                            pe.wait_ge(h_hs, g + 1)
                            wait(pe, h_t, g - 1)
                            wait(pe, h_v, g)
                            wait(pe, h_z, g)
                            nc.tensor.matmul(pF[p][:, :], WnT[:, :], hs[p][:, :], start=True, stop=True)
                            for k in range(G):
                                for o, W in ((pG, WnT), (pZ, Wl1T)):
                                    last = nc.tensor.matmul(o[:, k * D:(k + 1) * D],
                                                            hs[p][:, k * P:(k + 1) * P], W[:, :],
                                                            start=True, stop=True)
                            last.then_inc(h_mm, 1)

                        def through(g, p):
                            pe.wait_ge(h_t, g + 1)
                            wait(pe, h_w, 2 * g - 2)
                            for k in range(G):
                                last = nc.tensor.matmul(pY[p][:, k, :, :], hw[p][:, k * P:(k + 1) * P],
                                                        Wout[:, 0:2, :], start=True, stop=True)
                            last.then_inc(h_y, 1)
                        mul(0, 0)
                        mul(1, 1)
                        through(0, 0)

                        def two(g):
                            mul(g + 1, 0)
                            through(g, 1)
                            mul(g + 2, 1)
                            through(g + 1, 0)
                        two(1)
                        with pe.Fori(1, (NG - 3) // 2) as i:
                            two(i * 2 + 1)
                        mul(NG - 1, 0)
                        through(NG - 2, 1)
                        through(NG - 1, 0)

                    @block.vector
                    def _(dve):
                        nc.vector.memset(cnt1[:, :], 0.0).then_inc(h_c, 1)
                        dve.wait_ge(h_c, 1)
                        nc.vector.tensor_copy(cnt1[:, 0:NB], cntN[:, :]).then_inc(h_c, 1)
                        dve.wait_ge(h_c, 2)
                        nc.vector.tensor_scalar(has[:, :], cnt1[:, :], 1.0, None, ALU.min).then_inc(h_c, 1)
                        dve.wait_ge(h_c, 3)
                        nc.vector.tensor_scalar(cnt1[:, :], cnt1[:, :], 1.0, None, ALU.max).then_inc(h_c, 1)
                        dve.wait_ge(h_c, 4)
                        nc.vector.reciprocal(rcnt[:, :], cnt1[:, :]).then_inc(h_c, 1)
                        dve.wait_ge(h_c, 5)

                        def add(g, p, added):
                            nc.vector.tensor_tensor(xN[:, ds(g * G, G), :], xN[:, ds(g * G, G), :],
                                                    four(zt[p][:, :]), ALU.add).then_inc(added, 1)

                        def first(g, p):
                            dve.wait_ge(h_mm, g + 1)
                            wait(dve, h_mid, g - 1)
                            wait(dve, h_lo, g - 1)
                            nc.vector.tensor_tensor(four(hv[p][:, :]), four(pG[:, :]),
                                                    bnr[:, :].unsqueeze(1).to_broadcast([P, G, D]),
                                                    ALU.add).then_inc(h_v, 1)
                            wait(dve, h_yy, 2 * g - 2)
                            nc.vector.tensor_tensor(four(zt[p][:, :]), four(pZ[:, :]),
                                                    blr[:, :].unsqueeze(1).to_broadcast([P, G, D]),
                                                    ALU.add).then_inc(h_z, 1)
                            dve.wait_ge(h_z, g + 1)
                            add(g, p, h_zz)

                        def second(g, p):
                            dve.wait_ge(h_hi, g + 1)
                            dve.wait_ge(h_v, g + 1)
                            nc.vector.tensor_tensor(four(hv[p][:, :]), four(hv[p][:, :]),
                                                    gp[:, ds(g * G, G), 0, :], ALU.subtract).then_inc(h_rem, 1)
                            dve.wait_ge(h_y, g + 1)
                            for k, f in enumerate((rcnt, has)):
                                if k == 0:
                                    dve.wait_ge(h_zz, g + 1)
                                else:
                                    dve.wait_ge(h_yy, 2 * g + 1)
                                nc.vector.tensor_tensor(four(zt[p][:, :]), pY[p][:, :, k, :],
                                                        f[:, ds(g * G, G)].unsqueeze(2).to_broadcast([P, G, D]),
                                                        ALU.mult).then_inc(h_w, 1)
                                dve.wait_ge(h_w, 2 * g + k + 1)
                                add(g, p, h_yy)
                            dve.wait_ge(h_mid, g + 1)
                            dve.wait_ge(h_rem, g + 1)
                            nc.vector.tensor_tensor(gp[:, ds(g * G, G), 2, :], four(hv[p][:, :]),
                                                    gp[:, ds(g * G, G), 1, :], ALU.subtract).then_inc(h_lo, 1)
                        first(0, 0)

                        def two(g):
                            first(g + 1, 1)
                            second(g, 0)
                            first(g + 2, 0)
                            second(g + 1, 1)
                        two(0)
                        with dve.Fori(1, NG // 2) as i:
                            two(i * 2)
                        second(NG - 1, 0)

            posT = dinvT
            cr = ExitStack()
            with cr:
                COLS = CH * P
                sumT = sb("sumT", [P, NBP * P], f32, cr)
                idr = [sumT[:, :].bitcast(u8)[:, c * 2 * COLS:(c + 1) * 2 * COLS] for c in range(NCH)]
                agg0 = NCH * 2 * COLS // 4
                agg = sumT[:, agg0:agg0 + 2 * D].rearrange("p (v d) -> p v d", v=2)
                dif = sb("dif", [P, 1], f32, cr)
                pick = [sb(f"pick{i}", [P, 2 * COLS], bf16, cr) for i in range(2)]
                AC = (CH - 2) * P
                away = sumT[:, agg0 + 2 * D:agg0 + 2 * D + AC // 2].bitcast(bf16)
                put = [sb(f"put{i}", [P, P, CH], f32r, cr) for i in range(2)]
                msg = [sb(f"msg{i}", [P, CH, 2, 2, D], f32r, cr) for i in range(2)]
                nega = [sb(f"nega{i}", [P, 3, D], bf16, cr) for i in range(2)]
                pD = [ps(f"pD{i}", [P, 2 * G, P], cr) for i in range(2)]
                pAg = ps("pAg", [P, 2, D], cr)
                pTr = ps("pTr", [P, 2, P], cr)
                e_in = [sem(f"e_in{c}") for c in range(NCH)]
                e_picka, e_pickb, e_away, e_put, e_neg, e_gath, e_hi, e_low, e_sum, e_agg, e_tr, e_out = (
                    sem("e_" + n) for n in ("picka", "pickb", "away", "put", "neg", "gath", "hi", "low", "sum",
                                            "agg", "tr", "out"))

                def each(eng, body):
                    body(0, 0, True, False)
                    body(1, 1, False, False)
                    with eng.Fori(1, NB // 2) as i:
                        body(i * 2, 0, False, False)
                        body(i * 2 + 1, 1, False, False)
                    body(NB - 1, 0, False, True)

                with nc.Block() as block:
                    @block.sync
                    def _(sp):
                        flag = sp.value_load(ctl[0:1, FLAG:FLAG + 1], min_val=0, max_val=1)

                        def load(a):
                            for c in range(NCH):
                                wait(sp, e_picka, (a - 1) * NCH + c + 1)
                                wait(sp, e_pickb, (a - 1) * NCH + c + 1)
                                for v in range(2):
                                    sp.dma_start(idr[c][:, v * COLS:(v + 1) * COLS].bitcast(u16),
                                                 rows[v][ds(a, 1), c * CH:(c + 1) * CH, :]
                                                 .rearrange("o b r -> (o b r)").partition_broadcast(P)
                                                 ).then_inc(e_in[c], 16)
                        with sp.If(flag > 0):
                            load(0)
                            with sp.Fori(1, NB) as a:
                                load(a)

                    @block.vector
                    def _(dve):
                        flag = dve.value_load(ctl[0:1, FLAG:FLAG + 1], min_val=0, max_val=1)

                        def one_hot_nodes(a, c, q):
                            p = (q + c) % 2
                            dve.wait_ge(e_in[c], a * 32 + 32)
                            wait(dve, e_gath, a * NCH + c - 1)
                            nc.vector.tensor_scalar(pick[p][:, AC:], idr[c][:, AC:], idCol[:, 0:1], None,
                                                    ALU.is_equal).then_inc(e_pickb, 1)

                        def one_hot_slots(a, c, q):
                            p = (q + c) % 2
                            wait(dve, e_sum, a * NCH + c - 1)
                            nc.vector.tensor_tensor(
                                put[p][:, :, :], iotaN[:, :, :],
                                tab[:, c * CH:(c + 1) * CH, 0, ds(a, 1)].rearrange("p b o -> p (b o)")
                                .unsqueeze(1).to_broadcast([P, P, CH]), ALU.is_equal).then_inc(e_put, 1)

                        def low(a, c, q):
                            p = (q + c) % 2
                            dve.wait_ge(e_hi, (a * NCH + c) * 2 + 1)
                            nc.vector.tensor_tensor(msg[p][:, :, 1, 1, :], pD[p][:, 0:CH, :],
                                                    msg[p][:, :, 0, 1, :].bitcast(f32),
                                                    ALU.subtract).then_inc(e_low, 1)
                            dve.wait_ge(e_hi, (a * NCH + c) * 2 + 2)
                            nc.vector.scalar_tensor_tensor(
                                out=msg[p][:, :, 1, 0, :], in0=pD[p][:, 0:CH, :], scalar=0.0,
                                in1=msg[p][:, :, 0, 0, :].bitcast(f32), op0=ALU.max,
                                op1=ALU.subtract).then_inc(e_low, 1)

                        def block_of(a, q, first, last):
                            def ahead(make, c):
                                if c < NCH:
                                    make(a, c, q)
                                elif not last:
                                    make(a + 1, c - NCH, 1 - q)
                            if first:
                                one_hot_nodes(0, 0, 0)
                                one_hot_nodes(0, 1, 0)
                                one_hot_slots(0, 0, 0)
                            for c in range(NCH):
                                low(a, c, q)
                                ahead(one_hot_nodes, c + 2)
                                ahead(one_hot_slots, c + 1)
                        with dve.If(flag > 0):
                            each(dve, block_of)
                        with dve.Else():
                            nc.vector.memset(posT[:, :], 0.0)
                            nc.vector.memset(sumT[:, :], 0.0)
                            dve.drain()
                            with dve.Fori(0, N_EDGES) as e:
                                s = dve.value_load(src1[0:1, ds(e, 1)], min_val=0, max_val=N_NODES - 1)
                                d = dve.value_load(dst1[0:1, ds(e, 1)], min_val=0, max_val=N_NODES - 1)
                                nc.vector.tensor_tensor(dif[:, :], hT[:, ds(d, 1)], hT[:, ds(s, 1)],
                                                        ALU.subtract)
                                dve.drain()
                                nc.vector.tensor_tensor(sumT[:, ds(s, 1)], sumT[:, ds(s, 1)], dif[:, :], ALU.add)
                                nc.vector.scalar_tensor_tensor(out=posT[:, ds(s, 1)], in0=dif[:, :], scalar=0.0,
                                                               in1=posT[:, ds(s, 1)], op0=ALU.max,
                                                               op1=ALU.add)
                                dve.drain()
                            nc.vector.tensor_copy(hT[:, :], sumT[:, :])

                    @block.tensor
                    def _(pe):
                        flag = pe.value_load(ctl[0:1, FLAG:FLAG + 1], min_val=0, max_val=1)

                        def gather(a, c, q):
                            p = (q + c) % 2
                            pe.wait_ge(e_picka, a * NCH + c + 1)
                            pe.wait_ge(e_pickb, a * NCH + c + 1)
                            wait(pe, e_low, (a * NCH + c - 1) * 2)
                            if c == 0:
                                pe.wait_ge(e_neg, a + 1)
                            for k in range(CH):
                                for t in range(3):
                                    nc.tensor.matmul(pD[p][:, k, :], pick[p][:, k * P:(k + 1) * P],
                                                     nega[q][:, t, :], start=t == 0, stop=False)
                                for t in range(3):
                                    last = nc.tensor.matmul(pD[p][:, k, :],
                                                            pick[p][:, COLS + k * P:COLS + (k + 1) * P],
                                                            gp[:, c * CH + k, t, :], start=False, stop=t == 2)
                            last.then_inc(e_gath, 1)

                        def total(a, c, q):
                            p = (q + c) % 2
                            pe.wait_ge(e_put, a * NCH + c + 1)
                            pe.wait_ge(e_hi, (a * NCH + c + 1) * 2)
                            pe.wait_ge(e_low, (a * NCH + c + 1) * 2)
                            if c == 0:
                                wait(pe, e_agg, a)
                            for k in range(CH):
                                for t in range(2):
                                    last = nc.tensor.matmul(
                                        pAg[:, :, :], put[p][:, :, k], msg[p][:, k, t, :, :],
                                        start=c == 0 and k == 0 and t == 0,
                                        stop=c == NCH - 1 and k == CH - 1 and t == 1)
                            last.then_inc(e_sum, 1)

                        def turn(a):
                            pe.wait_ge(e_agg, a + 1)
                            wait(pe, e_out, a * 2)
                            for v in range(2):
                                last = nc.tensor.transpose(pTr[:, v, :], agg[:, v, :], ident[:, :])
                            last.then_inc(e_tr, 1)

                        def block_of(a, q, first, last):
                            if first:
                                gather(0, 0, 0)
                            for c in range(NCH):
                                if c + 1 < NCH:
                                    gather(a, c + 1, q)
                                elif not last:
                                    gather(a + 1, 0, 1 - q)
                                total(a, c, q)
                                if c == 1 and not first:
                                    turn(a - 1)
                            if last:
                                turn(a)
                        with pe.If(flag > 0):
                            each(pe, block_of)

                    @block.scalar
                    def _(act):
                        flag = act.value_load(ctl[0:1, FLAG:FLAG + 1], min_val=0, max_val=1)

                        def negate(a, q):
                            wait(act, e_sum, (a - 1) * NCH)
                            nc.scalar.activation(nega[q][:, :, :], gp[:, ds(a, 1), :, :].rearrange(
                                "p o t d -> p (o t) d"), ACT.Copy, scale=-1.0).then_inc(e_neg, 1)

                        def one_hot_nodes(a, c, q):
                            p = (q + c) % 2
                            act.wait_ge(e_in[c], a * 32 + 32)
                            wait(act, e_picka, a * NCH + c)
                            nc.scalar.activation(away[:, :], idr[c][:, 0:AC], ACT.Abs, scale=-1.0,
                                                 bias=idCol[:, 0:1]).then_inc(e_away, 1)
                            act.wait_ge(e_away, a * NCH + c + 1)
                            wait(act, e_gath, a * NCH + c - 1)
                            nc.scalar.activation(pick[p][:, 0:AC], away[:, :], ACT.Relu, scale=-1.0,
                                                 bias=onesf[:, 0:1]).then_inc(e_picka, 1)

                        def first_parts(a, c, q):
                            p = (q + c) % 2
                            act.wait_ge(e_gath, a * NCH + c + 1)
                            wait(act, e_sum, a * NCH + c - 1)
                            nc.scalar.activation(msg[p][:, :, 0, 1, :], pD[p][:, 0:CH, :],
                                                 ACT.Copy).then_inc(e_hi, 1)
                            act.wait_ge(e_hi, (a * NCH + c) * 2 + 1)
                            nc.scalar.activation(msg[p][:, :, 0, 0, :], msg[p][:, :, 0, 1, :].bitcast(f32),
                                                 ACT.Relu).then_inc(e_hi, 1)

                        def sums(a):
                            act.wait_ge(e_sum, (a + 1) * NCH)
                            wait(act, e_tr, a)
                            nc.scalar.activation(agg[:, :, :], pAg[:, :, :], ACT.Copy).then_inc(e_agg, 1)

                        def save(a):
                            act.wait_ge(e_tr, a + 1)
                            nc.scalar.activation(posT[:, ds(a * P, P)], pTr[:, 0, :], ACT.Copy).then_inc(e_out, 1)
                            nc.scalar.activation(hT[:, ds(a * P, P)], pTr[:, 1, :], ACT.Copy).then_inc(e_out, 1)

                        def block_of(a, q, first, last):
                            def ahead(c):
                                if c < NCH:
                                    one_hot_nodes(a, c, q)
                                elif not last:
                                    one_hot_nodes(a + 1, c - NCH, 1 - q)
                            if first:
                                negate(0, 0)
                                one_hot_nodes(0, 0, 0)
                                one_hot_nodes(0, 1, 0)
                            for c in range(NCH):
                                first_parts(a, c, q)
                                if c == 0 and not first:
                                    sums(a - 1)
                                ahead(c + 2)
                                if c == 2 and not first:
                                    save(a - 1)
                                if c == 3 and not last:
                                    negate(a + 1, 1 - q)
                            if last:
                                sums(a)
                                save(a)
                        with act.If(flag > 0):
                            each(act, block_of)

            hb = [sb(f"f_hb{i}", [P, 2, GC], f32, ch) for i in range(2)]
            u2, u3 = ([sb(f"f_{n}{i}", [P, G, D], f32, ch) for i in range(2)] for n in ("v", "w"))
            pO = [ps(f"f_p{i}", [P, G, D], ch) for i in range(2)]
            f_in, f_mm, f_u2, f_u3, f_dma0, f_dma1 = (
                sem("f_" + n) for n in ("in", "mm", "u2", "u3", "dma0", "dma1"))
            f_dma = (f_dma0, f_dma1)

            def each(eng, body):
                body(0, 0, G)
                body(1, 1, G)
                with eng.Fori(1, NG // 2) as i:
                    body(i * 2, 0, G)
                    body(i * 2 + 1, 1, G)
                body(NG - 1, 0, 1)

            with nc.Block() as block:
                @block.scalar
                def _(act):
                    def load(g, p, nj):
                        wait(act, f_mm, g - 1)
                        for k, t in enumerate((posT, hT)):
                            last = nc.scalar.activation(hb[p][:, k, 0:nj * P], t[:, ds(g * GC, nj * P)], ACT.Copy)
                        last.then_inc(f_in, 1)
                    each(act, load)

                @block.tensor
                def _(pe):
                    def mul(g, p, nj):
                        pe.wait_ge(f_in, g + 1)
                        wait(pe, f_u2, g - 1)
                        for j in range(nj):
                            for k, W in enumerate((W22, WD)):
                                last = nc.tensor.matmul(pO[p][:, j, :], hb[p][:, k, j * P:(j + 1) * P], W[:, :],
                                                        start=k == 0, stop=k == 1)
                        last.then_inc(f_mm, 1)
                    each(pe, mul)

                @block.vector
                def _(dve):
                    def leave(g, p, nj):
                        dve.wait_ge(f_mm, g + 1)
                        wait(dve, f_u3, g - 1)
                        for j in range(nj):
                            last = nc.vector.scalar_tensor_tensor(
                                out=u2[p][:, j, :], in0=ber[:, :], scalar=cntN[:, ds(g * G + j, 1)],
                                in1=pO[p][:, j, :], op0=ALU.mult, op1=ALU.add)
                        last.then_inc(f_u2, 1)
                        dve.wait_ge(f_u2, g + 1)
                        wait(dve, f_dma[p], (g - p) * 8)
                        for j in range(nj):
                            last = nc.vector.scalar_tensor_tensor(
                                out=u3[p][:, j, :], in0=u2[p][:, j, :], scalar=rcnt[:, ds(g * G + j, 1)],
                                in1=xN[:, ds(g * G + j, 1), :].rearrange("p o d -> p (o d)"),
                                op0=ALU.mult, op1=ALU.add)
                        last.then_inc(f_u3, 1)
                    each(dve, leave)

                @block.sync
                def _(sp):
                    def save(g, p, nj):
                        sp.wait_ge(f_u3, g + 1)
                        if nj == G:
                            sp.dma_start(out[ds(g * GC, GC), :].rearrange("(n p) d -> p n d", p=P),
                                         u3[p][:, :, :]).then_inc(f_dma[p], 16)
                        else:
                            sp.dma_start(out[g * GC:N_NODES, :], u3[p][0:LAST, 0, :]).then_inc(f_dma[p], 16)
                    each(sp, save)
                    sp.wait_ge(f_dma0, 16 * (NG // 2 + 1))
                    sp.wait_ge(f_dma1, 16 * (NG // 2))


_NAMES = ("x", "src", "dst", "L0_gnn_W1", "L0_gnn_b1", "L0_gnn_W2", "L0_gnn_b2", "L1_gnn_W_neigh",
          "L1_gnn_b_neigh", "L1_gnn_W_edge", "L1_gnn_b_edge", "L1_gnn_W_lin", "L1_gnn_b_lin")


def kernel(**inputs):
    import numpy as np
    import concourse.bacc as bacc
    from concourse.bass_utils import run_bass_kernel_spmd

    nc = bacc.Bacc("TRN2", target_bir_lowering=False, num_devices=1)
    arrays, args = {}, []
    for name in _NAMES:
        a = np.ascontiguousarray(inputs[name])
        arrays["in_" + name] = a
        args.append(nc.dram_tensor("in_" + name, a.shape, mybir.dt.from_np(a.dtype), kind="ExternalInput").ap())
    out = nc.dram_tensor("out", (N_NODES, D), mybir.dt.float32, kind="ExternalOutput").ap()
    gnn(nc, *args, out)
    got = run_bass_kernel_spmd(nc, [arrays], core_ids=[0])
    return got.results[0]["out"]
```
